# Optimizing a Trainium2 kernel written in Bass

```python
import numpy as np
import jax
import jax.numpy as jnp

def _softmax(x, axis=-1):
    return jax.nn.softmax(x, axis=axis)

def _gelu(x):
    return jax.nn.gelu(x, approximate=True)

def _silu(x):
    return jax.nn.silu(x)

def _sigmoid(x):
    return jax.nn.sigmoid(x)

def _layernorm(x, axis=-1, eps=1e-05):
    m = jnp.mean(x, axis=axis, keepdims=True)
    v = jnp.var(x, axis=axis, keepdims=True)
    return (x - m) / jnp.sqrt(v + eps)

def _scatter_add(tgt, idx, src, axis=0):
    return tgt.at[idx].add(src)

def _segment_sum(src, seg, n):
    return jax.ops.segment_sum(src, seg, n)
kernel_name = 'mk_gnn_resnorm_d2_gnn_r64_e0b596'

def setup_inputs(seed: int=0):
    np.random.seed(seed)
    _w = jnp.asarray

    def _rec_inputs():
        import jax
        import jax.numpy as jnp
        _gk = jax.random.key(seed)
        x = -0.0005121 + 1.001 * jax.random.normal(jax.random.fold_in(_gk, 1), (100000, 32), jnp.float32)
        src = jax.random.randint(jax.random.fold_in(_gk, 2), (25000,), 0, 100000, jnp.int32)
        dst = jnp.minimum((100000 * jax.random.uniform(jax.random.fold_in(_gk, 3), (25000,)) ** 2.0).astype(jnp.int32), 99999)
        _o = jnp.argsort(dst, stable=True)
        src = src[_o]
        dst = dst[_o]
        edge_attr_16 = -3.57403e-05 + 0.999761 * jax.random.normal(jax.random.fold_in(_gk, 12), (25000, 16), jnp.float32)
        return (x, src, dst, edge_attr_16)
    x, src, dst, edge_attr_16 = _rec_inputs()

    def _L0_gnn_setup():
        import jax, jax.numpy as jnp
        import numpy as np
        N = 100000
        E = 25000
        G = 64
        H = 4
        C = 64
        NODE_F = 32
        DRONE_F = 16
        OUT = 32
        L = 2
        LN_EPS = 1e-05
        NEG_SLOPE = 0.2

        def _layer_norm(x, g, b):
            mu = jnp.mean(x, axis=-1, keepdims=True)
            var = jnp.mean((x - mu) ** 2, axis=-1, keepdims=True)
            return (x - mu) * jax.lax.rsqrt(var + LN_EPS) * g + b

        def _gat_conv(h, src, dst, W, a_src, a_dst, b):
            xh = (h @ W.T).reshape(N, H, C)
            alpha_s = jnp.sum(xh * a_src[None], axis=-1)
            alpha_d = jnp.sum(xh * a_dst[None], axis=-1)
            e = jax.nn.leaky_relu(alpha_s[src] + alpha_d[dst], NEG_SLOPE)
            m = jax.ops.segment_max(e, dst, num_segments=N)
            ex = jnp.exp(e - m[dst])
            s = jax.ops.segment_sum(ex, dst, num_segments=N)
            alpha = ex / (s[dst] + 1e-16)
            out = jax.ops.segment_sum(xh[src] * alpha[:, :, None], dst, num_segments=N)
            return jnp.mean(out, axis=1) + b
        key = jax.random.key(seed)
        ks = jax.random.split(key, 20)
        gn = lambda k, shape, s=0.1: jax.random.normal(k, shape, jnp.float32) * s
        inp = {}
        inp['x'] = jax.random.normal(ks[0], (N, NODE_F), jnp.float32)
        inp['drone_feat'] = jax.random.normal(ks[1], (G, DRONE_F), jnp.float32)
        inp['edge_index'] = jax.random.randint(ks[2], (2, E), 0, N, jnp.int32)
        inp['batch'] = jnp.sort(jax.random.randint(ks[3], (N,), 0, G, jnp.int32))
        inp['node_W'] = gn(ks[4], (C, NODE_F))
        inp['node_b'] = jnp.zeros((C,), jnp.float32)
        inp['drone_W'] = gn(ks[5], (C, DRONE_F))
        inp['drone_b'] = jnp.zeros((C,), jnp.float32)
        for l in range(L):
            kk = jax.random.split(ks[6 + l], 3)
            inp[f'convW{l}'] = gn(kk[0], (H * C, C))
            inp[f'att_src{l}'] = gn(kk[1], (H, C))
            inp[f'att_dst{l}'] = gn(kk[2], (H, C))
            inp[f'convb{l}'] = jnp.zeros((C,), jnp.float32)
            inp[f'ln_g{l}'] = jnp.ones((C,), jnp.float32)
            inp[f'ln_b{l}'] = jnp.zeros((C,), jnp.float32)
        inp['out_W'] = gn(ks[10], (OUT, C))
        inp['out_b'] = jnp.zeros((OUT,), jnp.float32)
        return inp
    _L0_gnn_all = _L0_gnn_setup()
    _L0_gnn_in = {k: v for k, v in _L0_gnn_all.items() if k in ('drone_feat', 'node_W', 'node_b', 'drone_W', 'drone_b', 'convW0', 'att_src0', 'att_dst0', 'convb0', 'ln_g0', 'ln_b0', 'convW1', 'att_src1', 'att_dst1', 'convb1', 'ln_g1', 'ln_b1', 'out_W', 'out_b')}
    del _L0_gnn_all

    def _L1_gnn_setup():
        import jax, jax.numpy as jnp
        import numpy as np
        N_ATOMS = 100000
        N_EDGES = 300000
        ATOM_DIM = 32
        BOND_DIM = 16
        STEPS = 4

        def _gru_cell(x, h, W_ih, W_hh, b_ih, b_hh):
            gi = x @ W_ih.T + b_ih
            gh = h @ W_hh.T + b_hh
            i_r, i_z, i_n = jnp.split(gi, 3, axis=-1)
            h_r, h_z, h_n = jnp.split(gh, 3, axis=-1)
            r = jax.nn.sigmoid(i_r + h_r)
            z = jax.nn.sigmoid(i_z + h_z)
            n = jnp.tanh(i_n + r * h_n)
            return (1.0 - z) * n + z * h
        key = jax.random.key(seed)
        ks = jax.random.split(key, 8)
        atom_features = jax.random.normal(ks[0], (N_ATOMS, ATOM_DIM), dtype=jnp.float32)
        bond_features = jax.random.normal(ks[1], (N_EDGES, BOND_DIM), dtype=jnp.float32)
        pair_indices = jax.random.randint(ks[2], (N_EDGES, 2), 0, N_ATOMS, dtype=jnp.int64 if jax.config.jax_enable_x64 else jnp.int32)
        W_bond = jax.random.normal(ks[3], (BOND_DIM, ATOM_DIM * ATOM_DIM), dtype=jnp.float32) * 0.05
        b_bond = jnp.zeros((ATOM_DIM * ATOM_DIM,), dtype=jnp.float32)
        W_ih = jax.random.normal(ks[4], (3 * ATOM_DIM, ATOM_DIM), dtype=jnp.float32) * 0.1
        W_hh = jax.random.normal(ks[5], (3 * ATOM_DIM, ATOM_DIM), dtype=jnp.float32) * 0.1
        b_ih = jnp.zeros((3 * ATOM_DIM,), dtype=jnp.float32)
        b_hh = jnp.zeros((3 * ATOM_DIM,), dtype=jnp.float32)
        return {'atom_features': atom_features, 'bond_features': bond_features, 'pair_indices': pair_indices, 'W_bond': W_bond, 'b_bond': b_bond, 'W_ih': W_ih, 'W_hh': W_hh, 'b_ih': b_ih, 'b_hh': b_hh}
    _L1_gnn_all = _L1_gnn_setup()
    _L1_gnn_in = {k: v for k, v in _L1_gnn_all.items() if k in ('W_bond', 'b_bond', 'W_ih', 'W_hh', 'b_ih', 'b_hh')}
    del _L1_gnn_all
    return {'x': x, 'src': src, 'dst': dst, 'edge_attr_16': edge_attr_16, 'L0_gnn_drone_feat': _L0_gnn_in['drone_feat'], 'L0_gnn_node_W': _L0_gnn_in['node_W'], 'L0_gnn_node_b': _L0_gnn_in['node_b'], 'L0_gnn_drone_W': _L0_gnn_in['drone_W'], 'L0_gnn_drone_b': _L0_gnn_in['drone_b'], 'L0_gnn_convW0': _L0_gnn_in['convW0'], 'L0_gnn_att_src0': _L0_gnn_in['att_src0'], 'L0_gnn_att_dst0': _L0_gnn_in['att_dst0'], 'L0_gnn_convb0': _L0_gnn_in['convb0'], 'L0_gnn_ln_g0': _L0_gnn_in['ln_g0'], 'L0_gnn_ln_b0': _L0_gnn_in['ln_b0'], 'L0_gnn_convW1': _L0_gnn_in['convW1'], 'L0_gnn_att_src1': _L0_gnn_in['att_src1'], 'L0_gnn_att_dst1': _L0_gnn_in['att_dst1'], 'L0_gnn_convb1': _L0_gnn_in['convb1'], 'L0_gnn_ln_g1': _L0_gnn_in['ln_g1'], 'L0_gnn_ln_b1': _L0_gnn_in['ln_b1'], 'L0_gnn_out_W': _L0_gnn_in['out_W'], 'L0_gnn_out_b': _L0_gnn_in['out_b'], 'L1_gnn_W_bond': _L1_gnn_in['W_bond'], 'L1_gnn_b_bond': _L1_gnn_in['b_bond'], 'L1_gnn_W_ih': _L1_gnn_in['W_ih'], 'L1_gnn_W_hh': _L1_gnn_in['W_hh'], 'L1_gnn_b_ih': _L1_gnn_in['b_ih'], 'L1_gnn_b_hh': _L1_gnn_in['b_hh']}

def reference(x, src, dst, edge_attr_16, L0_gnn_drone_feat, L0_gnn_node_W, L0_gnn_node_b, L0_gnn_drone_W, L0_gnn_drone_b, L0_gnn_convW0, L0_gnn_att_src0, L0_gnn_att_dst0, L0_gnn_convb0, L0_gnn_ln_g0, L0_gnn_ln_b0, L0_gnn_convW1, L0_gnn_att_src1, L0_gnn_att_dst1, L0_gnn_convb1, L0_gnn_ln_g1, L0_gnn_ln_b1, L0_gnn_out_W, L0_gnn_out_b, L1_gnn_W_bond, L1_gnn_b_bond, L1_gnn_W_ih, L1_gnn_W_hh, L1_gnn_b_ih, L1_gnn_b_hh):
    import jax
    import jax.numpy as jnp

    def _L0_gnn_ref(x, edge_index, drone_feat, batch, node_W, node_b, drone_W, drone_b, convW0, att_src0, att_dst0, convb0, ln_g0, ln_b0, convW1, att_src1, att_dst1, convb1, ln_g1, ln_b1, out_W, out_b):
        import jax, jax.numpy as jnp
        import numpy as np
        N = 100000
        E = 25000
        G = 64
        H = 4
        C = 64
        NODE_F = 32
        DRONE_F = 16
        OUT = 32
        L = 2
        LN_EPS = 1e-05
        NEG_SLOPE = 0.2

        def _layer_norm(x, g, b):
            mu = jnp.mean(x, axis=-1, keepdims=True)
            var = jnp.mean((x - mu) ** 2, axis=-1, keepdims=True)
            return (x - mu) * jax.lax.rsqrt(var + LN_EPS) * g + b

        def _gat_conv(h, src, dst, W, a_src, a_dst, b):
            xh = (h @ W.T).reshape(N, H, C)
            alpha_s = jnp.sum(xh * a_src[None], axis=-1)
            alpha_d = jnp.sum(xh * a_dst[None], axis=-1)
            e = jax.nn.leaky_relu(alpha_s[src] + alpha_d[dst], NEG_SLOPE)
            m = jax.ops.segment_max(e, dst, num_segments=N)
            ex = jnp.exp(e - m[dst])
            s = jax.ops.segment_sum(ex, dst, num_segments=N)
            alpha = ex / (s[dst] + 1e-16)
            out = jax.ops.segment_sum(xh[src] * alpha[:, :, None], dst, num_segments=N)
            return jnp.mean(out, axis=1) + b
        loop = jnp.arange(N, dtype=edge_index.dtype)
        src = jnp.concatenate([edge_index[0], loop])
        dst = jnp.concatenate([edge_index[1], loop])
        h = x @ node_W.T + node_b + (drone_feat @ drone_W.T + drone_b)[batch]
        layers = [(convW0, att_src0, att_dst0, convb0, ln_g0, ln_b0), (convW1, att_src1, att_dst1, convb1, ln_g1, ln_b1)]
        for W, a_s, a_d, cb, g, lb in layers:
            h = h + jax.nn.relu(_layer_norm(_gat_conv(h, src, dst, W, a_s, a_d, cb), g, lb))
        return h @ out_W.T + out_b

    def _L1_gnn_ref(atom_features, bond_features, pair_indices, W_bond, b_bond, W_ih, W_hh, b_ih, b_hh):
        import jax, jax.numpy as jnp
        import numpy as np
        N_ATOMS = 100000
        N_EDGES = 300000
        ATOM_DIM = 32
        BOND_DIM = 16
        STEPS = 4

        def _gru_cell(x, h, W_ih, W_hh, b_ih, b_hh):
            gi = x @ W_ih.T + b_ih
            gh = h @ W_hh.T + b_hh
            i_r, i_z, i_n = jnp.split(gi, 3, axis=-1)
            h_r, h_z, h_n = jnp.split(gh, 3, axis=-1)
            r = jax.nn.sigmoid(i_r + h_r)
            z = jax.nn.sigmoid(i_z + h_z)
            n = jnp.tanh(i_n + r * h_n)
            return (1.0 - z) * n + z * h
        n_atoms, d = atom_features.shape
        edge_mats = (bond_features @ W_bond + b_bond).reshape(-1, d, d)
        dst = pair_indices[:, 0]
        nbr = pair_indices[:, 1]
        h = atom_features
        for _ in range(STEPS):
            msg = jnp.einsum('eij,ej->ei', edge_mats, h[nbr])
            agg = jax.ops.segment_sum(msg, dst, num_segments=n_atoms)
            h = _gru_cell(agg, h, W_ih, W_hh, b_ih, b_hh)
        return h
    edge_index = jnp.stack([src, dst])
    edge_index_t = jnp.stack([src, dst], axis=1)
    batch0 = jnp.zeros((100000,), jnp.int32)
    x = _layernorm(x + _L0_gnn_ref(x, edge_index, L0_gnn_drone_feat, batch0, L0_gnn_node_W, L0_gnn_node_b, L0_gnn_drone_W, L0_gnn_drone_b, L0_gnn_convW0, L0_gnn_att_src0, L0_gnn_att_dst0, L0_gnn_convb0, L0_gnn_ln_g0, L0_gnn_ln_b0, L0_gnn_convW1, L0_gnn_att_src1, L0_gnn_att_dst1, L0_gnn_convb1, L0_gnn_ln_g1, L0_gnn_ln_b1, L0_gnn_out_W, L0_gnn_out_b), axis=-1)
    x = _layernorm(x + _L1_gnn_ref(x, edge_attr_16, edge_index_t, L1_gnn_W_bond, L1_gnn_b_bond, L1_gnn_W_ih, L1_gnn_W_hh, L1_gnn_b_ih, L1_gnn_b_hh), axis=-1)
    return x

_drawn_inputs = setup_inputs


def setup_inputs(seed=0):
    import zlib

    import numpy as np

    out = dict(_drawn_inputs(seed))
    spreads = {'L0_gnn_node_b': (0.0, 0.1),
     'L0_gnn_drone_b': (0.0, 0.1),
     'L0_gnn_convb0': (0.0, 0.1),
     'L0_gnn_ln_g0': (1.0, 0.2),
     'L0_gnn_ln_b0': (0.0, 0.1),
     'L0_gnn_convb1': (0.0, 0.1),
     'L0_gnn_ln_g1': (1.0, 0.2),
     'L0_gnn_ln_b1': (0.0, 0.1),
     'L0_gnn_out_b': (0.0, 0.1),
     'L1_gnn_b_bond': (0.0, 0.1),
     'L1_gnn_b_ih': (0.0, 0.1),
     'L1_gnn_b_hh': (0.0, 0.1)}
    factors = {'L0_gnn_att_src0': 2.975,
     'L0_gnn_att_dst0': 6.426,
     'L0_gnn_att_src1': 3.219,
     'L0_gnn_att_dst1': 8.0}
    for name, (base, spread) in spreads.items():
        noise = np.random.default_rng([zlib.crc32(name.encode()), seed]).standard_normal(out[name].shape)
        drawn = base * np.exp(spread * noise) if base else spread * noise
        out[name] = jnp.asarray(drawn.astype(out[name].dtype))
    for name, factor in factors.items():
        out[name] = (out[name] * factor).astype(out[name].dtype)
    return out
```

```python
import numpy as np
import concourse.bass as bass
from concourse import mybir
from contextlib import ExitStack

F32 = mybir.dt.float32
I32 = mybir.dt.int32
ALU = mybir.AluOpType
ACT = mybir.ActivationFunctionType
AX = mybir.AxisListType

P = 128
N_NODES, N_EDGES = 100000, 25000
XF, HF, HEADS, BONDF, STEPS = 32, 64, 4, 16, 4
T = -(-N_EDGES // P)
EP = P * T
DB = -(-N_NODES // (16 * P))
NP = DB * 16 * P
NROWS = NP + EP
BT = 28
EB = T // BT
QB = BT // 4
NQ = T // 4
PAY = 2 + BONDF
BINS_LO, BINS_HI = 256, -(-(N_NODES + 1) // 256)
SENTINEL = 1 << 20
EPS = 1e-5
BIG = 1e30
PARTS = [(0, 512), (512, 384)]
UNITS = [(0, 2), (2, 2), (4, 2), (6, 1)]
ALL = 16 * T

K_ID, K_J64, K_C64, K_J32, K_C32, K_LT = (i * P for i in range(6))
K_IOTA = 6 * P
K_EDGE = K_IOTA + 512
K_JUNK = K_EDGE + T
K_END = K_JUNK + T
W_H0A, W_H0B = 0, P
W_XW = [2 * P, 2 * P + 512]
W_IH = W_XW[1] + 512
W_HH = W_IH + 3 * P
W_COL = W_HH + 3 * P
(C_NODEB, C_DRONEB, C_OUTB, C_BIHR, C_BIHZ, C_BIHN, C_BHHR, C_BHHZ, C_BHHN) = range(9)
C_CONVB, C_G, C_B = [9, 12], [10, 13], [11, 14]
N_COL = 15
W_END = W_COL + N_COL
V_WH = [0, 4 * P]
V_AS, V_AD1, V_AD2 = [8 * P, 8 * P + 96], [8 * P + 192, 8 * P + 288], [8 * P + 384, 8 * P + 480]
V_OA = 8 * P + 576
V_OB = V_OA + P
V_DW = V_OB + P
V_DF = V_DW + P
V_END = V_DF + 1
D_WC = [0, P]
D_OA, D_OB = 2 * P, 3 * P
D_RS, D_RD = [4 * P, 4 * P + 24], [4 * P + 48, 4 * P + 72]
D_C0 = 4 * P + 96
D_BC = [D_C0 + 1, D_C0 + 2]
D_OBC, D_EPS, D_BR, D_BZ = D_C0 + 3, D_C0 + 4, D_C0 + 5, D_C0 + 6
D_END = D_C0 + 7


def build(nc, x, src, dst, attr, consts, weights, prep, bondw, out, only=None):
    ctx = ExitStack()
    with ctx:
        def sem(name):
            return ctx.enter_context(nc.semaphore(name))

        def dram(name, shape, dt):
            return nc.dram_tensor(name, shape, dt, kind="Internal").ap()

        tmp_d = dram("tmp_d", (EP, 2), I32)
        sort_d = dram("sort_d", (EP + 2, 2), I32)
        tmp_s = dram("tmp_s", (EP, PAY), F32)
        sort_s = dram("sort_s", (EP + 2, PAY), F32)
        h1_tab = dram("h1_tab", (NROWS, HF), F32)
        x1_tab = dram("x1_tab", (NROWS, XF), F32)
        pos_tab = dram("pos_tab", (NROWS, 1), I32)
        agg_tab = dram("agg_tab", (EP + P, XF), F32)
        ht_dram = [dram(f"ht_dram{l}", (EB, P, QB * 512), F32) for l in range(2)]
        h1d_dram = dram("h1d_dram", (EB, P, QB * 256), F32)
        xs_dram = dram("xs_dram", (P, T * XF), F32)
        xt_dram = dram("xt_dram", (EB, P, QB * 256), F32)

        def sb(name, words):
            return ctx.enter_context(nc.sbuf_tensor(name, [P, words], F32))

        kc = sb("kc", K_END)
        wt = sb("wt", W_END)
        dv = sb("dv", D_END)
        r1 = sb("r1", T * HF)
        r2 = sb("r2", T * HF)
        r3 = sb("r3", 2 * QB * 512)
        stage = sb("stage", 2 * BT * HF)
        l12 = sb("l12", 12 * T)
        alpha = sb("alpha", 2 * T * HEADS)
        nst = sb("nst", 16 * T)
        small = sb("small", 23 * T + 5 * P + 300)
        ps = ctx.enter_context(nc.psum_tensor("ps", [P, 8, 512], F32))

        def k(c, n=P):
            return kc[:, c:c + n]

        ident = k(K_ID)

        def col(c):
            return wt[:, W_COL + c:W_COL + c + 1]

        def dcol(c):
            return dv[:, c:c + 1]

        at = [0]

        def carve(n):
            at[0] += n
            return small[:, at[0] - n:at[0]]

        ns_f, nl_f, pm, sm, last, ns_neg, nl_neg, pm_neg, sm_neg = (carve(T) for _ in range(9))
        ns_fs, pm_s = carve(T), carve(T)
        put_d, put_s, pos_val, pos_of = (carve(T).bitcast(I32) for _ in range(4))
        kid_d = carve(2 * T).bitcast(I32).rearrange("p (t c) -> p t c", c=2)
        kid_s = carve(2 * T).bitcast(I32).rearrange("p (t c) -> p t c", c=2)
        rank_i = [carve(T).bitcast(I32) for _ in range(4)]
        row_f, row_r, row_fn, row_rn, row_fs = (carve(P) for _ in range(5))
        edge_d, edge_s = carve(4).bitcast(I32), carve(4).bitcast(I32)
        end_c, carry, lanes = carve(64), carve(64), carve(130)

        phase_ended, phase_begins = sem("phase_ended"), sem("phase_begins")
        ends = {"sp": 0, "pe": 0, "act": 0, "dve": 0}

        def barrier(eng, who, clear=()):
            ends[who] += 1
            eng.drain().then_inc(phase_ended, 1)
            if who == "sp":
                eng.wait_ge(phase_ended, 4 * ends[who])
                for s in clear:
                    eng.sem_clear(s)
                eng.sem_inc(phase_begins, 1)
            else:
                eng.wait_ge(phase_begins, ends[who])

        def phase_sems(phase, names):
            return [nc.alloc_semaphore(name=f"{phase}_{n}") for n in names.split()]

        def phase_over(sems):
            for s in sems:
                nc.release_semaphore(s)

        def loop(eng, n, body):
            with eng.Fori(0, n // 2) as i:
                body(2 * i, i, 0)
                body(2 * i + 1, i, 1)
            body(n - 1, n // 2, 0)

        ld = sem("ld")
        ld_keys, ld_pay, ld_tmp_d, ld_tmp_s = sem("ld_keys"), sem("ld_pay"), sem("ld_tmp_d"), sem("ld_tmp_s")
        init_dram = sem("init_dram")
        rank_ready = sem("rank_ready")
        put_tmp_d, put_tmp_s, put_sort_d, put_sort_s = (sem(f"put_{n}") for n in
                                                         ("tmp_d", "tmp_s", "sort_d", "sort_s"))
        ld_kid_d, ld_kid_s, got_x, put_pos, got_pos = (sem(n) for n in
                                                       ("ld_kid_d", "ld_kid_s", "got_x", "put_pos", "got_pos"))
        flags_ready = sem("flags_ready")
        dense_done = sem("dense_done")
        rows_ready = sem("rows_ready")
        put_h1, got_h1, put_x1, got_x1 = (sem(n) for n in ("put_h1", "got_h1", "put_x1", "got_x1"))
        out_done = sem("out_done")
        agg_stored, got_agg, put_out = sem("agg_stored"), sem("got_agg"), sem("put_out")
        prep_pe, prep_dve = sem("prep_pe"), sem("prep_dve")
        sentinel_ready = sem("sentinel_ready")
        fl, fl_pe = sem("fl"), sem("fl_pe")
        tl_d, tl_p = sem("tl_d"), sem("tl_p")
        sx, sx_act = sem("sx"), sem("sx_act")
        sc = sem("sc")

        pw = r1[:, 0:V_END]
        fill = r2[:, 12000:12512]
        pos_fill = r2[:, 0:NP // P].bitcast(I32)

        def prep_sp(sp):
            sp.dma_start(kc[:], consts).then_inc(ld, 16)
            sp.dma_start(wt[:], weights).then_inc(ld, 16)
            sp.dma_start(pw, prep).then_inc(ld, 16)
            sp.dma_start(src_t, src.rearrange("(p t) -> p t", t=T)).then_inc(ld_keys, 16)
            sp.dma_start(dst_t, dst.rearrange("(p t) -> p t", t=T)).then_inc(ld_keys, 16)
            sp.dma_start(pay_s[:, :, 2:PAY], attr.rearrange("(p t) c -> p t c", t=T)).then_inc(ld_pay, 16)
            sp.wait_ge(sentinel_ready, 3)
            for r in (0, EP + 1):
                sp.dma_start(sort_d[r:r + 1, :], fill[0:1, 0:2].bitcast(I32)).then_inc(init_dram, 16)
                sp.dma_start(sort_s[r:r + 1, :], fill[0:1, 0:PAY]).then_inc(init_dram, 16)
            sp.dma_start(pos_tab[0:NP, :].rearrange("(p n) c -> p (n c)", p=P), pos_fill).then_inc(init_dram, 16)
            sp.dma_start(agg_tab[EP:EP + P, :], fill[:, 64:64 + XF]).then_inc(init_dram, 16)
            sp.wait_ge(init_dram, 16 * 6)

        def prep_dve_(dve):
            v = nc.vector
            v.memset(fill[:, 0:64].bitcast(I32), SENTINEL).then_inc(sentinel_ready, 1)
            v.memset(fill[:, 64:128], 0.0).then_inc(sentinel_ready, 1)
            v.memset(pos_fill, EP).then_inc(sentinel_ready, 1)
            v.memset(dcol(D_EPS), EPS)
            dve.wait_ge(ld, 48)
            dve.wait_ge(prep_pe, 1)
            v.tensor_tensor(dcol(D_C0), ps[:, 0, 0:1], col(C_NODEB), ALU.add).then_inc(prep_dve, 1)
            dve.wait_ge(prep_dve, 1)
            v.tensor_tensor(dcol(D_C0), dcol(D_C0), col(C_DRONEB), ALU.add)
            for l in range(2):
                v.tensor_single_scalar(dv[:, D_WC[l]:D_WC[l] + P], ps[:, 1 + l, 0:P], 1.0 / HEADS, ALU.mult)
                v.tensor_copy(dv[:, D_RS[l]:D_RS[l] + 24], ps[:, 1 + l, 128:152])
                v.tensor_copy(dv[:, D_RD[l]:D_RD[l] + 24], ps[:, 1 + l, 152:176])
                v.tensor_copy(dcol(D_BC[l]), ps[:, 1 + l, 176:177])
            v.tensor_copy(dv[:, D_OA:D_OA + 2 * P], ps[:, 3, 0:2 * P])
            v.tensor_copy(dcol(D_OBC), ps[:, 3, 256:257])
            v.tensor_tensor(dcol(D_BR), col(C_BIHR), col(C_BHHR), ALU.add)
            v.tensor_tensor(dcol(D_BZ), col(C_BIHZ), col(C_BHHZ), ALU.add)

        def prep_pe_(pe):
            mm = nc.tensor.matmul
            pe.wait_ge(ld, 48)
            mm(ps[:, 0, 0:1], pw[:, V_DW:V_DW + P], pw[:, V_DF:V_DF + 1], start=True, stop=True)
            for l in range(2):
                wh = [pw[:, V_WH[l] + h * P:V_WH[l] + (h + 1) * P] for h in range(HEADS)]
                for h in range(HEADS):
                    mm(ps[:, 1 + l, 0:P], wh[h], k(K_C64), start=h == 0, stop=h == HEADS - 1)
                for h in range(HEADS):
                    mm(ps[:, 1 + l, 128:152], wh[h], pw[:, V_AS[l] + 24 * h:V_AS[l] + 24 * h + 24],
                       start=h == 0, stop=h == HEADS - 1)
                for h in range(HEADS):
                    mm(ps[:, 1 + l, 152:176], wh[h], pw[:, V_AD1[l] + 24 * h:V_AD1[l] + 24 * h + 24],
                       start=h == 0, stop=False)
                    mm(ps[:, 1 + l, 152:176], wh[h], pw[:, V_AD2[l] + 24 * h:V_AD2[l] + 24 * h + 24],
                       start=False, stop=h == HEADS - 1)
                mm(ps[:, 1 + l, 176:177], k(K_C64), col(C_CONVB[l]), start=True, stop=True)
            mm(ps[:, 3, 0:P], pw[:, V_OA:V_OA + P], k(K_C32), start=True, stop=True)
            mm(ps[:, 3, P:2 * P], pw[:, V_OB:V_OB + P], k(K_C32), start=True, stop=True)
            mm(ps[:, 3, 256:257], k(K_C32), col(C_OUTB), start=True, stop=True).then_inc(prep_pe, 1)

        src_t, dst_t = r3[:, 0:T].bitcast(I32), r3[:, T:2 * T].bitcast(I32)
        pay_d = r3[:, 2 * T:4 * T].bitcast(I32).rearrange("p (t c) -> p t c", c=2)
        pay_s = r3[:, 4 * T:(4 + PAY) * T].rearrange("p (t c) -> p t c", c=PAY)
        pay_si = r3[:, 4 * T:(4 + PAY) * T].bitcast(I32).rearrange("p (t c) -> p t c", c=PAY)
        digit_i, digit, rank = r2[:, 1000:1000 + T].bitcast(I32), r2[:, 1200:1200 + T], r2[:, 1400:1400 + T]
        hist, start, junk, ones_b = (r2[:, 2000 + 512 * i:2512 + 512 * i] for i in range(4))
        s_hist, s_pref, s_dv = sem("s_hist"), sem("s_pref"), sem("s_dv")
        UN = 7

        def sort_dve(dve):
            v = nc.vector
            v.memset(ones_b[:], 1.0)
            dve.wait_ge(ld_keys, 32)
            v.tensor_copy(pay_d[:, :, 0], src_t)
            v.tensor_copy(pay_d[:, :, 1], dst_t)
            v.tensor_copy(pay_si[:, :, 0], src_t)
            v.tensor_copy(pay_si[:, :, 1], dst_t)
            n = [0]

            def chain(ins):
                ins.then_inc(s_dv, 1)
                n[0] += 1
                dve.wait_ge(s_dv, n[0])

            for i, (key, bins) in enumerate([(dst_t, BINS_LO), (src_t, BINS_LO),
                                             (pay_d[:, :, 1], BINS_HI), (pay_si[:, :, 0], BINS_HI)]):
                if i == 2:
                    dve.wait_ge(ld_tmp_d, 16)
                if i == 3:
                    dve.wait_ge(ld_tmp_s, 16)
                if i < 2:
                    chain(v.tensor_single_scalar(digit_i, key, 255, ALU.bitwise_and))
                else:
                    chain(v.tensor_single_scalar(digit_i, key, 8, ALU.logical_shift_right))
                v.tensor_copy(digit, digit_i)
                chain(v.memset(hist[:, 0:bins], 0.0))
                base = n[0]
                with dve.Fori(0, T // UN) as j:
                    for u in range(UN):
                        v.scalar_tensor_tensor(out=hist[:, 0:bins], in0=k(K_IOTA, bins),
                                               scalar=digit[:, bass.ds(j * UN + u, 1)], in1=hist[:, 0:bins],
                                               op0=ALU.is_equal, op1=ALU.add).then_inc(s_dv, 1)
                        dve.wait_ge(s_dv, j * UN + (base + u + 1))
                n[0] += T
                v.tensor_copy(start[:, 0:bins], hist[:, 0:bins]).then_inc(s_hist, 1)
                dve.wait_ge(s_pref, i + 1)
                chain(v.tensor_tensor_scan(junk[:, 0:bins], ones_b[:, 0:bins], ps[:, 5, 0:bins], 0.0,
                                           ALU.mult, ALU.add))
                chain(v.tensor_tensor(junk[:, 0:bins], junk[:, 0:bins], ps[:, 5, 0:bins], ALU.subtract))
                chain(v.tensor_tensor(start[:, 0:bins], junk[:, 0:bins], ps[:, 4, 0:bins], ALU.add))
                base = n[0]
                with dve.Fori(0, T // UN) as j:
                    for u in range(UN):
                        d = digit[:, bass.ds(j * UN + u, 1)]
                        v.scalar_tensor_tensor(out=junk[:, 0:bins], in0=k(K_IOTA, bins), scalar=d,
                                               in1=start[:, 0:bins], op0=ALU.is_equal, op1=ALU.mult,
                                               accum_out=rank[:, bass.ds(j * UN + u, 1)]).then_inc(s_dv, 1)
                        dve.wait_ge(s_dv, j * (2 * UN) + (base + 2 * u + 1))
                        v.scalar_tensor_tensor(out=start[:, 0:bins], in0=k(K_IOTA, bins), scalar=d,
                                               in1=start[:, 0:bins], op0=ALU.is_equal,
                                               op1=ALU.add).then_inc(s_dv, 1)
                        dve.wait_ge(s_dv, j * (2 * UN) + (base + 2 * u + 2))
                n[0] += 2 * T
                v.tensor_single_scalar(rank_i[i], rank, float(i // 2), ALU.add).then_inc(rank_ready, 1)

        def sort_pe(pe):
            mm = nc.tensor.matmul
            for i, bins in enumerate([BINS_LO, BINS_LO, BINS_HI, BINS_HI]):
                pe.wait_ge(s_hist, i + 1)
                mm(ps[:, 4, 0:bins], k(K_LT), start[:, 0:bins], start=True, stop=True)
                mm(ps[:, 5, 0:bins], ones_b[:, 0:P], start[:, 0:bins], start=True, stop=True).then_inc(s_pref, 1)

        def sort_sp(sp):
            sp.wait_ge(put_tmp_d, ALL)
            sp.dma_start(pay_d.rearrange("p t c -> p (t c)"),
                         tmp_d.rearrange("(p t) c -> p (t c)", t=T)).then_inc(ld_tmp_d, 16)
            sp.wait_ge(put_tmp_s, ALL)
            sp.dma_start(pay_s.rearrange("p t c -> p (t c)"),
                         tmp_s.rearrange("(p t) c -> p (t c)", t=T)).then_inc(ld_tmp_s, 16)

        dense_sems = phase_sems("dn", "x0 x1 tr xt hm h z zc sq v sd rs tn rl hn t1 t1e free xtr xe st")
        dn = dense_sems[0:2]
        (dn_tr, dn_xt, dn_hm, dn_h, dn_z, dn_zc, dn_sq, dn_v, dn_sd, dn_rs, dn_tn, dn_rl, dn_hn, dn_t1,
         dn_t1e, dn_free, dn_xtr, dn_xe, dn_st) = dense_sems[2:]
        phase_over(dense_sems)
        off = [0]

        def lay(region, n):
            off[0] += n
            return region[:, off[0] - n:off[0]]

        xr = [lay(r2, 512) for _ in range(2)]
        xt_b = lay(r2, 512)
        hb, zc, sq, sd, tn, rl, h1b = ([lay(r2, 512) for _ in range(2)] for _ in range(7))
        h1o = [lay(r2, 1024) for _ in range(2)]
        x1o = [lay(r2, 512) for _ in range(2)]
        x_blk = x.rearrange("(b p n) f -> b p (n f)", p=P, n=16)
        h1_blk = h1_tab[0:NP, :].rearrange("(b p n) f -> b p (n f)", p=P, n=16)
        x1_blk = x1_tab[0:NP, :].rearrange("(b p n) f -> b p (n f)", p=P, n=16)
        out_blk = out[0:NP, :].rearrange("(b p n) f -> b p (n f)", p=P, n=16)

        def blk(ap, b):
            return ap[bass.ds(b, 1)].rearrange("o p f -> (o p) f")

        def dense_sp(sp):
            def load(b, slot):
                sp.dma_start(xr[slot], blk(x_blk, b)).then_inc(dn[slot], 16)

            def body(b, half, slot, ahead=True):
                if ahead:
                    sp.wait_ge(dn_tr, b + 1)
                    load(b + 1, 1 - slot)
                sp.wait_ge(dn_t1e, 2 * b + 4)
                sp.dma_start(blk(h1_blk, b), h1o[slot]).then_inc(dn_st, 16)
                sp.wait_ge(dn_xe, b + 2)
                sp.dma_start(blk(x1_blk, b), x1o[slot]).then_inc(dn_st, 16)
                sp.wait_ge(dn_st, 32 * b + 32)
                sp.sem_inc(dn_free, 1)

            sp.sem_inc(dn_free, 2)
            load(0, 0)
            with sp.Fori(0, DB // 2) as i:
                body(2 * i, i, 0)
                body(2 * i + 1, i, 1)
            body(DB - 1, DB // 2, 0, ahead=False)
            sp.sem_inc(dense_done, 1)

        def dense_pe(pe):
            mm, tr = nc.tensor.matmul, nc.tensor.transpose

            def body(b, half, slot):
                pe.wait_ge(dn[slot], 16 * half + 16)
                pe.wait_ge(dn_xe, b + 1)
                for s in range(4):
                    t = tr(ps[:, 0, s * P:(s + 1) * P], xr[slot][:, s * P:(s + 1) * P], ident)
                t.then_inc(dn_tr, 1)
                pe.wait_ge(dn_xt, b + 1)
                for h in range(2):
                    mm(ps[:, 1 + h, :], wt[:, (W_H0A, W_H0B)[h]:(W_H0A, W_H0B)[h] + P], xt_b,
                       start=True, stop=True).then_inc(dn_hm, 1)
                for l in range(2):
                    for h in range(2):
                        if l == 0:
                            pe.wait_ge(dn_h, 2 * b + h + 1)
                        else:
                            pe.wait_ge(dn_hn, 4 * b + h + 1)
                        mm(ps[:, 1 + h, :], dv[:, D_WC[l]:D_WC[l] + P], (hb, h1b)[l][h],
                           start=True, stop=True).then_inc(dn_z, 1)
                    if l == 1:
                        for h in range(2):
                            pe.wait_ge(dn_t1e, 2 * b + h + 1)
                            for s in range(4):
                                t = tr(ps[:, 5 + h, s * P:(s + 1) * P], h1b[h][:, s * P:(s + 1) * P], ident)
                            t.then_inc(dn_t1, 1)
                    for h in range(2):
                        pe.wait_ge(dn_sq, 5 * b + 2 * l + h + 1)
                        mm(ps[:, 3 + h, :], k(K_J64), sq[h], start=True, stop=True).then_inc(dn_v, 1)
                pe.wait_ge(dn_hn, 4 * b + 4)
                mm(ps[:, 7, :], k(K_C32), xt_b, start=True, stop=False)
                mm(ps[:, 7, :], dv[:, D_OA:D_OA + P], hb[0], start=False, stop=False)
                mm(ps[:, 7, :], dv[:, D_OB:D_OB + P], hb[1], start=False, stop=True).then_inc(dn_z, 1)
                pe.wait_ge(dn_sq, 5 * b + 5)
                mm(ps[:, 3, :], k(K_J32), sq[0], start=True, stop=True).then_inc(dn_v, 1)
                pe.wait_ge(dn_tn, 5 * b + 5)
                for s in range(4):
                    t = tr(ps[:, 0, s * P:(s + 1) * P], tn[0][:, s * P:(s + 1) * P], ident)
                t.then_inc(dn_xtr, 1)

            pe.sem_inc(dn_tr, 1)
            loop(pe, DB, body)

        def dense_act(act):
            a = nc.scalar.activation

            def body(b, half, slot):
                act.wait_ge(dn_tr, b + 2)
                a(xt_b, ps[:, 0, :], ACT.Identity).then_inc(dn_xt, 1)
                for h in range(2):
                    act.wait_ge(dn_hm, 2 * b + h + 1)
                    a(hb[h], ps[:, 1 + h, :], ACT.Identity, bias=dcol(D_C0)).then_inc(dn_h, 1)
                for l in range(2):
                    for h in range(2):
                        act.wait_ge(dn_z, 5 * b + 2 * l + h + 1)
                        a(zc[h], ps[:, 1 + h, :], ACT.Identity, bias=dcol(D_BC[l])).then_inc(dn_zc, 1)
                        a(sq[h], ps[:, 1 + h, :], ACT.Square, bias=dcol(D_BC[l])).then_inc(dn_sq, 1)
                    for h in range(2):
                        act.wait_ge(dn_v, 5 * b + 2 * l + h + 1)
                        a(sd[h], ps[:, 3 + h, :], ACT.Sqrt, bias=dcol(D_EPS)).then_inc(dn_sd, 1)
                    for h in range(2):
                        act.wait_ge(dn_tn, 5 * b + 2 * l + h + 1)
                        a(rl[h], tn[h], ACT.Relu, bias=col(C_B[l]), scale=col(C_G[l])).then_inc(dn_rl, 1)
                act.wait_ge(dn_z, 5 * b + 5)
                a(zc[0], ps[:, 7, :], ACT.Identity, bias=dcol(D_OBC)).then_inc(dn_zc, 1)
                a(sq[0], ps[:, 7, :], ACT.Square, bias=dcol(D_OBC)).then_inc(dn_sq, 1)
                act.wait_ge(dn_v, 5 * b + 5)
                a(sd[0], ps[:, 3, :], ACT.Sqrt, bias=dcol(D_EPS)).then_inc(dn_sd, 1)

            loop(act, DB, body)

        def dense_dve(dve):
            v = nc.vector

            def norm(u, h):
                dve.wait_ge(dn_sd, u + 1)
                v.reciprocal(sd[h], sd[h]).then_inc(dn_rs, 1)
                dve.wait_ge(dn_rs, u + 1)
                dve.wait_ge(dn_zc, u + 1)
                v.tensor_tensor(tn[h], zc[h], sd[h], ALU.mult).then_inc(dn_tn, 1)

            def body(b, half, slot):
                dve.wait_ge(dn_free, b + 1)
                for l in range(2):
                    for h in range(2):
                        norm(5 * b + 2 * l + h, h)
                    for h in range(2):
                        dve.wait_ge(dn_rl, 4 * b + 2 * l + h + 1)
                        v.tensor_tensor((h1b, hb)[l][h], (hb, h1b)[l][h], rl[h], ALU.add).then_inc(dn_hn, 1)
                    if l == 0:
                        for h in range(2):
                            dve.wait_ge(dn_t1, 2 * b + h + 1)
                            v.tensor_copy(h1o[slot].rearrange("p (s h c) -> p s h c", s=4, h=2)[:, :, h, :],
                                          ps[:, 5 + h, :].rearrange("p (s c) -> p s c", s=4)).then_inc(dn_t1e, 1)
                norm(5 * b + 4, 0)
                dve.wait_ge(dn_xtr, b + 1)
                v.tensor_copy(x1o[slot], ps[:, 0, :]).then_inc(dn_xe, 1)

            dve.sem_inc(dn_t1e, 2)
            dve.sem_inc(dn_xe, 1)
            loop(dve, DB, body)

        kx = r2[:, 0:T + 2]
        kt = r2[:, 256:256 + T]
        diag = [r2[:, 512 + P * i:640 + P * i] for i in range(3)]
        nfl = [0]

        def flags_dve(dve):
            v = nc.vector

            def chain(ins):
                ins.then_inc(fl, 1)
                nfl[0] += 1
                dve.wait_ge(fl, nfl[0])

            dve.wait_ge(ld_kid_d, 48)
            dve.wait_ge(ld_kid_s, 48)
            v.tensor_copy(kid_s, pay_si[:, :, 0:2])
            for order in range(2):
                key = (kid_d[:, :, 1], pay_si[:, :, 0])[order]
                edge = (edge_d, edge_s)[order]
                nsf, pmx = ((ns_f, pm), (ns_fs, pm_s))[order]
                put = (put_d, put_s)[order]
                v.tensor_copy(kx[:, 0:1], edge[:, 1 - order:2 - order])
                v.tensor_copy(kx[:, T + 1:T + 2], edge[:, 3 - order:4 - order])
                chain(v.tensor_copy(kx[:, 1:T + 1], key))
                chain(v.tensor_tensor(nsf, kx[:, 1:T + 1], kx[:, 0:T], ALU.is_equal))
                chain(v.tensor_tensor_scan(pmx, nsf, nsf, 1.0, ALU.mult, ALU.min))
                chain(v.memset(nsf[:, 0:1], 0.0))
                chain(v.tensor_tensor(kt, kx[:, 1:T + 1], kx[:, 2:T + 2], ALU.is_equal))
                if order == 0:
                    chain(v.tensor_tensor_scan(sm[:, ::-1], kt[:, ::-1], kt[:, ::-1], 1.0, ALU.mult, ALU.min))
                    chain(v.tensor_copy(nl_f, kt))
                    chain(v.memset(nl_f[:, T - 1:T], 0.0))
                chain(v.tensor_scalar(kt, kt, -1.0, 1.0, ALU.mult, ALU.add))
                if order == 0:
                    chain(v.tensor_copy(last, kt))
                    for a, b in ((ns_neg, ns_f), (nl_neg, nl_f), (pm_neg, pm), (sm_neg, sm)):
                        chain(v.tensor_scalar(a, b, 1.0, BIG, ALU.subtract, ALU.mult))
                chain(v.tensor_tensor(kx[:, 1:T + 1], kx[:, 1:T + 1], k(K_JUNK, T), ALU.subtract))
                chain(v.tensor_tensor(kx[:, 1:T + 1], kx[:, 1:T + 1], kt, ALU.mult))
                chain(v.tensor_tensor(put, kx[:, 1:T + 1], k(K_JUNK, T), ALU.add))
            chain(v.tensor_copy(pos_val, k(K_EDGE, T)))
            chain(v.tensor_single_scalar(diag[0], ident, pm[:, T - 1:T], ALU.mult))
            chain(v.tensor_single_scalar(diag[1], ident, sm[:, 0:1], ALU.mult))
            chain(v.tensor_single_scalar(diag[2], ident, pm_s[:, T - 1:T], ALU.mult))
            v.memset(lanes[:], 1.0).then_inc(flags_ready, 1)
            dve.wait_ge(fl_pe, 1)
            for i, row in enumerate((row_f, row_r, row_fs)):
                chain(v.tensor_copy(row[0:64, :], ps[0:64, 7, i * P:(i + 1) * P]))
            chain(v.tensor_scalar(row_fn[0:64, :], row_f[0:64, :], 1.0, BIG, ALU.subtract, ALU.mult))
            chain(v.tensor_scalar(row_rn[0:64, :], row_r[0:64, :], 1.0, BIG, ALU.subtract, ALU.mult))

        def flags_pe(pe):
            pe.wait_ge(flags_ready, 1)
            for i in range(3):
                m = nc.tensor.matmul(ps[0:64, 7, i * P:(i + 1) * P], lanes[:, 0:64], diag[i], start=True, stop=True)
            m.then_inc(fl_pe, 1)

        ntl = {"d": 0, "p": 0, "pe_d": 0, "pe_p": 0}

        def carry_dve(dve, ends, kk, row, op0, op1, first, reverse=False):
            v = nc.vector

            def chain(ins):
                ins.then_inc(tl_d, 1)
                ntl["d"] += 1

            chain(v.tensor_copy(end_c[:, 0:kk], ends))
            ntl["p"] += 1
            dve.wait_ge(tl_p, ntl["p"])
            if reverse:
                v.memset(lanes[0:kk, P:P + 1], first)
                chain(v.tensor_tensor_scan(lanes[0:kk, 0:P][:, ::-1], row[0:kk, :][:, ::-1],
                                           ps[0:kk, 6, 0:P][:, ::-1], first, op0, op1))
            else:
                v.memset(lanes[0:kk, 0:1], first)
                chain(v.tensor_tensor_scan(lanes[0:kk, 1:P + 1], row[0:kk, :], ps[0:kk, 6, 0:P], first,
                                           op0, op1))
            ntl["p"] += 1
            dve.wait_ge(tl_p, ntl["p"])
            chain(v.tensor_copy(carry[:, 0:kk], ps[:, 7, 0:kk]))
            dve.wait_ge(tl_d, ntl["d"])

        def carry_pe(pe, kk, reverse=False):
            tr = nc.tensor.transpose
            ntl["pe_d"] += 1
            pe.wait_ge(tl_d, ntl["pe_d"])
            tr(ps[0:kk, 6, 0:P], end_c[:, 0:kk], ident).then_inc(tl_p, 1)
            ntl["pe_d"] += 1
            pe.wait_ge(tl_d, ntl["pe_d"])
            tr(ps[:, 7, 0:kk], lanes[0:kk, (1 if reverse else 0):(1 if reverse else 0) + P],
               ident[0:kk, 0:kk]).then_inc(tl_p, 1)
            ntl["pe_d"] += 1

        y64 = r1[:].rearrange("p (f t) -> p f t", t=T)
        rows64 = r2[:].rearrange("p (t f) -> p t f", f=HF)
        xg = r1[:].rearrange("p (d t f) -> p d t f", d=2, f=XF)
        SB = BT * XF
        x1rows = r2[:, 0:T * XF].rearrange("p (t f) -> p t f", f=XF)
        stg = [stage[:, s * BT * HF:(s + 1) * BT * HF] for s in range(2)]
        ht = [r3[:, s * QB * 512:(s + 1) * QB * 512].rearrange("p (q h d c) -> p q h d c", q=QB, h=2, d=2)
              for s in range(2)]
        ht_flat = [r3[:, s * QB * 512:(s + 1) * QB * 512] for s in range(2)]
        xtb = [r2[:, s * QB * 256:(s + 1) * QB * 256] for s in range(2)]
        l12v = l12[:].rearrange("p (j t) -> p j t", j=12)
        alv = alpha[:].rearrange("p (d t h) -> p d t h", d=2, h=HEADS)

        def gat_logits(l):
            sems = phase_sems(f"g{l}", "in0 in1 inh0 inh1 tr xt hm ht lg l12 free st")
            s_in, s_inh = sems[0:2], sems[2:4]
            s_tr, s_xt, s_hm, s_ht, s_lg, s_l12, s_free, s_st = sems[4:]
            phase_over(sems)
            ahead_ht = 2 * l

            def sp_(sp):
                def load(b, slot):
                    if l == 0:
                        sp.dma_start(stg[slot].rearrange("p (d c) -> p d c", d=2),
                                     r1[:].rearrange("p (d c) -> p d c", d=2)[:, :, bass.ds(b * SB, SB)])\
                            .then_inc(s_in[slot], 16)
                    else:
                        sp.dma_start(stg[slot], r2[:, bass.ds(b * (BT * HF), BT * HF)])\
                            .then_inc(s_in[slot], 16)
                        sp.dma_start(ht[slot][:, :, :, 1, :],
                                     blk(h1d_dram, b).rearrange("p (q h c) -> p q h c", q=QB, h=2)
                                     ).then_inc(s_inh[slot], 16)

                def body(b, half, slot, ahead=True):
                    if ahead:
                        sp.wait_ge(s_l12, b + 1)
                        load(b + 1, 1 - slot)
                    sp.wait_ge(s_ht, QB * b + QB + ahead_ht)
                    sp.dma_start(blk(ht_dram[l], b), ht_flat[slot]).then_inc(s_st, 16)
                    if l == 0:
                        sp.dma_start(blk(xt_dram, b), xtb[slot]).then_inc(s_st, 16)
                    sp.wait_ge(s_st, (32 - 16 * l) * b + (32 - 16 * l))
                    sp.sem_inc(s_free, 1)

                if l == 0:
                    sp.wait_ge(got_x, 2 * ALL)
                else:
                    sp.wait_ge(got_h1, ALL)
                sp.sem_inc(s_free, 2)
                load(0, 0)
                with sp.Fori(0, EB // 2) as i:
                    body(2 * i, i, 0)
                    body(2 * i + 1, i, 1)
                body(EB - 1, EB // 2, 0, ahead=False)

            def pe_(pe):
                mm, tr = nc.tensor.matmul, nc.tensor.transpose

                def body(b, half, slot):
                    pe.wait_ge(s_in[slot], 16 * half + 16)
                    if l == 1:
                        pe.wait_ge(s_inh[slot], 16 * half + 16)

                    def logits(q):
                        pe.wait_ge(s_ht, QB * b + q + 1 + ahead_ht)
                        for h in range(2):
                            o = ps[:, 4 + slot, (2 * q + h) * 24:(2 * q + h) * 24 + 24]
                            mm(o, ht[slot][:, q, h, 0, :], dv[:, D_RS[l]:D_RS[l] + 24], start=True, stop=False)
                            m = mm(o, ht[slot][:, q, h, 1, :], dv[:, D_RD[l]:D_RD[l] + 24],
                                   start=False, stop=True)
                        m.then_inc(s_lg, 1)

                    for q in range(QB):
                        pe.wait_ge((s_xt, s_ht)[l], QB * b + q + 1)
                        if l == 0:
                            tr(ps[:, q % 2, 0:P], stg[slot][:, q * P:(q + 1) * P], ident)
                            tr(ps[:, q % 2, P:2 * P], stg[slot][:, SB + q * P:SB + (q + 1) * P],
                               ident).then_inc(s_tr, 1)
                            pe.wait_ge(s_xt, QB * b + q + 3)
                            rhs = xtb[slot][:, q * 256:(q + 1) * 256]
                            mm(ps[:, 2 + q % 2, 0:256], wt[:, W_H0A:W_H0A + P], rhs, start=True, stop=True)
                            mm(ps[:, 2 + q % 2, 256:512], wt[:, W_H0B:W_H0B + P], rhs,
                               start=True, stop=True).then_inc(s_hm, 1)
                        else:
                            tr(ps[:, q % 2, 0:P], stg[slot][:, (2 * q) * P:(2 * q + 1) * P], ident)
                            tr(ps[:, q % 2, P:2 * P], stg[slot][:, (2 * q + 1) * P:(2 * q + 2) * P],
                               ident).then_inc(s_tr, 1)
                        if q:
                            logits(q - 1)
                    logits(QB - 1)

                loop(pe, EB, body)

            def act_(act):
                a = nc.scalar.activation

                def body(b, half, slot):
                    act.wait_ge(s_free, b + 1)
                    for q in range(QB):
                        act.wait_ge(s_tr, QB * b + q + 1)
                        if l == 0:
                            a(xtb[slot][:, q * 256:(q + 1) * 256], ps[:, q % 2, 0:256],
                              ACT.Identity).then_inc(s_xt, 1)
                            act.wait_ge(s_hm, QB * b + q + 1)
                            a(ht[slot][:, q].rearrange("p h d c -> p (h d c)"), ps[:, 2 + q % 2, :],
                              ACT.Identity, bias=dcol(D_C0)).then_inc(s_ht, 1)
                        else:
                            a(ht[slot][:, q, :, 0, :], ps[:, q % 2, 0:256].rearrange("p (h c) -> p h c", h=2),
                              ACT.Identity).then_inc(s_ht, 1)
                    act.wait_ge(s_lg, QB * b + QB)
                    a(l12v[:, :, bass.ds(b * BT, BT)],
                      ps[:, 4 + slot, 0:12 * BT].rearrange("p (t j) -> p j t", j=12),
                      ACT.Identity).then_inc(s_l12, 1)

                act.sem_inc((s_xt, s_ht)[l], 2)
                act.sem_inc(s_l12, 1)
                loop(act, EB, body)

            return sp_, pe_, act_, sems

        nsx = [0]
        nar = [r2[:, i * HEADS * T:(i + 1) * HEADS * T].rearrange("p (h t) -> p h t", h=HEADS) for i in range(7)]

        def softmax_dve(dve, l):
            v = nc.vector

            def chain(ins):
                ins.then_inc(sx, 1)
                nsx[0] += 1
                dve.wait_ge(sx, nsx[0])

            def scan(o, flag, val, first, op0, op1, rev=False):
                if rev:
                    return v.tensor_tensor_scan(o[:, ::-1], flag[:, ::-1], val[:, ::-1], first, op0, op1)
                return v.tensor_tensor_scan(o, flag, val, first, op0, op1)

            def bt(ap):
                return ap.unsqueeze(1).broadcast_to([P, HEADS, T])

            a_s, a_d, a_sd = (l12v[:, 4 * i:4 * i + 4, :] for i in range(3))
            e, sf, mf, mr, t0, t1, tot = nar
            if l == 1:
                for part in (a_d, a_sd):
                    for h in range(HEADS):
                        chain(v.tensor_tensor(t0[:, h, :], part[:, h, :], last, ALU.mult))
                    for h in range(HEADS):
                        chain(scan(part[:, h, :], nl_f, t0[:, h, :], 0.0, ALU.mult, ALU.add, True))
                    carry_dve(dve, part[:, :, 0], HEADS, row_r, ALU.mult, ALU.add, 0.0, reverse=True)
                    for h in range(HEADS):
                        chain(v.scalar_tensor_tensor(out=part[:, h, :], in0=sm, scalar=carry[:, h:h + 1],
                                                     in1=part[:, h, :], op0=ALU.mult, op1=ALU.add))
            chain(v.tensor_tensor(e, a_s, a_d, ALU.add))
            chain(v.scalar_tensor_tensor(out=e, in0=e, scalar=0.2, in1=e, op0=ALU.mult, op1=ALU.max))
            chain(v.scalar_tensor_tensor(out=sf, in0=a_sd, scalar=0.2, in1=a_sd, op0=ALU.mult, op1=ALU.max))
            chain(v.tensor_tensor(t0, e, sf, ALU.max))
            for h in range(HEADS):
                chain(scan(mf[:, h, :], ns_neg, t0[:, h, :], -BIG, ALU.add, ALU.max))
                chain(scan(mr[:, h, :], nl_neg, t0[:, h, :], -BIG, ALU.add, ALU.max, True))
            carry_dve(dve, mf[:, :, T - 1], HEADS, row_fn, ALU.add, ALU.max, -BIG)
            for h in range(HEADS):
                chain(v.scalar_tensor_tensor(out=mf[:, h, :], in0=pm_neg, scalar=carry[:, h:h + 1],
                                             in1=mf[:, h, :], op0=ALU.add, op1=ALU.max))
            carry_dve(dve, mr[:, :, 0], HEADS, row_rn, ALU.add, ALU.max, -BIG, reverse=True)
            for h in range(HEADS):
                chain(v.scalar_tensor_tensor(out=mr[:, h, :], in0=sm_neg, scalar=carry[:, h:h + 1],
                                             in1=mr[:, h, :], op0=ALU.add, op1=ALU.max))
            chain(v.tensor_tensor(mf, mf, mr, ALU.max))
            chain(v.tensor_tensor(t0, e, mf, ALU.subtract))
            chain(v.tensor_tensor(t1, sf, mf, ALU.subtract))
            dve.sem_inc(sx_act, 1)
            dve.wait_ge(sx_act, 3 * l + 3)
            for h in range(HEADS):
                chain(v.tensor_tensor(sf[:, h, :], t1[:, h, :], last, ALU.mult))
            chain(v.tensor_tensor(t1, e, sf, ALU.add))
            for h in range(HEADS):
                chain(scan(mf[:, h, :], ns_f, t1[:, h, :], 0.0, ALU.mult, ALU.add))
            carry_dve(dve, mf[:, :, T - 1], HEADS, row_f, ALU.mult, ALU.add, 0.0)
            for h in range(HEADS):
                chain(v.scalar_tensor_tensor(out=mf[:, h, :], in0=pm, scalar=carry[:, h:h + 1],
                                             in1=mf[:, h, :], op0=ALU.mult, op1=ALU.add))
            for h in range(HEADS):
                chain(v.tensor_tensor(mr[:, h, :], mf[:, h, :], last, ALU.mult))
            for h in range(HEADS):
                chain(scan(tot[:, h, :], nl_f, mr[:, h, :], 0.0, ALU.mult, ALU.add, True))
            carry_dve(dve, tot[:, :, 0], HEADS, row_r, ALU.mult, ALU.add, 0.0, reverse=True)
            for h in range(HEADS):
                chain(v.scalar_tensor_tensor(out=tot[:, h, :], in0=sm, scalar=carry[:, h:h + 1],
                                             in1=tot[:, h, :], op0=ALU.mult, op1=ALU.add))
            chain(v.tensor_single_scalar(tot, tot, 1e-16, ALU.add))
            chain(v.reciprocal(tot, tot))
            chain(v.tensor_single_scalar(tot, tot, 1.0 / HEADS, ALU.mult))
            chain(v.tensor_tensor(alv[:, 0].rearrange("p t h -> p h t"), e, tot, ALU.mult))
            chain(v.tensor_tensor(alv[:, 1].rearrange("p t h -> p h t"), sf, tot, ALU.mult))

        def softmax_act(act, l):
            e, sf, mf, mr, t0, t1, tot = nar
            act.wait_ge(sx_act, 3 * l + 1)
            nc.scalar.activation(e, t0, ACT.Exp).then_inc(sx_act, 1)
            nc.scalar.activation(t1, t1, ACT.Exp).then_inc(sx_act, 1)

        def softmax_pe(pe, l):
            if l == 1:
                carry_pe(pe, HEADS, reverse=True)
                carry_pe(pe, HEADS, reverse=True)
            carry_pe(pe, HEADS)
            carry_pe(pe, HEADS, reverse=True)
            carry_pe(pe, HEADS)
            carry_pe(pe, HEADS, reverse=True)

        prod = [stage[:, s * 1024:(s + 1) * 1024] for s in range(2)]
        fold = [stage[:, 2048 + s * 512:2560 + s * 512] for s in range(2)]

        def gat_values(l):
            sems = phase_sems(f"v{l}", "in0 in1 mm pr fd y")
            s_in = sems[0:2]
            s_mm, s_pr, s_fd, s_y = sems[2:]
            phase_over(sems)
            PB = 2 * QB

            def sp_(sp):
                def load(b, slot):
                    sp.dma_start(ht_flat[slot], blk(ht_dram[l], b)).then_inc(s_in[slot], 16)

                def body(b, half, slot):
                    sp.wait_ge(s_y, PB * b + 1)
                    load(b + 1, 1 - slot)

                load(0, 0)
                with sp.Fori(0, EB // 2) as i:
                    body(2 * i, i, 0)
                    body(2 * i + 1, i, 1)

            def pe_(pe):
                mm = nc.tensor.matmul

                def body(b, half, slot):
                    pe.wait_ge(s_in[slot], 16 * half + 16)
                    for j in range(PB):
                        pe.wait_ge(s_pr, PB * b + j + 1)
                        for d in range(2):
                            m = mm(ps[:, 2 * (j % 2) + d, :], ht[slot][:, j // 2, j % 2, d, :],
                                   wt[:, W_XW[l]:W_XW[l] + 512], start=True, stop=True)
                        m.then_inc(s_mm, 1)

                loop(pe, EB, body)

            def dve_(dve):
                v = nc.vector

                def finish(b, j):
                    g = j % 2
                    dve.wait_ge(s_pr, PB * b + j + 3)
                    v.tensor_tensor(fold[g], prod[g][:, 0:512], prod[g][:, 512:1024], ALU.add).then_inc(s_fd, 1)
                    dve.wait_ge(s_fd, PB * b + j + 1)
                    v.tensor_reduce(y64[:, :, bass.ds(b * BT + 2 * j, 2)].rearrange("p f t -> p t f"),
                                    fold[g].rearrange("p (t h f) -> p t f h", t=2, h=HEADS),
                                    AX.X, ALU.add).then_inc(s_y, 1)

                def body(b, half, slot):
                    for j in range(PB):
                        g = j % 2
                        dve.wait_ge(s_mm, PB * b + j + 1)
                        v.tensor_tensor(
                            prod[g].rearrange("p (d u f) -> p d u f", d=2, u=2 * HEADS),
                            ps[:, 2 * g:2 * g + 2, :].rearrange("p d (u f) -> p d u f", u=2 * HEADS),
                            alv[:, :, bass.ds(b * BT + 2 * j, 2), :].rearrange("p d t h -> p d (t h)")
                            .unsqueeze(3).broadcast_to([P, 2, 2 * HEADS, HF]),
                            ALU.mult).then_inc(s_pr, 1)
                        if j:
                            finish(b, j - 1)
                    finish(b, PB - 1)

                dve.sem_inc(s_pr, 2)
                loop(dve, EB, body)

            return sp_, pe_, dve_, sems

        nscn = [0]

        def tile_flags(dve, flag):
            nc.vector.tensor_copy(nst[:].rearrange("p (i t) -> p i t", t=T),
                                  flag.unsqueeze(1).broadcast_to([P, 16, T])).then_inc(sc, 1)
            nscn[0] += 1
            dve.wait_ge(sc, nscn[0])

        def scan_y(dve, feats):
            for i in range(feats // 16):
                part = r1[:, i * 16 * T:(i + 1) * 16 * T]
                nc.vector.tensor_tensor_scan(part, nst[:], part, 0.0, ALU.mult, ALU.add).then_inc(sc, 1)
                nscn[0] += 1
            dve.wait_ge(sc, nscn[0])

        ptmp = l12[:, 0:BT * HF]
        pbufs = [nst[:, i * 512:(i + 1) * 512] for i in range(6)] + \
                [alpha[:, i * 512:(i + 1) * 512] for i in range(3)] + [l12[:, 1792:2304]]
        pst, pzc, psq, psd, ptn = (pbufs[2 * i:2 * i + 2] for i in range(5))

        def gat_post(l):
            sems = phase_sems(f"p{l}", "in0 in1 tmp row tr st z zc sq v sd rs tn rl hn to oe free dma")
            s_in = sems[0:2]
            (s_tmp, s_row, s_tr, s_st, s_z, s_zc, s_sq, s_v, s_sd, s_rs, s_tn, s_rl, s_hn, s_to, s_oe,
             s_free, s_dma) = sems[2:]
            phase_over(sems)
            NU = len(UNITS)
            base = [r3[:, s * QB * 512:(s + 1) * QB * 512] for s in range(2)]
            res = [x_[:, 0:QB * 256] for x_ in base]
            hout = [x_[:, QB * 256:QB * 512] for x_ in base]
            xin = [r2[:, T * XF + s * QB * P:T * XF + (s + 1) * QB * P] for s in range(2)]
            per = 1 + l

            def sp_(sp):
                def load(b, slot):
                    if l == 0:
                        sp.dma_start(res[slot].rearrange("p (q h c) -> p q h c", q=QB, h=2),
                                     blk(ht_dram[0], b).rearrange("p (q h d c) -> p q h d c", q=QB, h=2, d=2)
                                     [:, :, :, 1, :]).then_inc(s_in[slot], 16)
                    else:
                        sp.dma_start(res[slot], blk(h1d_dram, b)).then_inc(s_in[slot], 16)
                        sp.dma_start(xin[slot].rearrange("p (q c) -> p q c", q=QB),
                                     blk(xt_dram, b).rearrange("p (q d c) -> p q d c", q=QB, d=2)
                                     [:, :, 1, :]).then_inc(s_in[slot], 16)

                def body(b, half, slot, ahead=True):
                    if ahead:
                        sp.wait_ge(s_oe, NU * b + 2)
                        load(b + 1, 1 - slot)
                    if l == 0:
                        sp.wait_ge(s_hn, NU * b + NU)
                        sp.dma_start(blk(h1d_dram, b), hout[slot]).then_inc(s_dma, 16)
                        sp.wait_ge(s_dma, 16 * b + 16)
                        sp.sem_inc(s_free, 1)

                if l == 0:
                    sp.sem_inc(s_free, 2)
                load(0, 0)
                with sp.Fori(0, EB // 2) as i:
                    body(2 * i, i, 0)
                    body(2 * i + 1, i, 1)
                body(EB - 1, EB // 2, 0, ahead=False)

            def pe_(pe):
                mm, tr = nc.tensor.matmul, nc.tensor.transpose

                def body(b, half, slot):
                    pe.wait_ge(s_row, b + 1)
                    for u, (q0, nq) in enumerate(UNITS):
                        n, g, w = nq * 256, u % 2, NU * b + u
                        pe.wait_ge(s_oe, w + 1)
                        for j in range(2 * nq):
                            c = (2 * q0 + j) * P
                            t = tr(ps[:, g, j * P:(j + 1) * P], stg[slot][:, c:c + P], ident)
                        t.then_inc(s_tr, 1)
                        pe.wait_ge(s_st, w + 1)
                        mm(ps[:, 2 + g, 0:n], k(K_C64), pst[g][:, 0:n], start=True, stop=True).then_inc(s_z, 1)
                        pe.wait_ge(s_sq, per * w + 1)
                        mm(ps[:, 4 + g, 0:n], k(K_J64), psq[g][:, 0:n], start=True, stop=True).then_inc(s_v, 1)
                        pe.wait_ge(s_hn, w + 1)
                        ho = hout[slot][:, q0 * 256:q0 * 256 + n]
                        if l == 0:
                            for j in range(2 * nq):
                                t = tr(ps[:, 6 + g, j * P:(j + 1) * P], ho[:, j * P:(j + 1) * P], ident)
                            t.then_inc(s_to, 1)
                        else:
                            m = nq * P
                            hv = ho.rearrange("p (q h c) -> p q h c", q=nq, h=2)
                            pe.wait_ge(s_in[slot], 32 * half + 32)
                            mm(ps[:, 6 + g, 0:m], k(K_C32), xin[slot][:, q0 * P:q0 * P + m],
                               start=True, stop=False)
                            mm(ps[:, 6 + g, 0:m], dv[:, D_OA:D_OA + P], hv[:, :, 0, :], start=False, stop=False)
                            mm(ps[:, 6 + g, 0:m], dv[:, D_OB:D_OB + P], hv[:, :, 1, :],
                               start=False, stop=True).then_inc(s_z, 1)
                            pe.wait_ge(s_sq, 2 * w + 2)
                            mm(ps[:, 4 + g, 0:m], k(K_J32), psq[g][:, 0:m], start=True, stop=True)\
                                .then_inc(s_v, 1)
                            pe.wait_ge(s_tn, 2 * w + 2)
                            for j in range(nq):
                                t = tr(ps[:, g, j * P:(j + 1) * P], ptn[g][:, j * P:(j + 1) * P], ident)
                            t.then_inc(s_to, 1)

                loop(pe, EB, body)

            def act_(act):
                a = nc.scalar.activation

                def body(b, half, slot):
                    for u, (q0, nq) in enumerate(UNITS):
                        n, g, w = nq * 256, u % 2, NU * b + u
                        act.wait_ge(s_tr, w + 1)
                        a(pst[g][:, 0:n], ps[:, g, 0:n], ACT.Identity).then_inc(s_st, 1)
                        act.wait_ge(s_z, per * w + 1)
                        a(pzc[g][:, 0:n], ps[:, 2 + g, 0:n], ACT.Identity, bias=dcol(D_BC[l])).then_inc(s_zc, 1)
                        a(psq[g][:, 0:n], ps[:, 2 + g, 0:n], ACT.Square, bias=dcol(D_BC[l])).then_inc(s_sq, 1)
                        act.wait_ge(s_v, per * w + 1)
                        a(psd[g][:, 0:n], ps[:, 4 + g, 0:n], ACT.Sqrt, bias=dcol(D_EPS)).then_inc(s_sd, 1)
                        act.wait_ge(s_tn, per * w + 1)
                        a(ptn[g][:, 0:n], ptn[g][:, 0:n], ACT.Relu, bias=col(C_B[l]), scale=col(C_G[l]))\
                            .then_inc(s_rl, 1)
                        if l == 1:
                            m = nq * P
                            act.wait_ge(s_z, 2 * w + 2)
                            a(pzc[g][:, 0:m], ps[:, 6 + g, 0:m], ACT.Identity, bias=dcol(D_OBC)).then_inc(s_zc, 1)
                            a(psq[g][:, 0:m], ps[:, 6 + g, 0:m], ACT.Square, bias=dcol(D_OBC)).then_inc(s_sq, 1)
                            act.wait_ge(s_v, 2 * w + 2)
                            a(psd[g][:, 0:m], ps[:, 4 + g, 0:m], ACT.Sqrt, bias=dcol(D_EPS)).then_inc(s_sd, 1)

                loop(act, EB, body)

            def dve_(dve):
                v = nc.vector

                def sums(b, slot):
                    v.tensor_tensor(ptmp.rearrange("p (t f) -> p t f", f=HF),
                                    pm[:, bass.ds(b * BT, BT)].unsqueeze(2).broadcast_to([P, BT, HF]),
                                    carry[:, 0:HF].unsqueeze(1).broadcast_to([P, BT, HF]),
                                    ALU.mult).then_inc(s_tmp, 1)
                    dve.wait_ge(s_tmp, b + 1)
                    v.tensor_tensor(stg[slot].rearrange("p (t f) -> p t f", f=HF),
                                    y64[:, :, bass.ds(b * BT, BT)].rearrange("p f t -> p t f"),
                                    ptmp.rearrange("p (t f) -> p t f", f=HF), ALU.add).then_inc(s_row, 1)

                def norm(w, g, n):
                    dve.wait_ge(s_sd, w + 1)
                    v.reciprocal(psd[g][:, 0:n], psd[g][:, 0:n]).then_inc(s_rs, 1)
                    dve.wait_ge(s_rs, w + 1)
                    dve.wait_ge(s_zc, w + 1)
                    v.tensor_tensor(ptn[g][:, 0:n], pzc[g][:, 0:n], psd[g][:, 0:n], ALU.mult).then_inc(s_tn, 1)

                def body(b, half, slot):
                    sums(b, slot)
                    if l == 0:
                        dve.wait_ge(s_free, b + 1)
                    dve.wait_ge(s_in[slot], (16 + 16 * l) * half + (16 + 16 * l))
                    for u, (q0, nq) in enumerate(UNITS):
                        n, g, w = nq * 256, u % 2, NU * b + u
                        norm(per * w, g, n)
                        dve.wait_ge(s_rl, w + 1)
                        v.tensor_tensor(hout[slot][:, q0 * 256:q0 * 256 + n], res[slot][:, q0 * 256:q0 * 256 + n],
                                        ptn[g][:, 0:n], ALU.add).then_inc(s_hn, 1)
                        if l == 0:
                            dve.wait_ge(s_to, w + 1)
                            v.tensor_copy(r2[:, bass.ds(b * (BT * HF) + q0 * 256, n)],
                                          ps[:, 6 + g, 0:n]).then_inc(s_oe, 1)
                        else:
                            norm(2 * w + 1, g, nq * P)
                            dve.wait_ge(s_to, w + 1)
                            v.tensor_copy(r2[:, bass.ds(b * (BT * XF) + q0 * P, nq * P)],
                                          ps[:, g, 0:nq * P]).then_inc(s_oe, 1)

                dve.sem_inc(s_oe, 2)
                loop(dve, EB, body)

            return sp_, pe_, act_, dve_, sems

        off[0] = 0
        gxr, gx, gh, g_r, g_z, g_u, g_n, g_d, go = ([lay(r2, 512) for _ in range(2)] for _ in range(9))
        gru_sems = phase_sems("q", "in0 in1 tr x mm rz u n dc h y c zc sq v sd rs o to oe free st")
        gi = gru_sems[0:2]
        (q_tr, q_x, q_mm, q_rz, q_u, q_n, q_dc, q_h, q_y, q_c, q_zc, q_sq, q_v, q_sd, q_rs, q_o, q_to, q_oe,
         q_free, q_st) = gru_sems[2:]
        phase_over(gru_sems)

        def gate(w, g):
            return wt[:, w + g * P:w + (g + 1) * P]

        def pairs(eng, n, body):
            with eng.Fori(0, n // 2) as i:
                body(2 * i, i, 2)
            body(n - 1, n // 2, 1)

        def dgru_sp(sp):
            def load(b, slot):
                sp.dma_start(gxr[slot], blk(x1_blk, b)).then_inc(gi[slot], 16)

            def body(b, i, ns):
                for s in range(ns):
                    sp.wait_ge(q_oe, b + s + 2 + 1)
                    sp.dma_start(blk(out_blk, b + s), go[s]).then_inc(q_st, 16)
                    sp.wait_ge(q_st, 16 * b + 16 * s + 16)
                    sp.sem_inc(q_free, 1)

            sp.wait_ge(put_x1, ALL)
            sp.sem_inc(q_free, 2)
            load(0, 0)
            load(1, 1)
            with sp.Fori(0, DB // 2 - 1) as i:
                sp.wait_ge(q_tr, 2 * i + 2)
                load(2 * i + 2, 0)
                load(2 * i + 3, 1)
                body(2 * i, i, 2)
            sp.wait_ge(q_tr, DB - 1)
            load(DB - 1, 0)
            body(DB - 3, DB // 2 - 1, 2)
            body(DB - 1, DB // 2, 1)
            sp.sem_inc(out_done, 1)

        def dgru_pe(pe):
            mm, tr = nc.tensor.matmul, nc.tensor.transpose

            def body(b, i, ns):
                for s in range(ns):
                    pe.wait_ge(gi[s], 16 * i + 16)
                    pe.wait_ge(q_oe, b + s + 1)
                    for j in range(4):
                        t = tr(ps[:, 6 + s, j * P:(j + 1) * P], gxr[s][:, j * P:(j + 1) * P], ident)
                    t.then_inc(q_tr, 1)
                for st in range(STEPS):
                    for s in range(ns):
                        c = 8 * i + ns * st + s
                        if st == 0:
                            pe.wait_ge(q_x, b + s + 1)
                        else:
                            pe.wait_ge(q_h, c - ns + 1)
                        for g in range(3):
                            mm(ps[:, 3 * s + g, :], gate(W_HH, g), (gx if st == 0 else gh)[s],
                               start=True, stop=True).then_inc(q_mm, 1)
                for s in range(ns):
                    pe.wait_ge(q_y, b + s + 1)
                    mm(ps[:, 3 * s, :], k(K_C32), g_u[s], start=True, stop=True).then_inc(q_c, 1)
                for s in range(ns):
                    pe.wait_ge(q_sq, b + s + 1)
                    mm(ps[:, 3 * s + 1, :], k(K_J32), g_z[s], start=True, stop=True).then_inc(q_v, 1)
                for s in range(ns):
                    pe.wait_ge(q_o, b + s + 1)
                    for j in range(4):
                        t = tr(ps[:, 6 + s, j * P:(j + 1) * P], g_d[s][:, j * P:(j + 1) * P], ident)
                    t.then_inc(q_to, 1)

            pairs(pe, DB, body)

        def dgru_act(act):
            a = nc.scalar.activation

            def body(b, i, ns):
                for s in range(ns):
                    act.wait_ge(q_tr, b + s + 1)
                    a(gx[s], ps[:, 6 + s, :], ACT.Identity).then_inc(q_x, 1)
                for st in range(STEPS):
                    for s in range(ns):
                        c = 8 * i + ns * st + s
                        act.wait_ge(q_mm, 3 * c + 1)
                        a(g_r[s], ps[:, 3 * s, :], ACT.Sigmoid, bias=dcol(D_BR)).then_inc(q_rz, 1)
                        act.wait_ge(q_mm, 3 * c + 2)
                        a(g_z[s], ps[:, 3 * s + 1, :], ACT.Sigmoid, bias=dcol(D_BZ)).then_inc(q_rz, 1)
                    for s in range(ns):
                        c = 8 * i + ns * st + s
                        act.wait_ge(q_u, c + 1)
                        a(g_n[s], g_u[s], ACT.Tanh, bias=col(C_BIHN)).then_inc(q_n, 1)
                for s in range(ns):
                    act.wait_ge(q_c, b + s + 1)
                    a(g_r[s], ps[:, 3 * s, :], ACT.Identity).then_inc(q_zc, 1)
                    a(g_z[s], ps[:, 3 * s, :], ACT.Square).then_inc(q_sq, 1)
                for s in range(ns):
                    act.wait_ge(q_v, b + s + 1)
                    a(g_n[s], ps[:, 3 * s + 1, :], ACT.Sqrt, bias=dcol(D_EPS)).then_inc(q_sd, 1)

            pairs(act, DB, body)

        def dgru_dve(dve):
            v = nc.vector

            def body(b, i, ns):
                for st in range(STEPS):
                    for s in range(ns):
                        c = 8 * i + ns * st + s
                        dve.wait_ge(q_mm, 3 * c + 3)
                        dve.wait_ge(q_rz, 2 * c + 1)
                        v.scalar_tensor_tensor(out=g_u[s], in0=ps[:, 3 * s + 2, :], scalar=col(C_BHHN),
                                               in1=g_r[s], op0=ALU.add, op1=ALU.mult).then_inc(q_u, 1)
                    for s in range(ns):
                        c = 8 * i + ns * st + s
                        dve.wait_ge(q_n, c + 1)
                        v.tensor_tensor(g_d[s], (gx if st == 0 else gh)[s], g_n[s], ALU.subtract)\
                            .then_inc(q_dc, 1)
                        dve.wait_ge(q_dc, 2 * c + 1)
                        dve.wait_ge(q_rz, 2 * c + 2)
                        v.tensor_tensor(g_d[s], g_d[s], g_z[s], ALU.mult).then_inc(q_dc, 1)
                        dve.wait_ge(q_dc, 2 * c + 2)
                        v.tensor_tensor(gh[s], g_d[s], g_n[s], ALU.add).then_inc(q_h, 1)
                for s in range(ns):
                    dve.wait_ge(q_h, 8 * i + ns * (STEPS - 1) + s + 1)
                    v.tensor_tensor(g_u[s], gx[s], gh[s], ALU.add).then_inc(q_y, 1)
                for s in range(ns):
                    dve.wait_ge(q_sd, b + s + 1)
                    v.reciprocal(g_n[s], g_n[s]).then_inc(q_rs, 1)
                    dve.wait_ge(q_rs, b + s + 1)
                    dve.wait_ge(q_zc, b + s + 1)
                    v.tensor_tensor(g_d[s], g_r[s], g_n[s], ALU.mult).then_inc(q_o, 1)
                for s in range(ns):
                    dve.wait_ge(q_to, b + s + 1)
                    dve.wait_ge(q_free, b + s + 1)
                    v.tensor_copy(go[s], ps[:, 6 + s, :]).then_inc(q_oe, 1)

            dve.sem_inc(q_oe, 2)
            pairs(dve, DB, body)

        hs = r2[:, T * XF:2 * T * XF]
        work = r2[:, T * BONDF:T * XF]
        bondv = r2[:, 0:T * BONDF].rearrange("p (t c) -> p t c", c=BONDF)
        hd = r3[:, 0:T * XF]
        y32 = r1[:, 0:T * XF].rearrange("p (f t) -> p f t", t=T)
        ag = r1[:, T * XF:2 * T * XF]
        uw = l12[:, 0:4 * 512]
        vb = l12[:, 2048:2048 + P]
        mi = [sem(f"mi_in{s}") for s in range(2)]
        mi_tr, mi_cp, ld_bond, ld_uw = sem("mi_tr"), sem("mi_cp"), sem("ld_bond"), sem("ld_uw")

        def init_sp(sp):
            def load(b, slot):
                sp.dma_start(stg[slot].rearrange("p (d c) -> p d c", d=2),
                             r1[:].rearrange("p (d c) -> p d c", d=2)[:, :, bass.ds(b * SB, SB)])\
                    .then_inc(mi[slot], 16)

            sp.dma_start(bondv, sort_s[1:EP + 1, 2:PAY].rearrange("(p t) c -> p t c", t=T)).then_inc(ld_bond, 16)
            sp.dma_start(l12[:, 0:2176], bondw).then_inc(ld_uw, 16)
            sp.wait_ge(got_x1, 2 * ALL)
            load(0, 0)
            with sp.Fori(0, EB // 2) as i:
                for s in range(2):
                    sp.wait_ge(mi_cp, 4 * i + 2 * s + 1)
                    load(2 * i + s + 1, 1 - s)

        def init_pe(pe):
            tr = nc.tensor.transpose

            def body(b, half, slot):
                pe.wait_ge(mi[slot], 16 * half + 16)
                pe.wait_ge(mi_cp, 2 * b + 1)
                for d in range(2):
                    for q in range(QB):
                        t = tr(ps[:, 2 * d + q // 4, (q % 4) * P:(q % 4 + 1) * P],
                               stg[slot][:, d * SB + q * P:d * SB + (q + 1) * P], ident)
                t.then_inc(mi_tr, 1)

            loop(pe, EB, body)

        def init_act(act):
            a = nc.scalar.activation

            def body(b, half, slot):
                act.wait_ge(mi_tr, b + 1)
                for o, d in ((hs, 0), (hd, 1)):
                    for p, (c, n) in enumerate(PARTS):
                        last_ = a(o[:, bass.ds(b * SB + c, n)], ps[:, 2 * d + p, 0:n], ACT.Identity)
                last_.then_inc(mi_cp, 2)

            act.sem_inc(mi_cp, 1)
            loop(act, EB, body)

        mg = [sem(f"mg_in{s}") for s in range(2)]
        mg_mm, mg_v, mg_pr, mg_rd, mg_y = (sem(f"mg_{n}") for n in ("mm", "v", "pr", "rd", "y"))
        hq = [stage[:, s * SB:(s + 1) * SB] for s in range(2)]
        msum = stage[:, 2 * SB:2 * SB + P]
        mprod = [nst[:, s * 1024:(s + 1) * 1024] for s in range(2)]
        uw4 = uw.rearrange("p (q c) -> p q c", q=4)
        PB = 2 * QB

        def msg_sp(sp, m):
            def load(b, slot):
                sp.dma_start(hq[slot], hd[:, bass.ds(b * SB, SB)]).then_inc(mg[slot], 16)

            load(0, 0)
            with sp.Fori(0, EB // 2) as i:
                for s in range(2):
                    sp.wait_ge(mg_y, QB * EB * m + 2 * QB * i + QB * s + 1)
                    load(2 * i + s + 1, 1 - s)

        def msg_pe(pe, m):
            mm = nc.tensor.matmul

            def body(b, half, slot):
                pe.wait_ge(mg[slot], 16 * (4 - slot) * m + 16 * half + 16)
                for q in range(QB):
                    lhs = hq[slot][:, q * P:(q + 1) * P]
                    for r in range(2):
                        w = PB * EB * m + PB * b + 2 * q + r
                        pe.wait_ge(mg_pr, w + 1)
                        for j in range(2):
                            t = mm(ps[:, 2 * r + j, :], lhs, uw4[:, 2 * r + j, :], start=True, stop=True)
                        t.then_inc(mg_mm, 1)
                    mm(ps[:, 4 + (slot + q) % 2, 0:P], lhs, vb, start=True, stop=True).then_inc(mg_v, 1)

            loop(pe, EB, body)

        def msg_dve(dve, m):
            v = nc.vector

            def reduce(w, r):
                dve.wait_ge(mg_pr, w + 3)
                v.tensor_reduce(msum[:, r * 64:(r + 1) * 64],
                                mprod[r].rearrange("p (u k) -> p u k", k=BONDF), AX.X, ALU.add).then_inc(mg_rd, 1)

            def body(b, half, slot):
                for q in range(QB):
                    w = PB * EB * m + PB * b + 2 * q
                    for r in range(2):
                        dve.wait_ge(mg_mm, w + r + 1)
                        v.tensor_tensor(
                            mprod[r].rearrange("p (t i k) -> p t i k", t=2, k=BONDF),
                            ps[:, 2 * r:2 * r + 2, :].rearrange("p t (i k) -> p t i k", k=BONDF),
                            bondv[:, bass.ds(b * BT + 4 * q + 2 * r, 2), :].unsqueeze(2)
                            .broadcast_to([P, 2, XF, BONDF]), ALU.mult).then_inc(mg_pr, 1)
                    for r in range(2):
                        reduce(w + r, r)
                    u = QB * EB * m + QB * b + q
                    dve.wait_ge(mg_v, u + 1)
                    dve.wait_ge(mg_rd, w + 2)
                    v.tensor_tensor(y32[:, :, bass.ds(b * BT + 4 * q, 4)].rearrange("p f t -> p t f"),
                                    msum.rearrange("p (t f) -> p t f", f=XF),
                                    ps[:, 4 + (slot + q) % 2, 0:P].rearrange("p (t f) -> p t f", f=XF),
                                    ALU.add).then_inc(mg_y, 1)
                    dve.wait_ge(mg_y, u + 2)

            if m == 0:
                dve.sem_inc(mg_pr, 2)
                dve.sem_inc(mg_y, 1)
            loop(dve, EB, body)

        eg = []
        for who in range(2):
            eg.append({n: sem(f"e{who}_{n}") for n in (
                "in0", "in1", "tmp", "row", "tr", "at", "mm", "rz", "u", "n", "dc", "h", "free", "st")})
        ering = [stage[:, s * SB:(s + 1) * SB] for s in range(2)]
        etmp = stage[:, 2 * SB:3 * SB]
        e_at, e_r, e_z = ([nst[:, i * SB + c:i * SB + c + n] for c, n in PARTS] for i in range(3))
        e_u, e_n, e_d = ([work[:, i * SB + c:i * SB + c + n] for c, n in PARTS] for i in range(3))

        def egru_sp(sp, m, who):
            s = eg[who]
            if who == 0:
                if m == STEPS - 1:
                    return

                def body(b, half, slot):
                    sp.wait_ge(s["row"], EB * m + b + 1)
                    sp.dma_start(agg_tab[0:EP, :].rearrange("(p t) f -> p (t f)", t=T)
                                 [:, bass.ds(b * SB, SB)], ering[slot]).then_inc(s["st"], 16)
                    sp.wait_ge(s["st"], 16 * EB * m + 16 * b + 16)
                    sp.sem_inc(s["free"], 1)

                loop(sp, EB, body)
                sp.sem_inc(agg_stored, 1)
            else:
                def load(b, slot):
                    sp.dma_start(ering[slot], ag[:, bass.ds(b * SB, SB)]).then_inc(s[f"in{slot}"], 16)

                sp.wait_ge(got_agg, ALL * (m + 1))
                load(0, 0)
                with sp.Fori(0, EB // 2) as i:
                    for t in range(2):
                        sp.wait_ge(s["h"], 2 * EB * m + 4 * i + 2 * t + 2)
                        load(2 * i + t + 1, 1 - t)

        def egru_pe(pe, m, who):
            s = eg[who]
            state = (hs, hd)[who]
            mm, tr = nc.tensor.matmul, nc.tensor.transpose

            def body(b, half, slot):
                if who == 0:
                    pe.wait_ge(s["row"], EB * m + b + 1)
                else:
                    pe.wait_ge(s[f"in{slot}"], 16 * (4 - slot) * m + 16 * half + 16)
                for p, (c, n) in enumerate(PARTS):
                    w = 2 * EB * m + 2 * b + p
                    pe.wait_ge(s["h"], w + 1)
                    for j in range(n // P):
                        t = tr(ps[:, 4 * p + 3, j * P:(j + 1) * P], ering[slot][:, c + j * P:c + (j + 1) * P],
                               ident)
                    t.then_inc(s["tr"], 1)
                for p, (c, n) in enumerate(PARTS):
                    w = 2 * EB * m + 2 * b + p
                    h = state[:, bass.ds(b * SB + c, n)]
                    a = e_at[p][:, 0:n]
                    pe.wait_ge(s["at"], w + 1)
                    for g in range(2):
                        mm(ps[:, 4 * p + g, 0:n], gate(W_IH, g), a, start=True, stop=False)
                        mm(ps[:, 4 * p + g, 0:n], gate(W_HH, g), h, start=False, stop=True).then_inc(s["mm"], 1)
                    mm(ps[:, 4 * p + 2, 0:n], gate(W_HH, 2), h, start=True, stop=True).then_inc(s["mm"], 1)
                    mm(ps[:, 4 * p + 3, 0:n], gate(W_IH, 2), a, start=True, stop=True).then_inc(s["mm"], 1)

            loop(pe, EB, body)

        def egru_act(act, m, who):
            s = eg[who]
            a = nc.scalar.activation

            def body(b, half, slot):
                for p, (c, n) in enumerate(PARTS):
                    w = 2 * EB * m + 2 * b + p
                    act.wait_ge(s["tr"], w + 1)
                    a(e_at[p][:, 0:n], ps[:, 4 * p + 3, 0:n], ACT.Identity).then_inc(s["at"], 1)
                for p, (c, n) in enumerate(PARTS):
                    w = 2 * EB * m + 2 * b + p
                    act.wait_ge(s["mm"], 4 * w + 1)
                    a(e_r[p][:, 0:n], ps[:, 4 * p, 0:n], ACT.Sigmoid, bias=dcol(D_BR)).then_inc(s["rz"], 1)
                    act.wait_ge(s["mm"], 4 * w + 2)
                    a(e_z[p][:, 0:n], ps[:, 4 * p + 1, 0:n], ACT.Sigmoid, bias=dcol(D_BZ)).then_inc(s["rz"], 1)
                for p, (c, n) in enumerate(PARTS):
                    w = 2 * EB * m + 2 * b + p
                    act.wait_ge(s["u"], w + 1)
                    a(e_n[p][:, 0:n], e_u[p][:, 0:n], ACT.Tanh, bias=col(C_BIHN)).then_inc(s["n"], 1)

            loop(act, EB, body)

        def egru_dve(dve, m, who):
            s = eg[who]
            state = (hs, hd)[who]
            v = nc.vector

            def body(b, half, slot):
                if who == 0:
                    if m < STEPS - 1:
                        dve.wait_ge(s["free"], EB * m + b + 1)
                    v.tensor_tensor(etmp.rearrange("p (t f) -> p t f", f=XF),
                                    pm_s[:, bass.ds(b * BT, BT)].unsqueeze(2).broadcast_to([P, BT, XF]),
                                    carry[:, 0:XF].unsqueeze(1).broadcast_to([P, BT, XF]),
                                    ALU.mult).then_inc(s["tmp"], 1)
                    dve.wait_ge(s["tmp"], EB * m + b + 1)
                    v.tensor_tensor(ering[slot].rearrange("p (t f) -> p t f", f=XF),
                                    y32[:, :, bass.ds(b * BT, BT)].rearrange("p f t -> p t f"),
                                    etmp.rearrange("p (t f) -> p t f", f=XF), ALU.add).then_inc(s["row"], 1)
                for p, (c, n) in enumerate(PARTS):
                    w = 2 * EB * m + 2 * b + p
                    dve.wait_ge(s["mm"], 4 * w + 3)
                    dve.wait_ge(s["rz"], 2 * w + 1)
                    v.scalar_tensor_tensor(out=e_u[p][:, 0:n], in0=ps[:, 4 * p + 2, 0:n], scalar=col(C_BHHN),
                                           in1=e_r[p][:, 0:n], op0=ALU.add, op1=ALU.mult).then_inc(s["dc"], 1)
                    dve.wait_ge(s["dc"], 6 * EB * m + 6 * b + p + 1)
                    dve.wait_ge(s["mm"], 4 * w + 4)
                    v.tensor_tensor(e_u[p][:, 0:n], e_u[p][:, 0:n], ps[:, 4 * p + 3, 0:n], ALU.add)\
                        .then_inc(s["u"], 1)
                for p, (c, n) in enumerate(PARTS):
                    w = 2 * EB * m + 2 * b + p
                    h = state[:, bass.ds(b * SB + c, n)]
                    dve.wait_ge(s["n"], w + 1)
                    v.tensor_tensor(e_d[p][:, 0:n], h, e_n[p][:, 0:n], ALU.subtract).then_inc(s["dc"], 1)
                    dve.wait_ge(s["dc"], 6 * EB * m + 6 * b + 2 * p + 3)
                    dve.wait_ge(s["rz"], 2 * w + 2)
                    v.tensor_tensor(e_d[p][:, 0:n], e_d[p][:, 0:n], e_z[p][:, 0:n], ALU.mult)\
                        .then_inc(s["dc"], 1)
                    dve.wait_ge(s["dc"], 6 * EB * m + 6 * b + 2 * p + 4)
                    v.tensor_tensor(h, e_d[p][:, 0:n], e_n[p][:, 0:n], ALU.add).then_inc(s["h"], 1)

            if m == 0:
                dve.sem_inc(s["h"], 2)
                if who == 0:
                    dve.sem_inc(s["free"], 2)
            loop(dve, EB, body)

        x1s = ag
        fin_rows = r3[:, 0:T * XF]
        fs = {n: sem(f"f_{n}") for n in ("ld", "y", "c", "zc", "sq", "v", "sd", "rs", "o", "to", "oe", "keep")}

        def keep_sp(sp):
            sp.dma_start(xs_dram, hs).then_inc(fs["keep"], 16)
            sp.wait_ge(fs["keep"], 16)

        def final_sp(sp):
            sp.dma_start(x1s, xs_dram).then_inc(fs["ld"], 16)

        def final_pe(pe):
            mm, tr = nc.tensor.matmul, nc.tensor.transpose

            def body(b, half, slot):
                for p, (c, n) in enumerate(PARTS):
                    w = 2 * b + p
                    pe.wait_ge(fs["y"], w + 1)
                    mm(ps[:, 4 * p, 0:n], k(K_C32), e_u[p], start=True, stop=True).then_inc(fs["c"], 1)
                for p, (c, n) in enumerate(PARTS):
                    w = 2 * b + p
                    pe.wait_ge(fs["sq"], w + 1)
                    mm(ps[:, 4 * p + 1, 0:n], k(K_J32), e_z[p], start=True, stop=True).then_inc(fs["v"], 1)
                for p, (c, n) in enumerate(PARTS):
                    w = 2 * b + p
                    pe.wait_ge(fs["o"], w + 1)
                    for j in range(n // P):
                        t = tr(ps[:, 4 * p + 2, j * P:(j + 1) * P], e_d[p][:, j * P:(j + 1) * P], ident)
                    t.then_inc(fs["to"], 1)

            loop(pe, EB, body)

        def final_act(act):
            a = nc.scalar.activation

            def body(b, half, slot):
                for p, (c, n) in enumerate(PARTS):
                    act.wait_ge(fs["c"], 2 * b + p + 1)
                    a(e_r[p], ps[:, 4 * p, 0:n], ACT.Identity).then_inc(fs["zc"], 1)
                    a(e_z[p], ps[:, 4 * p, 0:n], ACT.Square).then_inc(fs["sq"], 1)
                for p, (c, n) in enumerate(PARTS):
                    act.wait_ge(fs["v"], 2 * b + p + 1)
                    a(e_n[p], ps[:, 4 * p + 1, 0:n], ACT.Sqrt, bias=dcol(D_EPS)).then_inc(fs["sd"], 1)

            loop(act, EB, body)

        def final_dve(dve):
            v = nc.vector

            def body(b, half, slot):
                for p, (c, n) in enumerate(PARTS):
                    v.tensor_tensor(e_u[p], x1s[:, bass.ds(b * SB + c, n)], hs[:, bass.ds(b * SB + c, n)],
                                    ALU.add).then_inc(fs["y"], 1)
                for p, (c, n) in enumerate(PARTS):
                    w = 2 * b + p
                    dve.wait_ge(fs["sd"], w + 1)
                    v.reciprocal(e_n[p], e_n[p]).then_inc(fs["rs"], 1)
                    dve.wait_ge(fs["rs"], w + 1)
                    dve.wait_ge(fs["zc"], w + 1)
                    v.tensor_tensor(e_d[p], e_r[p], e_n[p], ALU.mult).then_inc(fs["o"], 1)
                for p, (c, n) in enumerate(PARTS):
                    dve.wait_ge(fs["to"], 2 * b + p + 1)
                    v.tensor_copy(fin_rows[:, bass.ds(b * SB + c, n)], ps[:, 4 * p + 2, 0:n])\
                        .then_inc(fs["oe"], 1)

            dve.wait_ge(fs["ld"], 16)
            loop(dve, EB, body)

        log0, log1 = gat_logits(0), gat_logits(1)
        val0, val1 = gat_values(0), gat_values(1)
        post0, post1 = gat_post(0), gat_post(1)
        block = ctx.enter_context(nc.Block())

        @block.sync
        def _(sp):
            prep_sp(sp)
            sort_sp(sp)
            barrier(sp, "sp")
            dense_sp(sp)
            barrier(sp, "sp", dense_sems)
            for log, val, post in ((log0, val0, post0), (log1, val1, post1)):
                log[0](sp)
                barrier(sp, "sp", log[-1])
                val[0](sp)
                barrier(sp, "sp", val[-1])
                post[0](sp)
                barrier(sp, "sp", post[-1])
            dgru_sp(sp)
            barrier(sp, "sp", gru_sems)
            init_sp(sp)
            barrier(sp, "sp")
            keep_sp(sp)
            for m in range(STEPS):
                msg_sp(sp, m)
                barrier(sp, "sp")
                egru_sp(sp, m, 0)
                barrier(sp, "sp")
                if m < STEPS - 1:
                    egru_sp(sp, m, 1)
                    barrier(sp, "sp")
            final_sp(sp)
            sp.wait_ge(put_out, ALL)

        @block.tensor
        def _(pe):
            prep_pe_(pe)
            sort_pe(pe)
            barrier(pe, "pe")
            dense_pe(pe)
            barrier(pe, "pe")
            flags_pe(pe)
            for l, (log, val, post) in enumerate(((log0, val0, post0), (log1, val1, post1))):
                log[1](pe)
                barrier(pe, "pe")
                softmax_pe(pe, l)
                val[1](pe)
                barrier(pe, "pe")
                carry_pe(pe, HF)
                post[1](pe)
                barrier(pe, "pe")
            dgru_pe(pe)
            barrier(pe, "pe")
            init_pe(pe)
            barrier(pe, "pe")
            for m in range(STEPS):
                msg_pe(pe, m)
                barrier(pe, "pe")
                carry_pe(pe, XF)
                egru_pe(pe, m, 0)
                barrier(pe, "pe")
                if m < STEPS - 1:
                    egru_pe(pe, m, 1)
                    barrier(pe, "pe")
            final_pe(pe)

        @block.scalar
        def _(act):
            barrier(act, "act")
            dense_act(act)
            barrier(act, "act")
            for l, (log, val, post) in enumerate(((log0, val0, post0), (log1, val1, post1))):
                log[2](act)
                barrier(act, "act")
                softmax_act(act, l)
                barrier(act, "act")
                post[2](act)
                barrier(act, "act")
            dgru_act(act)
            barrier(act, "act")
            init_act(act)
            barrier(act, "act")
            for m in range(STEPS):
                barrier(act, "act")
                egru_act(act, m, 0)
                barrier(act, "act")
                if m < STEPS - 1:
                    egru_act(act, m, 1)
                    barrier(act, "act")
            final_act(act)

        @block.vector
        def _(dve):
            prep_dve_(dve)
            sort_dve(dve)
            barrier(dve, "dve")
            dense_dve(dve)
            barrier(dve, "dve")
            flags_dve(dve)
            for l, (log, val, post) in enumerate(((log0, val0, post0), (log1, val1, post1))):
                barrier(dve, "dve")
                softmax_dve(dve, l)
                tile_flags(dve, ns_f)
                val[2](dve)
                barrier(dve, "dve")
                scan_y(dve, HF)
                carry_dve(dve, y64[:, :, T - 1], HF, row_f, ALU.mult, ALU.add, 0.0)
                post[3](dve)
                dve.drain().then_inc(rows_ready, 1)
                barrier(dve, "dve")
            dgru_dve(dve)
            barrier(dve, "dve")
            barrier(dve, "dve")
            dve.wait_ge(ld_bond, 16)
            for m in range(STEPS):
                msg_dve(dve, m)
                barrier(dve, "dve")
                tile_flags(dve, ns_fs)
                scan_y(dve, XF)
                carry_dve(dve, y32[:, :, T - 1], XF, row_fs, ALU.mult, ALU.add, 0.0)
                egru_dve(dve, m, 0)
                barrier(dve, "dve")
                if m < STEPS - 1:
                    egru_dve(dve, m, 1)
                    barrier(dve, "dve")
            final_dve(dve)
            dve.drain().then_inc(rows_ready, 1)

        @block.gpsimd
        def _(pool):
            def scatter(table, index, rows, done):
                for t in range(T):
                    nc.gpsimd.indirect_dma_start(table, bass.IndirectOffsetOnAxis(ap=index(t), axis=0),
                                                 rows(t), None).then_inc(done, 16)

            def gather(rows, table, index, done):
                for t in range(T):
                    nc.gpsimd.indirect_dma_start(rows(t), None, table,
                                                 bass.IndirectOffsetOnAxis(ap=index(t), axis=0)).then_inc(done, 16)

            def at_step(index):
                return lambda t: index[:, t:t + 1]

            pool.wait_ge(rank_ready, 1)
            scatter(tmp_d, at_step(rank_i[0]), lambda t: pay_d[:, t, :], put_tmp_d)
            pool.wait_ge(rank_ready, 2)
            pool.wait_ge(ld_pay, 16)
            scatter(tmp_s, at_step(rank_i[1]), lambda t: pay_s[:, t, :], put_tmp_s)
            pool.wait_ge(rank_ready, 3)
            pool.wait_ge(init_dram, 16 * 6)
            scatter(sort_d, at_step(rank_i[2]), lambda t: pay_d[:, t, :], put_sort_d)
            pool.wait_ge(put_sort_d, ALL)
            lists = ((sort_d, kid_d, edge_d, ld_kid_d), (sort_s.bitcast(I32), pay_si, edge_s, ld_kid_s))

            def load_list(tab, to, edge, done):
                pool.dma_start(to, tab[1:EP + 1, :].rearrange("(p t) c -> p t c", t=T)).then_inc(done, 16)
                pool.dma_start(edge[:, 0:2], tab[0:EP, :].rearrange("(p t) c -> p t c", t=T)[:, 0, 0:2])\
                    .then_inc(done, 16)
                pool.dma_start(edge[:, 2:4], tab[2:EP + 2, :].rearrange("(p t) c -> p t c", t=T)[:, T - 1, 0:2])\
                    .then_inc(done, 16)

            load_list(*lists[0])
            pool.wait_ge(rank_ready, 4)
            scatter(sort_s, at_step(rank_i[3]), lambda t: pay_s[:, t, :], put_sort_s)
            pool.wait_ge(put_sort_s, ALL)
            load_list(*lists[1])
            pool.wait_ge(ld_kid_d, 48)
            gather(lambda t: xg[:, 0, t, :], x, lambda t: kid_d[:, t, 0:1], got_x)
            gather(lambda t: xg[:, 1, t, :], x, lambda t: kid_d[:, t, 1:2], got_x)
            pool.wait_ge(flags_ready, 1)
            scatter(pos_tab, at_step(put_s), at_step(pos_val), put_pos)
            pool.wait_ge(put_pos, ALL)
            gather(at_step(pos_of), pos_tab[0:NP, :], lambda t: kid_s[:, t, 1:2], got_pos)
            pool.wait_ge(dense_done, 1)
            pool.wait_ge(rows_ready, 1)
            scatter(h1_tab, at_step(put_d), lambda t: rows64[:, t, :], put_h1)
            pool.wait_ge(put_h1, ALL)
            gather(lambda t: rows64[:, t, :], h1_tab[0:NP, :], lambda t: kid_d[:, t, 0:1], got_h1)
            pool.wait_ge(rows_ready, 2)
            scatter(x1_tab, at_step(put_d), lambda t: x1rows[:, t, :], put_x1)
            pool.wait_ge(put_x1, ALL)
            gather(lambda t: xg[:, 0, t, :], x1_tab[0:NP, :], lambda t: kid_s[:, t, 0:1], got_x1)
            gather(lambda t: xg[:, 1, t, :], x1_tab[0:NP, :], lambda t: kid_s[:, t, 1:2], got_x1)
            pool.wait_ge(got_pos, ALL)
            for m in range(STEPS - 1):
                pool.wait_ge(agg_stored, m + 1)
                gather(lambda t: ag[:, t * XF:(t + 1) * XF], agg_tab, at_step(pos_of), got_agg)
            pool.wait_ge(rows_ready, 3)
            pool.wait_ge(out_done, 1)
            scatter(out, at_step(put_s), lambda t: fin_rows[:, t * XF:(t + 1) * XF], put_out)
            pool.wait_ge(put_out, ALL)


def kernel(**inputs):
    import concourse.bacc as _bacc
    from concourse.bass_utils import run_bass_kernel_spmd as _run

    w = {n: np.asarray(a) for n, a in inputs.items()}
    f4 = np.float32

    def diag(block, n, rows=None, cols=None, places=None):
        r, c = block.shape
        m = np.zeros((rows or n * r, cols or n * c), f4)
        for i in range(n):
            ri, ci = (i, i) if places is None else places[i]
            m[ri * r:ri * r + r, ci * c:ci * c + c] = block
        return m

    eye, j64, j32 = np.eye(P, dtype=f4), np.full((64, 64), 1 / 64, f4), np.full((32, 32), 1 / 32, f4)
    j64, j32 = diag(j64, 2), diag(j32, 4)
    edge = np.arange(EP, dtype=f4).reshape(P, T)
    consts = np.concatenate([eye, j64, eye - j64, j32, eye - j32, np.triu(np.ones((P, P), f4), 1),
                             np.broadcast_to(np.arange(512, dtype=f4), (P, 512)), edge, edge + NP], 1)

    nw = w["L0_gnn_node_W"].T
    h0 = [diag(nw, 2, rows=P, places=[(2 * h, 0), (2 * h + 1, 1)]) for h in range(2)]
    xw, wh, at_s, at_d1, at_d2 = [], [], [], [], []
    for l in range(2):
        cw = w[f"L0_gnn_convW{l}"].reshape(HEADS, HF, HF)
        xw.append(diag(cw.transpose(2, 0, 1).reshape(HF, HEADS * HF), 2))
        wh += [diag(cw[h], 2) for h in range(HEADS)]
        for to, name, at in ((at_s, "src", (0,)), (at_d1, "dst", (4, 8)), (at_d2, "src", (8,))):
            for h in range(HEADS):
                m = np.zeros((HF, 12), f4)
                for c in at:
                    m[:, c + h] = w[f"L0_gnn_att_{name}{l}"][h]
                to.append(diag(m, 2))

    def gates(name):
        m = w[name].reshape(3, XF, XF)
        return [diag(m[g].T, 4) for g in range(3)]

    def cols(name, times, parts=1):
        return [np.tile(a, times)[:, None] for a in w[name].reshape(parts, -1)]

    weights = np.concatenate(
        h0 + xw + gates("L1_gnn_W_ih") + gates("L1_gnn_W_hh")
        + cols("L0_gnn_node_b", 2) + cols("L0_gnn_drone_b", 2) + cols("L0_gnn_out_b", 4)
        + cols("L1_gnn_b_ih", 4, 3) + cols("L1_gnn_b_hh", 4, 3)
        + [c for l in range(2) for n in ("convb", "ln_g", "ln_b") for c in cols(f"L0_gnn_{n}{l}", 2)], 1)
    ow = w["L0_gnn_out_W"]
    out_ab = [diag(ow, 2, rows=P, places=[(2 * h, 0), (2 * h + 1, 1)]) for h in range(2)]
    drone = np.zeros((P, P + 1), f4)
    drone[0:16, 0:P] = np.concatenate([w["L0_gnn_drone_W"].T] * 2, 1)
    drone[0:16, P] = w["L0_gnn_drone_feat"][0]
    prep = np.concatenate(wh + at_s + at_d1 + at_d2 + out_ab + [drone], 1)
    ub = w["L1_gnn_W_bond"].reshape(BONDF, XF, XF).transpose(2, 1, 0).reshape(XF, XF * BONDF)
    vbm = w["L1_gnn_b_bond"].reshape(XF, XF).T
    bondw = np.concatenate([diag(ub, 4), diag(vbm, 4)], 1)

    def padded(a, n, value):
        return np.concatenate([a, np.full((n - len(a),) + a.shape[1:], value, a.dtype)])

    arrays = {
        "x_in": padded(w["x"], NP, 0), "src_in": padded(w["src"], EP, N_NODES),
        "dst_in": padded(w["dst"], EP, N_NODES), "attr_in": padded(w["edge_attr_16"], EP, 0),
        "consts_in": consts, "weights_in": weights, "prep_in": prep, "bondw_in": bondw,
    }
    arrays = {n: np.ascontiguousarray(a) for n, a in arrays.items()}
    nc = _bacc.Bacc("TRN2", target_bir_lowering=False, num_devices=1)
    args = [nc.dram_tensor(n, a.shape, mybir.dt.from_np(a.dtype), kind="ExternalInput").ap()
            for n, a in arrays.items()]
    out = nc.dram_tensor("out_0", (NROWS, XF), F32, kind="ExternalOutput").ap()
    build(nc, *args, out)
    r = _run(nc, [arrays], core_ids=[0])
    return r.results[0]["out_0"][0:N_NODES]
```

```python
import numpy as np
import concourse.bass as bass
from concourse import mybir
from contextlib import ExitStack

F32 = mybir.dt.float32
I32 = mybir.dt.int32
ALU = mybir.AluOpType
ACT = mybir.ActivationFunctionType
AX = mybir.AxisListType

P = 128
N_NODES, N_EDGES = 100000, 25000
XF, HF, HEADS, BONDF, STEPS = 32, 64, 4, 16, 4
T = -(-N_EDGES // P)
EP = P * T
DB = -(-N_NODES // (16 * P))
NP = DB * 16 * P
NROWS = NP + EP
BT = 28
EB = T // BT
QB = BT // 4
PAY = 2 + BONDF
BINS_LO, BINS_HI = 256, -(-(N_NODES + 1) // 256)
SENTINEL = 1 << 20
EPS = 1e-5
BIG = 1e30
PARTS = [(0, 512), (512, 384)]
UNITS = [(0, 2), (2, 2), (4, 2), (6, 1)]
ALL = 16 * T

K_ID, K_C64, K_C32, K_LT = (i * P for i in range(4))
K_J2, K_J4 = 4 * P, 4 * P + 2
K_IOTA = 4 * P + 6
K_EDGE = K_IOTA + 512
K_JUNK = K_EDGE + T
K_END = K_JUNK + T
W_H0A, W_H0B = 0, P
W_XW = [2 * P, 2 * P + 512]
W_IH = W_XW[1] + 512
W_HH = W_IH + 3 * P
W_COL = W_HH + 3 * P
(C_NODEB, C_DRONEB, C_OUTB, C_BIHR, C_BIHZ, C_BIHN, C_BHHR, C_BHHZ, C_BHHN) = range(9)
C_CONVB, C_G, C_B = [9, 12], [10, 13], [11, 14]
N_COL = 15
W_END = W_COL + N_COL
V_WH = [0, 4 * P]
V_AS, V_AD1, V_AD2 = [8 * P, 8 * P + 96], [8 * P + 192, 8 * P + 288], [8 * P + 384, 8 * P + 480]
V_OA = 8 * P + 576
V_OB = V_OA + P
V_DW = V_OB + P
V_DF = V_DW + P
V_END = V_DF + 1
D_WC = [0, P]
D_OA, D_OB = 2 * P, 3 * P
D_RS, D_RD = [4 * P, 4 * P + 24], [4 * P + 48, 4 * P + 72]
D_C0 = 4 * P + 96
D_BC = [D_C0 + 1, D_C0 + 2]
D_OBC, D_EPS, D_BR, D_BZ, D_NBZ = D_C0 + 3, D_C0 + 4, D_C0 + 5, D_C0 + 6, D_C0 + 7
D_END = D_C0 + 8


def build(nc, x, src, dst, attr, consts, weights, prep, bondw, sel, out):
    ctx = ExitStack()
    with ctx:
        def sem(name):
            return ctx.enter_context(nc.semaphore(name))

        def dram(name, shape, dt):
            return nc.dram_tensor(name, shape, dt, kind="Internal").ap()

        tmp_d = dram("tmp_d", (EP, 2), I32)
        sort_d = dram("sort_d", (EP + 2, 2), I32)
        tmp_s = dram("tmp_s", (EP, PAY), F32)
        sort_s = dram("sort_s", (EP + 2, PAY), F32)
        h1_tab = dram("h1_tab", (NROWS, HF), F32)
        x1_tab = dram("x1_tab", (NROWS, XF), F32)
        pos_tab = dram("pos_tab", (NROWS, 1), I32)
        agg_tab = dram("agg_tab", (EP + P, XF), F32)
        ht_dram = [dram(f"ht_dram{l}", (EB, P, QB * 512), F32) for l in range(2)]
        h1d_dram = dram("h1d_dram", (EB, P, QB * 256), F32)
        xs_dram = dram("xs_dram", (P, T * XF), F32)
        xt_dram = dram("xt_dram", (EB, P, QB * 256), F32)

        def sb(name, words):
            return ctx.enter_context(nc.sbuf_tensor(name, [P, words], F32))

        kc = sb("kc", K_END)
        wt = sb("wt", W_END)
        dv = sb("dv", D_END)
        r1 = sb("r1", T * HF)
        r2 = sb("r2", T * HF)
        r3 = sb("r3", 2 * QB * 512)
        stage = sb("stage", 2 * BT * HF)
        l12 = sb("l12", 12 * T)
        alpha = sb("alpha", 2 * T * HEADS)
        nst = sb("nst", PAY * T)
        small = sb("small", 23 * T + 5 * P + 300)
        ps = ctx.enter_context(nc.psum_tensor("ps", [P, 8, 512], F32))

        def k(c, n=P):
            return kc[:, c:c + n]

        ident = k(K_ID)

        def col(c):
            return wt[:, W_COL + c:W_COL + c + 1]

        def dcol(c):
            return dv[:, c:c + 1]

        at = [0]

        def carve(n):
            at[0] += n
            return small[:, at[0] - n:at[0]]

        ns_f, nl_f, pm, sm, last, ns_neg, nl_neg, pm_neg, sm_neg = (carve(T) for _ in range(9))
        ns_fs, pm_s = carve(T), carve(T)
        put_d, put_s, pos_val, pos_of = (carve(T).bitcast(I32) for _ in range(4))
        kid_d = carve(2 * T).bitcast(I32).rearrange("p (t c) -> p t c", c=2)
        kid_s = carve(2 * T).bitcast(I32).rearrange("p (t c) -> p t c", c=2)
        rank_i = [carve(T).bitcast(I32) for _ in range(4)]
        row_f, row_r, row_fn, row_rn, row_fs = (carve(P) for _ in range(5))
        edge_d, edge_s = carve(4).bitcast(I32), carve(4).bitcast(I32)
        end_c, carry, lanes = carve(64), carve(64), carve(130)

        phase_ended, phase_begins = sem("phase_ended"), sem("phase_begins")
        ends = {"sp": 0, "pe": 0, "act": 0, "dve": 0}

        def barrier(eng, who, clear=()):
            ends[who] += 1
            eng.drain().then_inc(phase_ended, 1)
            if who == "sp":
                eng.wait_ge(phase_ended, 4 * ends[who])
                for s in clear:
                    eng.sem_clear(s)
                eng.sem_inc(phase_begins, 1)
            else:
                eng.wait_ge(phase_begins, ends[who])

        def phase_sems(phase, names):
            return [nc.alloc_semaphore(name=f"{phase}_{n}") for n in names.split()]

        def phase_over(sems):
            for s in sems:
                nc.release_semaphore(s)

        def loop(eng, n, body):
            with eng.Fori(0, n // 2) as i:
                body(2 * i, i, 0)
                body(2 * i + 1, i, 1)
            body(n - 1, n // 2, 0)

        ld = sem("ld")
        ld_keys, ld_pay, ld_tmp_d, ld_tmp_s = sem("ld_keys"), sem("ld_pay"), sem("ld_tmp_d"), sem("ld_tmp_s")
        init_dram = sem("init_dram")
        rank_ready = sem("rank_ready")
        put_tmp_d, put_tmp_s, put_sort_d, put_sort_s = (sem(f"put_{n}") for n in
                                                         ("tmp_d", "tmp_s", "sort_d", "sort_s"))
        ld_kid_d, ld_kid_s, put_pos, got_pos = (sem(n) for n in ("ld_kid_d", "ld_kid_s", "put_pos", "got_pos"))
        got_even, got_odd = sem("got_even"), sem("got_odd")
        x_in, h1_in, agg_in = sem("x_in"), sem("h1_in"), sem("agg_in")
        flags_ready = sem("flags_ready")
        dense_done = sem("dense_done")
        rows_ready = sem("rows_ready")
        put_h1, put_x1, got_x1 = (sem(n) for n in ("put_h1", "put_x1", "got_x1"))
        out_done = sem("out_done")
        agg_stored, put_out = sem("agg_stored"), sem("put_out")
        prep_pe, prep_dve = sem("prep_pe"), sem("prep_dve")
        sentinel_ready = sem("sentinel_ready")
        fl, fl_pe = sem("fl"), sem("fl_pe")
        tl_d, tl_p = sem("tl_d"), sem("tl_p")
        sx, sx_act = sem("sx"), sem("sx_act")
        sc = sem("sc")

        pw = r1[:, 0:V_END]
        dsel = l12[0:16, 0:1536]
        fill = alpha[:, 0:128]
        pos_fill = alpha[:, 128:128 + NP // P].bitcast(I32)

        def prep_sp(sp):
            sp.dma_start(kc[:], consts).then_inc(ld, 16)
            sp.dma_start(wt[:], weights).then_inc(ld, 16)
            sp.dma_start(pw, prep).then_inc(ld, 16)
            sp.dma_start(dsel, sel).then_inc(ld, 16)
            sp.dma_start(src_t, src.rearrange("(p t) -> p t", t=T)).then_inc(ld_keys, 16)
            sp.dma_start(dst_t, dst.rearrange("(p t) -> p t", t=T)).then_inc(ld_keys, 16)
            sp.dma_start(pay_s[:, :, 2:PAY], attr.rearrange("(p t) c -> p t c", t=T)).then_inc(ld_pay, 16)
            sp.wait_ge(sentinel_ready, 3)
            for r in (0, EP + 1):
                sp.dma_start(sort_d[r:r + 1, :], fill[0:1, 0:2].bitcast(I32)).then_inc(init_dram, 16)
                sp.dma_start(sort_s[r:r + 1, :], fill[0:1, 0:PAY]).then_inc(init_dram, 16)
            sp.dma_start(pos_tab[0:NP, :].rearrange("(p n) c -> p (n c)", p=P), pos_fill).then_inc(init_dram, 16)
            sp.dma_start(agg_tab[EP:EP + P, :], fill[:, 64:64 + XF]).then_inc(init_dram, 16)
            sp.wait_ge(init_dram, 16 * 6)

        def prep_dve_(dve):
            v = nc.vector
            v.memset(fill[:, 0:64].bitcast(I32), SENTINEL).then_inc(sentinel_ready, 1)
            v.memset(fill[:, 64:128], 0.0).then_inc(sentinel_ready, 1)
            v.memset(pos_fill, EP).then_inc(sentinel_ready, 1)
            v.memset(dcol(D_EPS), EPS)
            dve.wait_ge(ld, 64)
            dve.wait_ge(prep_pe, 1)
            v.tensor_tensor(dcol(D_C0), ps[:, 0, 0:1], col(C_NODEB), ALU.add).then_inc(prep_dve, 1)
            dve.wait_ge(prep_dve, 1)
            v.tensor_tensor(dcol(D_C0), dcol(D_C0), col(C_DRONEB), ALU.add)
            for l in range(2):
                v.tensor_single_scalar(dv[:, D_WC[l]:D_WC[l] + P], ps[:, 1 + l, 0:P], 1.0 / HEADS, ALU.mult)
                v.tensor_copy(dv[:, D_RS[l]:D_RS[l] + 24], ps[:, 1 + l, 128:152])
                v.tensor_copy(dv[:, D_RD[l]:D_RD[l] + 24], ps[:, 1 + l, 152:176])
                v.tensor_copy(dcol(D_BC[l]), ps[:, 1 + l, 176:177])
            v.tensor_copy(dv[:, D_OA:D_OA + 2 * P], ps[:, 3, 0:2 * P])
            v.tensor_copy(dcol(D_OBC), ps[:, 3, 256:257])
            v.tensor_tensor(dcol(D_BR), col(C_BIHR), col(C_BHHR), ALU.add)
            v.tensor_tensor(dcol(D_BZ), col(C_BIHZ), col(C_BHHZ), ALU.add).then_inc(prep_dve, 1)
            dve.wait_ge(prep_dve, 2)
            v.tensor_single_scalar(dcol(D_NBZ), dcol(D_BZ), -1.0, ALU.mult)

        def prep_pe_(pe):
            mm = nc.tensor.matmul
            pe.wait_ge(ld, 64)
            mm(ps[:, 0, 0:1], pw[:, V_DW:V_DW + P], pw[:, V_DF:V_DF + 1], start=True, stop=True)
            for l in range(2):
                wh = [pw[:, V_WH[l] + h * P:V_WH[l] + (h + 1) * P] for h in range(HEADS)]
                for h in range(HEADS):
                    mm(ps[:, 1 + l, 0:P], wh[h], k(K_C64), start=h == 0, stop=h == HEADS - 1)
                for h in range(HEADS):
                    mm(ps[:, 1 + l, 128:152], wh[h], pw[:, V_AS[l] + 24 * h:V_AS[l] + 24 * h + 24],
                       start=h == 0, stop=h == HEADS - 1)
                for h in range(HEADS):
                    mm(ps[:, 1 + l, 152:176], wh[h], pw[:, V_AD1[l] + 24 * h:V_AD1[l] + 24 * h + 24],
                       start=h == 0, stop=False)
                    mm(ps[:, 1 + l, 152:176], wh[h], pw[:, V_AD2[l] + 24 * h:V_AD2[l] + 24 * h + 24],
                       start=False, stop=h == HEADS - 1)
                mm(ps[:, 1 + l, 176:177], k(K_C64), col(C_CONVB[l]), start=True, stop=True)
            mm(ps[:, 3, 0:P], pw[:, V_OA:V_OA + P], k(K_C32), start=True, stop=True)
            mm(ps[:, 3, P:2 * P], pw[:, V_OB:V_OB + P], k(K_C32), start=True, stop=True)
            mm(ps[:, 3, 256:257], k(K_C32), col(C_OUTB), start=True, stop=True).then_inc(prep_pe, 1)

        src_t, dst_t = r3[:, 0:T].bitcast(I32), r3[:, T:2 * T].bitcast(I32)
        pay_d = r3[:, 2 * T:4 * T].bitcast(I32).rearrange("p (t c) -> p t c", c=2)
        pay_s = nst[:].rearrange("p (t c) -> p t c", c=PAY)
        pay_si = nst[:].bitcast(I32).rearrange("p (t c) -> p t c", c=PAY)
        digit_i, digit, rank = (r3[:, (4 + i) * T:(5 + i) * T] for i in range(3))
        digit_i = digit_i.bitcast(I32)
        hist, start, junk, ones_b = (r3[:, 8 * T + 512 * i:8 * T + 512 * (i + 1)] for i in range(4))
        s_hist, s_pref, s_pref_used, s_dv = sem("s_hist"), sem("s_pref"), sem("s_pref_used"), sem("s_dv")
        BINS = [BINS_LO, BINS_LO, BINS_HI, BINS_HI]
        COUNT_PAIRS, RANK_PAIRS, SLOTS = 2, 4, 14
        CE, RE = T // COUNT_PAIRS, T // RANK_PAIRS
        n_dv = [0]

        def chain_dv(dve, ins):
            ins.then_inc(s_dv, 1)
            n_dv[0] += 1
            dve.wait_ge(s_dv, n_dv[0])

        def sort_start(dve):
            v = nc.vector
            v.memset(ones_b[:], 1.0)
            dve.wait_ge(ld_keys, 32)
            v.tensor_copy(pay_d[:, :, 0], src_t)
            v.tensor_copy(pay_d[:, :, 1], dst_t)
            v.tensor_copy(pay_si[:, :, 0], src_t)
            v.tensor_copy(pay_si[:, :, 1], dst_t)

        def sort_digits(dve, i):
            v, bins = nc.vector, BINS[i]
            key = (dst_t, src_t, pay_d[:, :, 1], pay_si[:, :, 0])[i]
            if i == 2:
                dve.wait_ge(ld_tmp_d, 16)
            if i == 3:
                dve.wait_ge(ld_tmp_s, 16)
            if i < 2:
                chain_dv(dve, v.tensor_single_scalar(digit_i, key, 255, ALU.bitwise_and))
            else:
                chain_dv(dve, v.tensor_single_scalar(digit_i, key, 8, ALU.logical_shift_right))
            v.tensor_copy(digit, digit_i)
            chain_dv(dve, v.memset(hist[:, 0:bins], 0.0))

        def sort_count(dve, i, base, pair, slot):
            v, bins = nc.vector, BINS[i]
            for u in range(CE // SLOTS):
                e = pair * CE + (slot * (CE // SLOTS) + u - 6 * i * CE)
                v.scalar_tensor_tensor(out=hist[:, 0:bins], in0=k(K_IOTA, bins), scalar=digit[:, bass.ds(e, 1)],
                                       in1=hist[:, 0:bins], op0=ALU.is_equal, op1=ALU.add).then_inc(s_dv, 1)
                dve.wait_ge(s_dv, e + (base + 1))

        def sort_starts(dve, i):
            v, bins = nc.vector, BINS[i]
            v.tensor_copy(start[:, 0:bins], hist[:, 0:bins]).then_inc(s_hist, 1)
            dve.wait_ge(s_pref, i + 1)
            chain_dv(dve, v.tensor_tensor_scan(junk[:, 0:bins], ones_b[:, 0:bins], ps[:, 5, 0:bins], 0.0,
                                               ALU.mult, ALU.add))
            chain_dv(dve, v.tensor_tensor(junk[:, 0:bins], junk[:, 0:bins], ps[:, 5, 0:bins], ALU.subtract))
            chain_dv(dve, v.tensor_tensor(start[:, 0:bins], junk[:, 0:bins], ps[:, 4, 0:bins], ALU.add))
            dve.sem_inc(s_pref_used, 1)

        def sort_rank(dve, i, base, pair, slot):
            v, bins = nc.vector, BINS[i]
            for u in range(*((0, 4) if slot % 2 == 0 else (4, 7))):
                e = pair * RE + (slot // 2 * 7 + u - (6 * i + COUNT_PAIRS) * RE)
                d = digit[:, bass.ds(e, 1)]
                v.scalar_tensor_tensor(out=junk[:, 0:bins], in0=k(K_IOTA, bins), scalar=d,
                                       in1=start[:, 0:bins], op0=ALU.is_equal, op1=ALU.mult,
                                       accum_out=rank[:, bass.ds(e, 1)]).then_inc(s_dv, 1)
                dve.wait_ge(s_dv, e * 2 + (base + 1))
                v.scalar_tensor_tensor(out=start[:, 0:bins], in0=k(K_IOTA, bins), scalar=d,
                                       in1=start[:, 0:bins], op0=ALU.is_equal,
                                       op1=ALU.add).then_inc(s_dv, 1)
                dve.wait_ge(s_dv, e * 2 + (base + 2))

        def sort_dve(dve):
            sort_start(dve)
            for i in range(4):
                b0, b1, b2 = 12 * i, 12 * i + 2 * COUNT_PAIRS, 12 * i + 12
                sort_digits(dve, i)
                base = n_dv[0]
                dense_dve(dve, b0, b1, lambda pair, slot: sort_count(dve, i, base, pair, slot))
                n_dv[0] += T
                sort_starts(dve, i)
                base = n_dv[0]
                dense_dve(dve, b1, b2, lambda pair, slot: sort_rank(dve, i, base, pair, slot))
                n_dv[0] += 2 * T
                nc.vector.tensor_single_scalar(rank_i[i], rank, float(i // 2), ALU.add)\
                    .then_inc(rank_ready, 1)
            dense_dve(dve, 48, DB)

        def sort_pe(pe):
            mm = nc.tensor.matmul
            for i, bins in enumerate(BINS):
                dense_pe(pe, 12 * i, 12 * i + 2 * COUNT_PAIRS)
                pe.wait_ge(s_hist, i + 1)
                mm(ps[:, 4, 0:bins], k(K_LT), start[:, 0:bins], start=True, stop=True)
                mm(ps[:, 5, 0:bins], ones_b[:, 0:P], start[:, 0:bins], start=True, stop=True).then_inc(s_pref, 1)
                pe.wait_ge(s_pref_used, i + 1)
                dense_pe(pe, 12 * i + 2 * COUNT_PAIRS, 12 * i + 12)
            dense_pe(pe, 48, DB)

        dense_sems = phase_sems("dn", "x0 x1 tr xt hm h z zc sq v sd rs rt re r tn rl hn t1 t1e free xtr xe st")
        dn = dense_sems[0:2]
        (dn_tr, dn_xt, dn_hm, dn_h, dn_z, dn_zc, dn_sq, dn_v, dn_sd, dn_rs, dn_rt, dn_re, dn_r, dn_tn, dn_rl,
         dn_hn, dn_t1, dn_t1e, dn_free, dn_xtr, dn_xe, dn_st) = dense_sems[2:]
        phase_over(dense_sems)
        off = [0]

        def lay(region, n):
            off[0] += n
            return region[:, off[0] - n:off[0]]

        xr, xt_b = [lay(r2, 512) for _ in range(2)], [lay(r2, 512) for _ in range(2)]
        hb, h1b, zc, sq, tn = ([lay(r2, 1024) for _ in range(2)] for _ in range(5))
        h1o = [stage[:, s * 1024:(s + 1) * 1024] for s in range(2)]
        x1o = [stage[:, 2048 + s * 512:2560 + s * 512] for s in range(2)]
        rst = [stage[:, 3072 + s * 16:3088 + s * 16] for s in range(2)]
        rtt = [stage[0:16, 3104 + s * P:3104 + (s + 1) * P] for s in range(2)]
        x_blk = x.rearrange("(b p n) f -> b p (n f)", p=P, n=16)
        h1_blk = h1_tab[0:NP, :].rearrange("(b p n) f -> b p (n f)", p=P, n=16)
        x1_blk = x1_tab[0:NP, :].rearrange("(b p n) f -> b p (n f)", p=P, n=16)
        out_blk = out[0:NP, :].rearrange("(b p n) f -> b p (n f)", p=P, n=16)

        def blk(ap, b):
            return ap[bass.ds(b, 1)].rearrange("o p f -> (o p) f")

        def pairs(eng, first, n, body):
            if n - first > 1:
                with eng.Fori(first // 2, n // 2) as i:
                    body(2 * i, i, 2)
            if n % 2:
                body(n - 1, n // 2, 1)

        def two(s, lo):
            return ps[:, 4 * s + 2 * lo:4 * s + 2 * lo + 2, :]

        def wide(ap):
            return ap.rearrange("p (k c) -> p k c", k=2)

        def dense_sp(sp, first, n):
            def load(b, s):
                sp.dma_start(xr[s], blk(x_blk, b)).then_inc(dn[s], 16)

            def store(b, s):
                sp.wait_ge(dn_t1e, b + s + 3)
                sp.dma_start(blk(h1_blk, b + s), h1o[s]).then_inc(dn_st, 16)
                sp.wait_ge(dn_xe, b + s + 3)
                sp.dma_start(blk(x1_blk, b + s), x1o[s]).then_inc(dn_st, 16)
                sp.wait_ge(dn_st, 32 * b + 32 * s + 32)
                sp.sem_inc(dn_free, 1)

            if first == 0:
                sp.sem_inc(dn_free, 2)
            load(first, 0)
            load(first + 1, 1)
            with sp.Fori(first // 2, n // 2 - 1) as i:
                sp.wait_ge(dn_tr, 2 * i + 2)
                load(2 * i + 2, 0)
                load(2 * i + 3, 1)
                store(2 * i, 0)
                store(2 * i, 1)
            if n % 2:
                sp.wait_ge(dn_tr, n - 1)
                load(n - 1, 0)
            b = n // 2 * 2 - 2
            store(b, 0)
            store(b, 1)
            if n % 2:
                store(n - 1, 0)

        def dense_pe(pe, first, n):
            mm, tr = nc.tensor.matmul, nc.tensor.transpose

            def body(b, i, ns):
                def stats(kk, units):
                    for s in range(ns):
                        pe.wait_ge(dn_sq, 6 * i + ns * kk + s + 1)
                        for j in range(units):
                            c, w = (j % 4 * P + j // 4 * 512, 2) if units == 8 else (j * P, 4)
                            at_ = 4 * (j % 4) + 2 * (j // 4) if units == 8 else 4 * j
                            m = mm(ps[:, 4 * s + 2, at_:at_ + w], sq[s][:, c:c + P],
                                   k(K_J2 if w == 2 else K_J4, w), start=True, stop=True)
                        m.then_inc(dn_v, 1)
                    for s in range(ns):
                        pe.wait_ge(dn_rs, 6 * i + ns * kk + s + 1)
                        tr(ps[0:16, 4 * s + 2, P:2 * P], rst[s], ident).then_inc(dn_rt, 1)
                    for s in range(ns):
                        pe.wait_ge(dn_re, 6 * i + ns * kk + s + 1)
                        for j in range(units):
                            if units == 8:
                                w0 = (4 * (j % 4) + 2 * (j // 4)) * 64
                                o = ps[:, 4 * s + 2 + j // 4, j % 4 * P:(j % 4 + 1) * P]
                            else:
                                w0 = 1024 + j * P
                                o = ps[:, 4 * s + 3, j * P:(j + 1) * P]
                            m = mm(o, dsel[:, w0:w0 + P], rtt[s], start=True, stop=True)
                        m.then_inc(dn_r, 1)

                for s in range(ns):
                    pe.wait_ge(dn[s], 16 * i + 16)
                    pe.wait_ge(dn_xe, b + s + 1)
                    for j in range(4):
                        t = tr(ps[:, 4 * s, j * P:(j + 1) * P], xr[s][:, j * P:(j + 1) * P], ident)
                    t.then_inc(dn_tr, 1)
                for s in range(ns):
                    pe.wait_ge(dn_xt, b + s + 1)
                    for h in range(2):
                        m = mm(ps[:, 4 * s + 2 + h, :], wt[:, (W_H0A, W_H0B)[h]:(W_H0A, W_H0B)[h] + P],
                               xt_b[s], start=True, stop=True)
                    m.then_inc(dn_hm, 1)
                for l in range(2):
                    for s in range(ns):
                        if l == 0:
                            pe.wait_ge(dn_h, b + s + 1)
                        else:
                            pe.wait_ge(dn_hn, 4 * i + s + 1)
                        for h in range(2):
                            m = mm(ps[:, 4 * s + h, :], dv[:, D_WC[l]:D_WC[l] + P],
                                   (hb, h1b)[l][s][:, h * 512:(h + 1) * 512], start=True, stop=True)
                        m.then_inc(dn_z, 1)
                    if l == 1:
                        for s in range(ns):
                            for j in range(8):
                                t = tr(ps[:, 4 * s + 2 + j // 4, j % 4 * P:(j % 4 + 1) * P],
                                       h1b[s][:, j * P:(j + 1) * P], ident)
                            t.then_inc(dn_t1, 1)
                        for s in range(ns):
                            pe.wait_ge(dn_t1e, b + s + 3)
                    stats(l, 8)
                for s in range(ns):
                    pe.wait_ge(dn_hn, 4 * i + ns + s + 1)
                    mm(ps[:, 4 * s, :], k(K_C32), xt_b[s], start=True, stop=False)
                    mm(ps[:, 4 * s, :], dv[:, D_OA:D_OA + P], hb[s][:, 0:512], start=False, stop=False)
                    mm(ps[:, 4 * s, :], dv[:, D_OB:D_OB + P], hb[s][:, 512:1024], start=False,
                       stop=True).then_inc(dn_z, 1)
                stats(2, 4)
                for s in range(ns):
                    pe.wait_ge(dn_tn, 6 * i + 2 * ns + s + 1)
                    for j in range(4):
                        t = tr(ps[:, 4 * s + 1, j * P:(j + 1) * P], tn[s][:, j * P:(j + 1) * P], ident)
                    t.then_inc(dn_xtr, 1)

            pairs(pe, first, n, body)

        def dense_act(act, first, n):
            a = nc.scalar.activation

            def body(b, i, ns):
                def stats(kk):
                    for s in range(ns):
                        act.wait_ge(dn_v, 6 * i + ns * kk + s + 1)
                        a(rst[s], ps[:, 4 * s + 2, 0:16], ACT.Sqrt, bias=dcol(D_EPS)).then_inc(dn_sd, 1)
                    for s in range(ns):
                        act.wait_ge(dn_rt, 6 * i + ns * kk + s + 1)
                        a(rtt[s], ps[0:16, 4 * s + 2, P:2 * P], ACT.Identity).then_inc(dn_re, 1)

                for s in range(ns):
                    act.wait_ge(dn_tr, b + s + 1)
                    a(xt_b[s], ps[:, 4 * s, :], ACT.Identity).then_inc(dn_xt, 1)
                for s in range(ns):
                    act.wait_ge(dn_hm, b + s + 1)
                    a(wide(hb[s]), two(s, 1), ACT.Identity, bias=dcol(D_C0)).then_inc(dn_h, 1)
                for l in range(2):
                    for s in range(ns):
                        act.wait_ge(dn_z, 6 * i + ns * l + s + 1)
                        a(wide(sq[s]), two(s, 0), ACT.Square, bias=dcol(D_BC[l])).then_inc(dn_sq, 1)
                        a(wide(zc[s]), two(s, 0), ACT.Identity, bias=dcol(D_BC[l])).then_inc(dn_zc, 1)
                    stats(l)
                    for s in range(ns):
                        act.wait_ge(dn_tn, 6 * i + ns * l + s + 1)
                        a(tn[s], tn[s], ACT.Relu, bias=col(C_B[l]), scale=col(C_G[l])).then_inc(dn_rl, 1)
                for s in range(ns):
                    act.wait_ge(dn_z, 6 * i + ns * 2 + s + 1)
                    a(sq[s][:, 0:512], ps[:, 4 * s, :], ACT.Square, bias=dcol(D_OBC)).then_inc(dn_sq, 1)
                    a(zc[s][:, 0:512], ps[:, 4 * s, :], ACT.Identity, bias=dcol(D_OBC)).then_inc(dn_zc, 1)
                stats(2)

            pairs(act, first, n, body)

        def dense_dve(dve, first, n, between=None):
            v = nc.vector

            def body(b, i, ns):
                slot = [0]

                def meanwhile(slots):
                    for _ in range(slots if between and ns == 2 else 0):
                        between(i, slot[0])
                        slot[0] += 1

                def norm(kk, slots):
                    meanwhile(slots[0])
                    for s in range(ns):
                        dve.wait_ge(dn_sd, 6 * i + ns * kk + s + 1)
                        v.reciprocal(rst[s], rst[s]).then_inc(dn_rs, 1)
                    meanwhile(slots[1])
                    for s in range(ns):
                        dve.wait_ge(dn_r, 6 * i + ns * kk + s + 1)
                        dve.wait_ge(dn_zc, 6 * i + ns * kk + s + 1)
                        if kk < 2:
                            v.tensor_tensor(wide(tn[s]), wide(zc[s]), two(s, 1), ALU.mult).then_inc(dn_tn, 1)
                        else:
                            v.tensor_tensor(tn[s][:, 0:512], zc[s][:, 0:512], ps[:, 4 * s + 3, :],
                                            ALU.mult).then_inc(dn_tn, 1)
                    meanwhile(slots[2])

                for l in range(2):
                    norm(l, ((4, 2, 1), (1, 2, 1))[l])
                    for s in range(ns):
                        dve.wait_ge(dn_rl, 4 * i + ns * l + s + 1)
                        v.tensor_tensor((h1b, hb)[l][s], (hb, h1b)[l][s], tn[s], ALU.add).then_inc(dn_hn, 1)
                    if l == 0:
                        for s in range(ns):
                            dve.wait_ge(dn_free, b + s + 1)
                            dve.wait_ge(dn_t1, b + s + 1)
                            v.tensor_copy(h1o[s].rearrange("p (j h c) -> p h j c", j=4, h=2),
                                          two(s, 1).rearrange("p h (j c) -> p h j c", j=4)).then_inc(dn_t1e, 1)
                norm(2, (1, 1, 1))
                for s in range(ns):
                    dve.wait_ge(dn_xtr, b + s + 1)
                    v.tensor_copy(x1o[s], ps[:, 4 * s + 1, :]).then_inc(dn_xe, 1)

            if first == 0:
                dve.sem_inc(dn_t1e, 2)
                dve.sem_inc(dn_xe, 2)
            pairs(dve, first, n, body)

        kx = r2[:, 7000:7000 + T + 2]
        kt = r2[:, 7256:7256 + T]
        border = [r2[:, 7512 + P * i:7640 + P * i] for i in range(3)]
        nfl = [0]

        def flags_dve(dve, order):
            v = nc.vector

            def chain(ins):
                ins.then_inc(fl, 1)
                nfl[0] += 1
                dve.wait_ge(fl, nfl[0])

            dve.wait_ge((ld_kid_d, ld_kid_s)[order], 48)
            if order == 1:
                chain(v.tensor_copy(kid_s, pay_si[:, :, 0:2]))
            key = (kid_d[:, :, 1], kid_s[:, :, 0])[order]
            edge = (edge_d, edge_s)[order]
            nsf, pmx = ((ns_f, pm), (ns_fs, pm_s))[order]
            put = (put_d, put_s)[order]
            v.tensor_copy(kx[:, 0:1], edge[:, 1 - order:2 - order])
            v.tensor_copy(kx[:, T + 1:T + 2], edge[:, 3 - order:4 - order])
            chain(v.tensor_copy(kx[:, 1:T + 1], key))
            chain(v.tensor_tensor(nsf, kx[:, 1:T + 1], kx[:, 0:T], ALU.is_equal))
            chain(v.tensor_tensor_scan(pmx, nsf, nsf, 1.0, ALU.mult, ALU.min))
            chain(v.memset(nsf[:, 0:1], 0.0))
            chain(v.tensor_tensor(kt, kx[:, 1:T + 1], kx[:, 2:T + 2], ALU.is_equal))
            if order == 0:
                chain(v.tensor_tensor_scan(sm[:, ::-1], kt[:, ::-1], kt[:, ::-1], 1.0, ALU.mult, ALU.min))
                chain(v.tensor_copy(nl_f, kt))
                chain(v.memset(nl_f[:, T - 1:T], 0.0))
            chain(v.tensor_scalar(kt, kt, -1.0, 1.0, ALU.mult, ALU.add))
            if order == 0:
                chain(v.tensor_copy(last, kt))
                for a, b in ((ns_neg, ns_f), (nl_neg, nl_f), (pm_neg, pm), (sm_neg, sm)):
                    chain(v.tensor_scalar(a, b, 1.0, BIG, ALU.subtract, ALU.mult))
            chain(v.tensor_tensor(kx[:, 1:T + 1], kx[:, 1:T + 1], k(K_JUNK, T), ALU.subtract))
            chain(v.tensor_tensor(kx[:, 1:T + 1], kx[:, 1:T + 1], kt, ALU.mult))
            chain(v.tensor_tensor(put, kx[:, 1:T + 1], k(K_JUNK, T), ALU.add))
            if order == 0:
                chain(v.tensor_single_scalar(border[0], ident, pm[:, T - 1:T], ALU.mult))
                chain(v.tensor_single_scalar(border[1], ident, sm[:, 0:1], ALU.mult))
            else:
                chain(v.tensor_copy(pos_val, k(K_EDGE, T)))
                chain(v.tensor_single_scalar(border[2], ident, pm_s[:, T - 1:T], ALU.mult))
            v.memset(lanes[:], 1.0).then_inc(flags_ready, 1)
            dve.wait_ge(fl_pe, order + 1)
            for i, row in ((0, row_f), (1, row_r)) if order == 0 else ((2, row_fs),):
                chain(v.tensor_copy(row[0:64, :], ps[0:64, 7, i * P:(i + 1) * P]))
            if order == 0:
                chain(v.tensor_scalar(row_fn[0:64, :], row_f[0:64, :], 1.0, BIG, ALU.subtract, ALU.mult))
                chain(v.tensor_scalar(row_rn[0:64, :], row_r[0:64, :], 1.0, BIG, ALU.subtract, ALU.mult))

        def flags_pe(pe, order):
            pe.wait_ge(flags_ready, order + 1)
            for i in ((0, 1), (2,))[order]:
                m = nc.tensor.matmul(ps[0:64, 7, i * P:(i + 1) * P], lanes[:, 0:64], border[i],
                                     start=True, stop=True)
            m.then_inc(fl_pe, 1)

        ntl = {"d": 0, "p": 0, "pe_d": 0, "pe_p": 0}

        def carry_dve(dve, ends, kk, row, op0, op1, first, reverse=False):
            v = nc.vector

            def chain(ins):
                ins.then_inc(tl_d, 1)
                ntl["d"] += 1

            chain(v.tensor_copy(end_c[:, 0:kk], ends))
            ntl["p"] += 1
            dve.wait_ge(tl_p, ntl["p"])
            if reverse:
                v.memset(lanes[0:kk, P:P + 1], first)
                chain(v.tensor_tensor_scan(lanes[0:kk, 0:P][:, ::-1], row[0:kk, :][:, ::-1],
                                           ps[0:kk, 6, 0:P][:, ::-1], first, op0, op1))
            else:
                v.memset(lanes[0:kk, 0:1], first)
                chain(v.tensor_tensor_scan(lanes[0:kk, 1:P + 1], row[0:kk, :], ps[0:kk, 6, 0:P], first,
                                           op0, op1))
            ntl["p"] += 1
            dve.wait_ge(tl_p, ntl["p"])
            chain(v.tensor_copy(carry[:, 0:kk], ps[:, 7, 0:kk]))
            dve.wait_ge(tl_d, ntl["d"])

        def carry_pe(pe, kk, reverse=False):
            tr = nc.tensor.transpose
            ntl["pe_d"] += 1
            pe.wait_ge(tl_d, ntl["pe_d"])
            tr(ps[0:kk, 6, 0:P], end_c[:, 0:kk], ident).then_inc(tl_p, 1)
            ntl["pe_d"] += 1
            pe.wait_ge(tl_d, ntl["pe_d"])
            tr(ps[:, 7, 0:kk], lanes[0:kk, (1 if reverse else 0):(1 if reverse else 0) + P],
               ident[0:kk, 0:kk]).then_inc(tl_p, 1)
            ntl["pe_d"] += 1

        y64 = r1[:].rearrange("p (f t) -> p f t", t=T)
        rows64 = r2[:].rearrange("p (t f) -> p t f", f=HF)
        xg = r1[:].rearrange("p (d t f) -> p d t f", d=2, f=XF)
        SB = BT * XF
        x1rows = r2[:, 0:T * XF].rearrange("p (t f) -> p t f", f=XF)
        stg = [stage[:, s * BT * HF:(s + 1) * BT * HF] for s in range(2)]
        ht = [r3[:, s * QB * 512:(s + 1) * QB * 512].rearrange("p (q h d c) -> p q h d c", q=QB, h=2, d=2)
              for s in range(2)]
        ht_flat = [r3[:, s * QB * 512:(s + 1) * QB * 512] for s in range(2)]
        xtb = [r2[:, s * QB * 256:(s + 1) * QB * 256] for s in range(2)]
        l12v = l12[:].rearrange("p (j t) -> p j t", j=12)
        alv = alpha[:].rearrange("p (d t h) -> p d t h", d=2, h=HEADS)

        def gat_logits(l):
            sems = phase_sems(f"g{l}", "in0 in1 inh0 inh1 tr xt hm ht lg l12 free st off")
            s_in, s_inh = sems[0:2], sems[2:4]
            s_tr, s_xt, s_hm, s_ht, s_lg, s_l12, s_free, s_st, s_off = sems[4:]
            phase_over(sems)
            ahead_ht = 2 * l

            def sp_(sp):
                def load(b, slot):
                    if l == 0:
                        sp.dma_start(stg[slot].rearrange("p (d c) -> p d c", d=2),
                                     r1[:].rearrange("p (d c) -> p d c", d=2)[:, :, bass.ds(b * SB, SB)])\
                            .then_inc(s_in[slot], 16)
                    else:
                        sp.dma_start(stg[slot], r2[:, bass.ds(b * (BT * HF), BT * HF)])\
                            .then_inc(s_in[slot], 16)
                        sp.dma_start(ht[slot][:, :, :, 1, :],
                                     blk(h1d_dram, b).rearrange("p (q h c) -> p q h c", q=QB, h=2)
                                     ).then_inc(s_inh[slot], 16)

                def body(b, half, slot, ahead=True):
                    if ahead:
                        sp.wait_ge(s_l12, b + 1)
                        sp.sem_inc(s_off, 1)
                        sp.wait_ge((x_in, h1_in)[l], b + 2)
                        load(b + 1, 1 - slot)
                    sp.wait_ge(s_ht, QB * b + QB + ahead_ht)
                    sp.dma_start(blk(ht_dram[l], b), ht_flat[slot]).then_inc(s_st, 16)
                    if l == 0:
                        sp.dma_start(blk(xt_dram, b), xtb[slot]).then_inc(s_st, 16)
                    sp.wait_ge(s_st, (32 - 16 * l) * b + (32 - 16 * l))
                    sp.sem_inc(s_free, 1)

                sp.wait_ge((x_in, h1_in)[l], 1)
                sp.sem_inc(s_free, 2)
                load(0, 0)
                with sp.Fori(0, EB // 2) as i:
                    body(2 * i, i, 0)
                    body(2 * i + 1, i, 1)
                body(EB - 1, EB // 2, 0, ahead=False)

            def pe_(pe):
                mm, tr = nc.tensor.matmul, nc.tensor.transpose

                def body(b, half, slot):
                    pe.wait_ge(s_in[slot], 16 * half + 16)
                    if l == 1:
                        pe.wait_ge(s_inh[slot], 16 * half + 16)

                    def logits(q):
                        pe.wait_ge(s_ht, QB * b + q + 1 + ahead_ht)
                        for h in range(2):
                            o = ps[:, 4 + slot, (2 * q + h) * 24:(2 * q + h) * 24 + 24]
                            mm(o, ht[slot][:, q, h, 0, :], dv[:, D_RS[l]:D_RS[l] + 24], start=True, stop=False)
                            m = mm(o, ht[slot][:, q, h, 1, :], dv[:, D_RD[l]:D_RD[l] + 24],
                                   start=False, stop=True)
                        m.then_inc(s_lg, 1)

                    for q in range(QB):
                        pe.wait_ge((s_xt, s_ht)[l], QB * b + q + 1)
                        if l == 0:
                            tr(ps[:, q % 2, 0:P], stg[slot][:, q * P:(q + 1) * P], ident)
                            tr(ps[:, q % 2, P:2 * P], stg[slot][:, SB + q * P:SB + (q + 1) * P],
                               ident).then_inc(s_tr, 1)
                            pe.wait_ge(s_xt, QB * b + q + 3)
                            rhs = xtb[slot][:, q * 256:(q + 1) * 256]
                            mm(ps[:, 2 + q % 2, 0:256], wt[:, W_H0A:W_H0A + P], rhs, start=True, stop=True)
                            mm(ps[:, 2 + q % 2, 256:512], wt[:, W_H0B:W_H0B + P], rhs,
                               start=True, stop=True).then_inc(s_hm, 1)
                        else:
                            tr(ps[:, q % 2, 0:P], stg[slot][:, (2 * q) * P:(2 * q + 1) * P], ident)
                            tr(ps[:, q % 2, P:2 * P], stg[slot][:, (2 * q + 1) * P:(2 * q + 2) * P],
                               ident).then_inc(s_tr, 1)
                        if q:
                            logits(q - 1)
                    logits(QB - 1)

                loop(pe, EB, body)

            def act_(act):
                a = nc.scalar.activation

                def body(b, half, slot):
                    act.wait_ge(s_free, b + 1)
                    for q in range(QB):
                        act.wait_ge(s_tr, QB * b + q + 1)
                        if l == 0:
                            a(xtb[slot][:, q * 256:(q + 1) * 256], ps[:, q % 2, 0:256],
                              ACT.Identity).then_inc(s_xt, 1)
                            act.wait_ge(s_hm, QB * b + q + 1)
                            a(ht[slot][:, q].rearrange("p h d c -> p (h d c)"), ps[:, 2 + q % 2, :],
                              ACT.Identity, bias=dcol(D_C0)).then_inc(s_ht, 1)
                        else:
                            a(ht[slot][:, q, :, 0, :], ps[:, q % 2, 0:256].rearrange("p (h c) -> p h c", h=2),
                              ACT.Identity).then_inc(s_ht, 1)
                    act.wait_ge(s_lg, QB * b + QB)
                    a(l12v[:, :, bass.ds(b * BT, BT)],
                      ps[:, 4 + slot, 0:12 * BT].rearrange("p (t j) -> p j t", j=12),
                      ACT.Identity).then_inc(s_l12, 1)

                act.sem_inc((s_xt, s_ht)[l], 2)
                act.sem_inc(s_l12, 1)
                loop(act, EB, body)

            return sp_, pe_, act_, sems

        nsx = [0]
        nar = [r2[:, i * HEADS * T:(i + 1) * HEADS * T].rearrange("p (h t) -> p h t", h=HEADS) for i in range(7)]

        def softmax_dve(dve, l):
            v = nc.vector

            def chain(ins):
                ins.then_inc(sx, 1)
                nsx[0] += 1
                dve.wait_ge(sx, nsx[0])

            def scan(o, flag, val, first, op0, op1, rev=False):
                if rev:
                    return v.tensor_tensor_scan(o[:, ::-1], flag[:, ::-1], val[:, ::-1], first, op0, op1)
                return v.tensor_tensor_scan(o, flag, val, first, op0, op1)

            def bt(ap):
                return ap.unsqueeze(1).broadcast_to([P, HEADS, T])

            a_s, a_d, a_sd = (l12v[:, 4 * i:4 * i + 4, :] for i in range(3))
            e, sf, mf, mr, t0, t1, tot = nar
            if l == 1:
                for part in (a_d, a_sd):
                    for h in range(HEADS):
                        chain(v.tensor_tensor(t0[:, h, :], part[:, h, :], last, ALU.mult))
                    for h in range(HEADS):
                        chain(scan(part[:, h, :], nl_f, t0[:, h, :], 0.0, ALU.mult, ALU.add, True))
                    carry_dve(dve, part[:, :, 0], HEADS, row_r, ALU.mult, ALU.add, 0.0, reverse=True)
                    for h in range(HEADS):
                        chain(v.scalar_tensor_tensor(out=part[:, h, :], in0=sm, scalar=carry[:, h:h + 1],
                                                     in1=part[:, h, :], op0=ALU.mult, op1=ALU.add))
            chain(v.tensor_tensor(e, a_s, a_d, ALU.add))
            chain(v.scalar_tensor_tensor(out=e, in0=e, scalar=0.2, in1=e, op0=ALU.mult, op1=ALU.max))
            chain(v.scalar_tensor_tensor(out=sf, in0=a_sd, scalar=0.2, in1=a_sd, op0=ALU.mult, op1=ALU.max))
            chain(v.tensor_tensor(t0, e, sf, ALU.max))
            for h in range(HEADS):
                chain(scan(mf[:, h, :], ns_neg, t0[:, h, :], -BIG, ALU.add, ALU.max))
                chain(scan(mr[:, h, :], nl_neg, t0[:, h, :], -BIG, ALU.add, ALU.max, True))
            carry_dve(dve, mf[:, :, T - 1], HEADS, row_fn, ALU.add, ALU.max, -BIG)
            for h in range(HEADS):
                chain(v.scalar_tensor_tensor(out=mf[:, h, :], in0=pm_neg, scalar=carry[:, h:h + 1],
                                             in1=mf[:, h, :], op0=ALU.add, op1=ALU.max))
            carry_dve(dve, mr[:, :, 0], HEADS, row_rn, ALU.add, ALU.max, -BIG, reverse=True)
            for h in range(HEADS):
                chain(v.scalar_tensor_tensor(out=mr[:, h, :], in0=sm_neg, scalar=carry[:, h:h + 1],
                                             in1=mr[:, h, :], op0=ALU.add, op1=ALU.max))
            chain(v.tensor_tensor(mf, mf, mr, ALU.max))
            chain(v.tensor_tensor(t0, e, mf, ALU.subtract))
            chain(v.tensor_tensor(t1, sf, mf, ALU.subtract))
            dve.sem_inc(sx_act, 1)
            dve.wait_ge(sx_act, 3 * l + 3)
            for h in range(HEADS):
                chain(v.tensor_tensor(sf[:, h, :], t1[:, h, :], last, ALU.mult))
            chain(v.tensor_tensor(t1, e, sf, ALU.add))
            for h in range(HEADS):
                chain(scan(mf[:, h, :], ns_f, t1[:, h, :], 0.0, ALU.mult, ALU.add))
            carry_dve(dve, mf[:, :, T - 1], HEADS, row_f, ALU.mult, ALU.add, 0.0)
            for h in range(HEADS):
                chain(v.scalar_tensor_tensor(out=mf[:, h, :], in0=pm, scalar=carry[:, h:h + 1],
                                             in1=mf[:, h, :], op0=ALU.mult, op1=ALU.add))
            for h in range(HEADS):
                chain(v.tensor_tensor(mr[:, h, :], mf[:, h, :], last, ALU.mult))
            for h in range(HEADS):
                chain(scan(tot[:, h, :], nl_f, mr[:, h, :], 0.0, ALU.mult, ALU.add, True))
            carry_dve(dve, tot[:, :, 0], HEADS, row_r, ALU.mult, ALU.add, 0.0, reverse=True)
            for h in range(HEADS):
                chain(v.scalar_tensor_tensor(out=tot[:, h, :], in0=sm, scalar=carry[:, h:h + 1],
                                             in1=tot[:, h, :], op0=ALU.mult, op1=ALU.add))
            chain(v.tensor_single_scalar(tot, tot, 1e-16, ALU.add))
            chain(v.reciprocal(tot, tot))
            chain(v.tensor_single_scalar(tot, tot, 1.0 / HEADS, ALU.mult))
            chain(v.tensor_tensor(alv[:, 0].rearrange("p t h -> p h t"), e, tot, ALU.mult))
            chain(v.tensor_tensor(alv[:, 1].rearrange("p t h -> p h t"), sf, tot, ALU.mult))

        def softmax_act(act, l):
            e, sf, mf, mr, t0, t1, tot = nar
            act.wait_ge(sx_act, 3 * l + 1)
            nc.scalar.activation(e, t0, ACT.Exp).then_inc(sx_act, 1)
            nc.scalar.activation(t1, t1, ACT.Exp).then_inc(sx_act, 1)

        def softmax_pe(pe, l):
            if l == 1:
                carry_pe(pe, HEADS, reverse=True)
                carry_pe(pe, HEADS, reverse=True)
            carry_pe(pe, HEADS)
            carry_pe(pe, HEADS, reverse=True)
            carry_pe(pe, HEADS)
            carry_pe(pe, HEADS, reverse=True)

        prod = [stage[:, s * 1024:(s + 1) * 1024] for s in range(2)]
        fold = [stage[:, 2048 + s * 512:2560 + s * 512] for s in range(2)]

        def gat_values(l):
            sems = phase_sems(f"v{l}", "in0 in1 mm pr fd y")
            s_in = sems[0:2]
            s_mm, s_pr, s_fd, s_y = sems[2:]
            phase_over(sems)
            PB = 2 * QB

            def sp_(sp):
                def load(b, slot):
                    sp.dma_start(ht_flat[slot], blk(ht_dram[l], b)).then_inc(s_in[slot], 16)

                def body(b, half, slot):
                    sp.wait_ge(s_y, PB * b + 1)
                    load(b + 1, 1 - slot)

                load(0, 0)
                with sp.Fori(0, EB // 2) as i:
                    body(2 * i, i, 0)
                    body(2 * i + 1, i, 1)

            def pe_(pe):
                mm = nc.tensor.matmul

                def body(b, half, slot):
                    pe.wait_ge(s_in[slot], 16 * half + 16)
                    for j in range(PB):
                        pe.wait_ge(s_pr, PB * b + j + 1)
                        for d in range(2):
                            m = mm(ps[:, 2 * (j % 2) + d, :], ht[slot][:, j // 2, j % 2, d, :],
                                   wt[:, W_XW[l]:W_XW[l] + 512], start=True, stop=True)
                        m.then_inc(s_mm, 1)

                loop(pe, EB, body)

            def dve_(dve):
                v = nc.vector

                def finish(b, j):
                    g = j % 2
                    dve.wait_ge(s_pr, PB * b + j + 3)
                    v.tensor_tensor(fold[g], prod[g][:, 0:512], prod[g][:, 512:1024], ALU.add).then_inc(s_fd, 1)
                    dve.wait_ge(s_fd, PB * b + j + 1)
                    v.tensor_reduce(y64[:, :, bass.ds(b * BT + 2 * j, 2)].rearrange("p f t -> p t f"),
                                    fold[g].rearrange("p (t h f) -> p t f h", t=2, h=HEADS),
                                    AX.X, ALU.add).then_inc(s_y, 1)

                def body(b, half, slot):
                    for j in range(PB):
                        g = j % 2
                        dve.wait_ge(s_mm, PB * b + j + 1)
                        v.tensor_tensor(
                            prod[g].rearrange("p (d u f) -> p d u f", d=2, u=2 * HEADS),
                            ps[:, 2 * g:2 * g + 2, :].rearrange("p d (u f) -> p d u f", u=2 * HEADS),
                            alv[:, :, bass.ds(b * BT + 2 * j, 2), :].rearrange("p d t h -> p d (t h)")
                            .unsqueeze(3).broadcast_to([P, 2, 2 * HEADS, HF]),
                            ALU.mult).then_inc(s_pr, 1)
                        if j:
                            finish(b, j - 1)
                    finish(b, PB - 1)

                dve.sem_inc(s_pr, 2)
                loop(dve, EB, body)

            return sp_, pe_, dve_, sems

        nscn = [0]
        steps = nst[:, 0:16 * T]

        def tile_flags(dve, flag):
            nc.vector.tensor_copy(steps.rearrange("p (i t) -> p i t", t=T),
                                  flag.unsqueeze(1).broadcast_to([P, 16, T])).then_inc(sc, 1)
            nscn[0] += 1
            dve.wait_ge(sc, nscn[0])

        def scan_y(dve, feats):
            for i in range(feats // 16):
                part = r1[:, i * 16 * T:(i + 1) * 16 * T]
                nc.vector.tensor_tensor_scan(part, steps, part, 0.0, ALU.mult, ALU.add).then_inc(sc, 1)
                nscn[0] += 1
            dve.wait_ge(sc, nscn[0])

        ptmp = l12[:, 0:BT * HF]
        pbufs = [nst[:, i * 512:(i + 1) * 512] for i in range(6)] + [alpha[:, 1040:1552], l12[:, 1792:2304]]
        pst, pzc, psq, ptn = (pbufs[2 * i:2 * i + 2] for i in range(4))
        psel = [alpha[0:8, 0:512], alpha[0:8, 512:768]]
        prs = [alpha[:, 768 + 8 * g:776 + 8 * g] for g in range(2)]
        prt = [alpha[0:8, 784 + g * P:784 + (g + 1) * P] for g in range(2)]

        def gat_post(l):
            sems = phase_sems(f"p{l}", "in0 in1 sel tmp row tr st z zc sq v sd rs rt re r tn rl hn to oe free dma")
            s_in = sems[0:2]
            (s_sel, s_tmp, s_row, s_tr, s_st, s_z, s_zc, s_sq, s_v, s_sd, s_rs, s_rt, s_re, s_r, s_tn, s_rl,
             s_hn, s_to, s_oe, s_free, s_dma) = sems[2:]
            phase_over(sems)
            NU = len(UNITS)
            base = [r3[:, s * QB * 512:(s + 1) * QB * 512] for s in range(2)]
            res = [x_[:, 0:QB * 256] for x_ in base]
            hout = [x_[:, QB * 256:QB * 512] for x_ in base]
            xin = [r2[:, T * XF + s * QB * P:T * XF + (s + 1) * QB * P] for s in range(2)]
            per = 1 + l
            couples = [(i, [(g,) + UNITS[i + g] for g in range(2)]) for i in (0, 2)]

            def sp_(sp):
                def load(b, slot):
                    if l == 0:
                        sp.dma_start(res[slot].rearrange("p (q h c) -> p q h c", q=QB, h=2),
                                     blk(ht_dram[0], b).rearrange("p (q h d c) -> p q h d c", q=QB, h=2, d=2)
                                     [:, :, :, 1, :]).then_inc(s_in[slot], 16)
                    else:
                        sp.dma_start(res[slot], blk(h1d_dram, b)).then_inc(s_in[slot], 16)
                        sp.dma_start(xin[slot].rearrange("p (q c) -> p q c", q=QB),
                                     blk(xt_dram, b).rearrange("p (q d c) -> p q d c", q=QB, d=2)
                                     [:, :, 1, :]).then_inc(s_in[slot], 16)

                def body(b, half, slot, ahead=True):
                    if ahead:
                        sp.wait_ge(s_oe, NU * b + 2)
                        load(b + 1, 1 - slot)
                    if l == 0:
                        sp.wait_ge(s_hn, NU * b + NU)
                        sp.dma_start(blk(h1d_dram, b), hout[slot]).then_inc(s_dma, 16)
                        sp.wait_ge(s_dma, 16 * b + 16)
                        sp.sem_inc(s_free, 1)

                if l == 0:
                    sp.sem_inc(s_free, 2)
                for part, c in zip(psel, (0, 1024)):
                    sp.dma_start(part, sel[0:8, c:c + part.shape[1]]).then_inc(s_sel, 16)
                load(0, 0)
                with sp.Fori(0, EB // 2) as i:
                    body(2 * i, i, 0)
                    body(2 * i + 1, i, 1)
                body(EB - 1, EB // 2, 0, ahead=False)

            def pe_(pe):
                mm, tr = nc.tensor.matmul, nc.tensor.transpose

                def body(b, half, slot):
                    pe.wait_ge(s_row, b + 1)
                    for i, couple in couples:
                        w = NU * b + i

                        def stats(kk):
                            for g, q0, nq in couple:
                                pe.wait_ge(s_sq, per * w + 2 * kk + g + 1)
                                for j in range((2 - kk) * nq):
                                    c = 2 + 2 * kk
                                    m = mm(ps[:, 4 + g, c * j:c * (j + 1)], psq[g][:, j * P:(j + 1) * P],
                                           k((K_J2, K_J4)[kk], c), start=True, stop=True)
                                m.then_inc(s_v, 1)
                            for g, q0, nq in couple:
                                pe.wait_ge(s_rs, per * w + 2 * kk + g + 1)
                                tr(ps[0:4 * nq, 4 + g, P:2 * P], prs[g][:, 0:4 * nq], ident).then_inc(s_rt, 1)
                            for g, q0, nq in couple:
                                pe.wait_ge(s_re, per * w + 2 * kk + g + 1)
                                for j in range((2 - kk) * nq):
                                    m = mm(ps[:, 4 + g, j * P:(j + 1) * P],
                                           psel[kk][0:4 * nq, j * P:(j + 1) * P], prt[g][0:4 * nq, :],
                                           start=True, stop=True)
                                m.then_inc(s_r, 1)

                        for g, q0, nq in couple:
                            pe.wait_ge(s_oe, w + g + 1)
                            for j in range(2 * nq):
                                c = (2 * q0 + j) * P
                                t = tr(ps[:, g, j * P:(j + 1) * P], stg[slot][:, c:c + P], ident)
                            t.then_inc(s_tr, 1)
                        for g, q0, nq in couple:
                            pe.wait_ge(s_st, w + g + 1)
                            mm(ps[:, 2 + g, 0:nq * 256], k(K_C64), pst[g][:, 0:nq * 256],
                               start=True, stop=True).then_inc(s_z, 1)
                        stats(0)
                        for g, q0, nq in couple:
                            pe.wait_ge(s_hn, w + g + 1)
                            ho = hout[slot][:, q0 * 256:(q0 + nq) * 256]
                            if l == 0:
                                for j in range(2 * nq):
                                    t = tr(ps[:, 6 + g, j * P:(j + 1) * P], ho[:, j * P:(j + 1) * P], ident)
                                t.then_inc(s_to, 1)
                            else:
                                m = nq * P
                                hv = ho.rearrange("p (q h c) -> p q h c", q=nq, h=2)
                                pe.wait_ge(s_in[slot], 32 * half + 32)
                                mm(ps[:, 6 + g, 0:m], k(K_C32), xin[slot][:, q0 * P:q0 * P + m],
                                   start=True, stop=False)
                                mm(ps[:, 6 + g, 0:m], dv[:, D_OA:D_OA + P], hv[:, :, 0, :],
                                   start=False, stop=False)
                                mm(ps[:, 6 + g, 0:m], dv[:, D_OB:D_OB + P], hv[:, :, 1, :],
                                   start=False, stop=True).then_inc(s_z, 1)
                        if l == 1:
                            stats(1)
                            for g, q0, nq in couple:
                                pe.wait_ge(s_tn, 2 * w + 2 + g + 1)
                                for j in range(nq):
                                    t = tr(ps[:, g, j * P:(j + 1) * P], ptn[g][:, j * P:(j + 1) * P], ident)
                                t.then_inc(s_to, 1)

                pe.wait_ge(s_sel, 32)
                loop(pe, EB, body)

            def act_(act):
                a = nc.scalar.activation

                def body(b, half, slot):
                    for i, couple in couples:
                        w = NU * b + i

                        def stats(kk):
                            for g, q0, nq in couple:
                                act.wait_ge(s_v, per * w + 2 * kk + g + 1)
                                a(prs[g][:, 0:4 * nq], ps[:, 4 + g, 0:4 * nq], ACT.Sqrt,
                                  bias=dcol(D_EPS)).then_inc(s_sd, 1)
                            for g, q0, nq in couple:
                                act.wait_ge(s_rt, per * w + 2 * kk + g + 1)
                                a(prt[g][0:4 * nq, :], ps[0:4 * nq, 4 + g, P:2 * P],
                                  ACT.Identity).then_inc(s_re, 1)

                        for g, q0, nq in couple:
                            act.wait_ge(s_tr, w + g + 1)
                            a(pst[g][:, 0:nq * 256], ps[:, g, 0:nq * 256], ACT.Identity).then_inc(s_st, 1)
                        for g, q0, nq in couple:
                            act.wait_ge(s_z, per * w + g + 1)
                            a(psq[g][:, 0:nq * 256], ps[:, 2 + g, 0:nq * 256], ACT.Square,
                              bias=dcol(D_BC[l])).then_inc(s_sq, 1)
                            a(pzc[g][:, 0:nq * 256], ps[:, 2 + g, 0:nq * 256], ACT.Identity,
                              bias=dcol(D_BC[l])).then_inc(s_zc, 1)
                        stats(0)
                        for g, q0, nq in couple:
                            act.wait_ge(s_tn, per * w + g + 1)
                            a(ptn[g][:, 0:nq * 256], ptn[g][:, 0:nq * 256], ACT.Relu, bias=col(C_B[l]),
                              scale=col(C_G[l])).then_inc(s_rl, 1)
                        if l == 1:
                            for g, q0, nq in couple:
                                m = nq * P
                                act.wait_ge(s_z, 2 * w + 2 + g + 1)
                                a(psq[g][:, 0:m], ps[:, 6 + g, 0:m], ACT.Square,
                                  bias=dcol(D_OBC)).then_inc(s_sq, 1)
                                a(pzc[g][:, 0:m], ps[:, 6 + g, 0:m], ACT.Identity,
                                  bias=dcol(D_OBC)).then_inc(s_zc, 1)
                            stats(1)

                loop(act, EB, body)

            def dve_(dve):
                v = nc.vector

                def sums(b, slot):
                    v.tensor_tensor(ptmp.rearrange("p (t f) -> p t f", f=HF),
                                    pm[:, bass.ds(b * BT, BT)].unsqueeze(2).broadcast_to([P, BT, HF]),
                                    carry[:, 0:HF].unsqueeze(1).broadcast_to([P, BT, HF]),
                                    ALU.mult).then_inc(s_tmp, 1)
                    dve.wait_ge(s_tmp, b + 1)
                    v.tensor_tensor(stg[slot].rearrange("p (t f) -> p t f", f=HF),
                                    y64[:, :, bass.ds(b * BT, BT)].rearrange("p f t -> p t f"),
                                    ptmp.rearrange("p (t f) -> p t f", f=HF), ALU.add).then_inc(s_row, 1)

                def body(b, half, slot):
                    sums(b, slot)
                    if l == 0:
                        dve.wait_ge(s_free, b + 1)
                    dve.wait_ge(s_in[slot], (16 + 16 * l) * half + (16 + 16 * l))
                    for i, couple in couples:
                        w = NU * b + i

                        def norm(kk):
                            for g, q0, nq in couple:
                                dve.wait_ge(s_sd, per * w + 2 * kk + g + 1)
                                v.reciprocal(prs[g][:, 0:4 * nq], prs[g][:, 0:4 * nq]).then_inc(s_rs, 1)
                            for g, q0, nq in couple:
                                n = nq * (256, P)[kk]
                                dve.wait_ge(s_r, per * w + 2 * kk + g + 1)
                                dve.wait_ge(s_zc, per * w + 2 * kk + g + 1)
                                v.tensor_tensor(ptn[g][:, 0:n], pzc[g][:, 0:n], ps[:, 4 + g, 0:n],
                                                ALU.mult).then_inc(s_tn, 1)

                        norm(0)
                        for g, q0, nq in couple:
                            dve.wait_ge(s_rl, w + g + 1)
                            v.tensor_tensor(hout[slot][:, q0 * 256:(q0 + nq) * 256],
                                            res[slot][:, q0 * 256:(q0 + nq) * 256],
                                            ptn[g][:, 0:nq * 256], ALU.add).then_inc(s_hn, 1)
                        if l == 1:
                            norm(1)
                        for g, q0, nq in couple:
                            dve.wait_ge(s_to, w + g + 1)
                            if l == 0:
                                v.tensor_copy(r2[:, bass.ds(b * (BT * HF) + q0 * 256, nq * 256)],
                                              ps[:, 6 + g, 0:nq * 256]).then_inc(s_oe, 1)
                            else:
                                v.tensor_copy(r2[:, bass.ds(b * (BT * XF) + q0 * P, nq * P)],
                                              ps[:, g, 0:nq * P]).then_inc(s_oe, 1)
                    dve.wait_ge(s_oe, NU * b + NU + 2)
                    dve.sem_inc(rows_ready, 1)

                dve.sem_inc(s_oe, 2)
                loop(dve, EB, body)

            return sp_, pe_, act_, dve_, sems

        off[0] = 0
        gxr, gx, gh, g_r, g_z, g_w, g_u, g_n, g_d, go = ([lay(r2, 512) for _ in range(2)] for _ in range(10))
        gru_sems = phase_sems("q", "in0 in1 sel tr x mm rz u n zh dc h y c zc sq v sd rs rt re r o to oe free st")
        gi = gru_sems[0:2]
        (q_sel, q_tr, q_x, q_mm, q_rz, q_u, q_n, q_zh, q_dc, q_h, q_y, q_c, q_zc, q_sq, q_v, q_sd, q_rs, q_rt, q_re,
         q_r, q_o, q_to, q_oe, q_free, q_st) = gru_sems[2:]
        qsel = l12[0:16, 0:512]
        qrs = [g_n[s][:, 0:16] for s in range(2)]
        qrt = [g_n[s][0:16, P:2 * P] for s in range(2)]
        phase_over(gru_sems)

        def gate(w, g):
            return wt[:, w + g * P:w + (g + 1) * P]

        def dgru_sp(sp):
            def load(b, slot):
                sp.dma_start(gxr[slot], blk(x1_blk, b)).then_inc(gi[slot], 16)

            def body(b, i, ns):
                for s in range(ns):
                    sp.wait_ge(q_oe, b + s + 2 + 1)
                    sp.dma_start(blk(out_blk, b + s), go[s]).then_inc(q_st, 16)
                    sp.wait_ge(q_st, 16 * b + 16 * s + 16)
                    sp.sem_inc(q_free, 1)

            sp.dma_start(qsel, sel[:, 1024:1536]).then_inc(q_sel, 16)
            sp.wait_ge(put_x1, ALL)
            sp.sem_inc(q_free, 2)
            load(0, 0)
            load(1, 1)
            with sp.Fori(0, DB // 2 - 1) as i:
                sp.wait_ge(q_tr, 2 * i + 2)
                load(2 * i + 2, 0)
                load(2 * i + 3, 1)
                body(2 * i, i, 2)
            sp.wait_ge(q_tr, DB - 1)
            load(DB - 1, 0)
            body(DB - 3, DB // 2 - 1, 2)
            body(DB - 1, DB // 2, 1)
            sp.sem_inc(out_done, 1)

        def dgru_pe(pe):
            mm, tr = nc.tensor.matmul, nc.tensor.transpose

            def body(b, i, ns):
                for s in range(ns):
                    pe.wait_ge(gi[s], 16 * i + 16)
                    pe.wait_ge(q_oe, b + s + 1)
                    for j in range(4):
                        t = tr(ps[:, 6 + s, j * P:(j + 1) * P], gxr[s][:, j * P:(j + 1) * P], ident)
                    t.then_inc(q_tr, 1)
                for st in range(STEPS):
                    for s in range(ns):
                        c = 8 * i + ns * st + s
                        if st == 0:
                            pe.wait_ge(q_x, b + s + 1)
                        else:
                            pe.wait_ge(q_h, c - ns + 1)
                        for g in (1, 0, 2):
                            mm(ps[:, 3 * s + g, :], gate(W_HH, g), (gx if st == 0 else gh)[s],
                               start=True, stop=True).then_inc(q_mm, 1)
                for s in range(ns):
                    pe.wait_ge(q_y, b + s + 1)
                    mm(ps[:, 3 * s, :], k(K_C32), g_u[s], start=True, stop=True).then_inc(q_c, 1)
                for s in range(ns):
                    pe.wait_ge(q_sq, b + s + 1)
                    for j in range(4):
                        m = mm(ps[:, 3 * s + 1, 4 * j:4 * j + 4], g_z[s][:, j * P:(j + 1) * P], k(K_J4, 4),
                               start=True, stop=True)
                    m.then_inc(q_v, 1)
                for s in range(ns):
                    pe.wait_ge(q_rs, b + s + 1)
                    tr(ps[0:16, 3 * s + 1, P:2 * P], qrs[s], ident).then_inc(q_rt, 1)
                for s in range(ns):
                    pe.wait_ge(q_re, b + s + 1)
                    for j in range(4):
                        m = mm(ps[:, 3 * s + 1, j * P:(j + 1) * P], qsel[:, j * P:(j + 1) * P], qrt[s],
                               start=True, stop=True)
                    m.then_inc(q_r, 1)
                for s in range(ns):
                    pe.wait_ge(q_o, b + s + 1)
                    for j in range(4):
                        t = tr(ps[:, 6 + s, j * P:(j + 1) * P], g_d[s][:, j * P:(j + 1) * P], ident)
                    t.then_inc(q_to, 1)

            pe.wait_ge(q_sel, 16)
            pairs(pe, 0, DB, body)

        def dgru_act(act):
            a = nc.scalar.activation

            def body(b, i, ns):
                for s in range(ns):
                    act.wait_ge(q_tr, b + s + 1)
                    a(gx[s], ps[:, 6 + s, :], ACT.Identity).then_inc(q_x, 1)
                for st in range(STEPS):
                    for s in range(ns):
                        c = 8 * i + ns * st + s
                        act.wait_ge(q_mm, 3 * c + 1)
                        a(g_z[s], ps[:, 3 * s + 1, :], ACT.Sigmoid, bias=dcol(D_BZ)).then_inc(q_rz, 1)
                        a(g_w[s], ps[:, 3 * s + 1, :], ACT.Sigmoid, bias=dcol(D_NBZ), scale=-1.0)\
                            .then_inc(q_rz, 1)
                        act.wait_ge(q_mm, 3 * c + 2)
                        a(g_r[s], ps[:, 3 * s, :], ACT.Sigmoid, bias=dcol(D_BR)).then_inc(q_rz, 1)
                    for s in range(ns):
                        c = 8 * i + ns * st + s
                        act.wait_ge(q_u, c + 1)
                        a(g_n[s], g_u[s], ACT.Tanh, bias=col(C_BIHN)).then_inc(q_n, 1)
                for s in range(ns):
                    act.wait_ge(q_c, b + s + 1)
                    a(g_z[s], ps[:, 3 * s, :], ACT.Square).then_inc(q_sq, 1)
                    a(g_r[s], ps[:, 3 * s, :], ACT.Identity).then_inc(q_zc, 1)
                for s in range(ns):
                    act.wait_ge(q_v, b + s + 1)
                    a(qrs[s], ps[:, 3 * s + 1, 0:16], ACT.Sqrt, bias=dcol(D_EPS)).then_inc(q_sd, 1)
                for s in range(ns):
                    act.wait_ge(q_rt, b + s + 1)
                    a(qrt[s], ps[0:16, 3 * s + 1, P:2 * P], ACT.Identity).then_inc(q_re, 1)

            pairs(act, 0, DB, body)

        def dgru_dve(dve):
            v = nc.vector

            def body(b, i, ns):
                for st in range(STEPS):
                    for s in range(ns):
                        c = 8 * i + ns * st + s
                        h = (gx if st == 0 else gh)[s]
                        dve.wait_ge(q_rz, 3 * c + 1)
                        if st:
                            dve.wait_ge(q_h, c - ns + 1)
                        v.tensor_tensor(g_z[s], g_z[s], h, ALU.mult).then_inc(q_zh, 1)
                        dve.wait_ge(q_mm, 3 * c + 3)
                        dve.wait_ge(q_rz, 3 * c + 3)
                        v.scalar_tensor_tensor(out=g_u[s], in0=ps[:, 3 * s + 2, :], scalar=col(C_BHHN),
                                               in1=g_r[s], op0=ALU.add, op1=ALU.mult).then_inc(q_u, 1)
                    for s in range(ns):
                        c = 8 * i + ns * st + s
                        dve.wait_ge(q_n, c + 1)
                        v.tensor_tensor(g_d[s], g_w[s], g_n[s], ALU.mult).then_inc(q_dc, 1)
                        dve.wait_ge(q_dc, c + 1)
                        dve.wait_ge(q_zh, c + 1)
                        v.tensor_tensor(gh[s], g_d[s], g_z[s], ALU.add).then_inc(q_h, 1)
                for s in range(ns):
                    dve.wait_ge(q_h, 8 * i + ns * (STEPS - 1) + s + 1)
                    v.tensor_tensor(g_u[s], gx[s], gh[s], ALU.add).then_inc(q_y, 1)
                for s in range(ns):
                    dve.wait_ge(q_sd, b + s + 1)
                    v.reciprocal(qrs[s], qrs[s]).then_inc(q_rs, 1)
                for s in range(ns):
                    dve.wait_ge(q_r, b + s + 1)
                    dve.wait_ge(q_zc, b + s + 1)
                    v.tensor_tensor(g_d[s], g_r[s], ps[:, 3 * s + 1, :], ALU.mult).then_inc(q_o, 1)
                for s in range(ns):
                    dve.wait_ge(q_to, b + s + 1)
                    dve.wait_ge(q_free, b + s + 1)
                    v.tensor_copy(go[s], ps[:, 6 + s, :]).then_inc(q_oe, 1)

            dve.sem_inc(q_oe, 2)
            pairs(dve, 0, DB, body)

        hs = r2[:, T * XF:2 * T * XF]
        work = r2[:, T * BONDF:T * XF]
        bondv = r2[:, 0:T * BONDF].rearrange("p (t c) -> p t c", c=BONDF)
        hd = r3[:, 0:T * XF]
        y32 = r1[:, 0:T * XF].rearrange("p (f t) -> p f t", t=T)
        ag = r1[:, T * XF:2 * T * XF]
        uw = l12[:, 0:4 * 512]
        vb = l12[:, 2048:2048 + P]
        mi = [sem(f"mi_in{s}") for s in range(2)]
        mi_tr, mi_cp, ld_bond, ld_uw = sem("mi_tr"), sem("mi_cp"), sem("ld_bond"), sem("ld_uw")

        def init_sp(sp):
            def load(b, slot):
                sp.dma_start(stg[slot].rearrange("p (d c) -> p d c", d=2),
                             r1[:].rearrange("p (d c) -> p d c", d=2)[:, :, bass.ds(b * SB, SB)])\
                    .then_inc(mi[slot], 16)

            sp.dma_start(bondv, sort_s[1:EP + 1, 2:PAY].rearrange("(p t) c -> p t c", t=T)).then_inc(ld_bond, 16)
            sp.dma_start(l12[:, 0:2176], bondw).then_inc(ld_uw, 16)
            sp.wait_ge(got_x1, 2 * ALL)
            load(0, 0)
            with sp.Fori(0, EB // 2) as i:
                for s in range(2):
                    sp.wait_ge(mi_cp, 4 * i + 2 * s + 1)
                    load(2 * i + s + 1, 1 - s)

        def init_pe(pe):
            tr = nc.tensor.transpose

            def body(b, half, slot):
                pe.wait_ge(mi[slot], 16 * half + 16)
                pe.wait_ge(mi_cp, 2 * b + 1)
                for d in range(2):
                    for q in range(QB):
                        t = tr(ps[:, 2 * d + q // 4, (q % 4) * P:(q % 4 + 1) * P],
                               stg[slot][:, d * SB + q * P:d * SB + (q + 1) * P], ident)
                t.then_inc(mi_tr, 1)

            loop(pe, EB, body)

        def init_act(act):
            a = nc.scalar.activation

            def body(b, half, slot):
                act.wait_ge(mi_tr, b + 1)
                for o, d in ((hs, 0), (hd, 1)):
                    for p, (c, n) in enumerate(PARTS):
                        last_ = a(o[:, bass.ds(b * SB + c, n)], ps[:, 2 * d + p, 0:n], ACT.Identity)
                last_.then_inc(mi_cp, 2)

            act.sem_inc(mi_cp, 1)
            loop(act, EB, body)

        mg = [sem(f"mg_in{s}") for s in range(2)]
        mg_mm, mg_v, mg_pr, mg_rd, mg_y = (sem(f"mg_{n}") for n in ("mm", "v", "pr", "rd", "y"))
        hq = [stage[:, s * SB:(s + 1) * SB] for s in range(2)]
        msum = stage[:, 2 * SB:2 * SB + P]
        mprod = [nst[:, s * 1024:(s + 1) * 1024] for s in range(2)]
        uw4 = uw.rearrange("p (q c) -> p q c", q=4)
        PB = 2 * QB

        def msg_sp(sp, m):
            def load(b, slot):
                sp.dma_start(hq[slot], hd[:, bass.ds(b * SB, SB)]).then_inc(mg[slot], 16)

            load(0, 0)
            with sp.Fori(0, EB // 2) as i:
                for s in range(2):
                    sp.wait_ge(mg_y, QB * EB * m + 2 * QB * i + QB * s + 1)
                    load(2 * i + s + 1, 1 - s)

        def msg_pe(pe, m):
            mm = nc.tensor.matmul

            def body(b, half, slot):
                pe.wait_ge(mg[slot], 16 * (4 - slot) * m + 16 * half + 16)
                for q in range(QB):
                    lhs = hq[slot][:, q * P:(q + 1) * P]
                    for r in range(2):
                        w = PB * EB * m + PB * b + 2 * q + r
                        pe.wait_ge(mg_pr, w + 1)
                        for j in range(2):
                            t = mm(ps[:, 2 * r + j, :], lhs, uw4[:, 2 * r + j, :], start=True, stop=True)
                        t.then_inc(mg_mm, 1)
                    mm(ps[:, 4 + (slot + q) % 2, 0:P], lhs, vb, start=True, stop=True).then_inc(mg_v, 1)

            loop(pe, EB, body)

        def msg_dve(dve, m):
            v = nc.vector

            def reduce(w, r):
                dve.wait_ge(mg_pr, w + 3)
                v.tensor_reduce(msum[:, r * 64:(r + 1) * 64],
                                mprod[r].rearrange("p (u k) -> p u k", k=BONDF), AX.X, ALU.add).then_inc(mg_rd, 1)

            def body(b, half, slot):
                for q in range(QB):
                    w = PB * EB * m + PB * b + 2 * q
                    for r in range(2):
                        dve.wait_ge(mg_mm, w + r + 1)
                        v.tensor_tensor(
                            mprod[r].rearrange("p (t i k) -> p t i k", t=2, k=BONDF),
                            ps[:, 2 * r:2 * r + 2, :].rearrange("p t (i k) -> p t i k", k=BONDF),
                            bondv[:, bass.ds(b * BT + 4 * q + 2 * r, 2), :].unsqueeze(2)
                            .broadcast_to([P, 2, XF, BONDF]), ALU.mult).then_inc(mg_pr, 1)
                    for r in range(2):
                        reduce(w + r, r)
                    u = QB * EB * m + QB * b + q
                    dve.wait_ge(mg_v, u + 1)
                    dve.wait_ge(mg_rd, w + 2)
                    v.tensor_tensor(y32[:, :, bass.ds(b * BT + 4 * q, 4)].rearrange("p f t -> p t f"),
                                    msum.rearrange("p (t f) -> p t f", f=XF),
                                    ps[:, 4 + (slot + q) % 2, 0:P].rearrange("p (t f) -> p t f", f=XF),
                                    ALU.add).then_inc(mg_y, 1)
                    dve.wait_ge(mg_y, u + 2)

            if m == 0:
                dve.sem_inc(mg_pr, 2)
                dve.sem_inc(mg_y, 1)
            loop(dve, EB, body)

        eg = []
        for who in range(2):
            eg.append({n: sem(f"e{who}_{n}") for n in (
                "in0", "in1", "tmp", "row", "tr", "at", "mm", "rz", "u", "n", "dc", "h", "free", "st")})
        ering = [stage[:, s * SB:(s + 1) * SB] for s in range(2)]
        etmp = stage[:, 2 * SB:3 * SB]
        e_at, e_r, e_z = ([nst[:, i * SB + c:i * SB + c + n] for c, n in PARTS] for i in range(3))
        e_u, e_n, e_d = ([work[:, i * SB + c:i * SB + c + n] for c, n in PARTS] for i in range(3))

        def egru_sp(sp, m, who):
            s = eg[who]
            if who == 0:
                if m == STEPS - 1:
                    return

                def body(b, half, slot):
                    sp.wait_ge(s["row"], EB * m + b + 1)
                    sp.dma_start(agg_tab[0:EP, :].rearrange("(p t) f -> p (t f)", t=T)
                                 [:, bass.ds(b * SB, SB)], ering[slot]).then_inc(s["st"], 16)
                    sp.wait_ge(s["st"], 16 * EB * m + 16 * b + 16)
                    sp.sem_inc(s["free"], 1)

                loop(sp, EB, body)
                sp.sem_inc(agg_stored, 1)
            else:
                def load(b, slot):
                    sp.dma_start(ering[slot], ag[:, bass.ds(b * SB, SB)]).then_inc(s[f"in{slot}"], 16)

                sp.wait_ge(agg_in, EB * (m + 1))
                load(0, 0)
                with sp.Fori(0, EB // 2) as i:
                    for t in range(2):
                        sp.wait_ge(s["h"], 2 * EB * m + 4 * i + 2 * t + 2)
                        load(2 * i + t + 1, 1 - t)

        def egru_pe(pe, m, who):
            s = eg[who]
            state = (hs, hd)[who]
            mm, tr = nc.tensor.matmul, nc.tensor.transpose

            def body(b, half, slot):
                if who == 0:
                    pe.wait_ge(s["row"], EB * m + b + 1)
                else:
                    pe.wait_ge(s[f"in{slot}"], 16 * (4 - slot) * m + 16 * half + 16)
                for p, (c, n) in enumerate(PARTS):
                    w = 2 * EB * m + 2 * b + p
                    pe.wait_ge(s["h"], w + 1)
                    for j in range(n // P):
                        t = tr(ps[:, 4 * p + 3, j * P:(j + 1) * P], ering[slot][:, c + j * P:c + (j + 1) * P],
                               ident)
                    t.then_inc(s["tr"], 1)
                for p, (c, n) in enumerate(PARTS):
                    w = 2 * EB * m + 2 * b + p
                    h = state[:, bass.ds(b * SB + c, n)]
                    a = e_at[p][:, 0:n]
                    pe.wait_ge(s["at"], w + 1)
                    for g in range(2):
                        mm(ps[:, 4 * p + g, 0:n], gate(W_IH, g), a, start=True, stop=False)
                        mm(ps[:, 4 * p + g, 0:n], gate(W_HH, g), h, start=False, stop=True).then_inc(s["mm"], 1)
                    mm(ps[:, 4 * p + 2, 0:n], gate(W_HH, 2), h, start=True, stop=True).then_inc(s["mm"], 1)
                    mm(ps[:, 4 * p + 3, 0:n], gate(W_IH, 2), a, start=True, stop=True).then_inc(s["mm"], 1)

            loop(pe, EB, body)

        def egru_act(act, m, who):
            s = eg[who]
            a = nc.scalar.activation

            def body(b, half, slot):
                for p, (c, n) in enumerate(PARTS):
                    w = 2 * EB * m + 2 * b + p
                    act.wait_ge(s["tr"], w + 1)
                    a(e_at[p][:, 0:n], ps[:, 4 * p + 3, 0:n], ACT.Identity).then_inc(s["at"], 1)
                for p, (c, n) in enumerate(PARTS):
                    w = 2 * EB * m + 2 * b + p
                    act.wait_ge(s["mm"], 4 * w + 1)
                    a(e_r[p][:, 0:n], ps[:, 4 * p, 0:n], ACT.Sigmoid, bias=dcol(D_BR)).then_inc(s["rz"], 1)
                    act.wait_ge(s["mm"], 4 * w + 2)
                    a(e_z[p][:, 0:n], ps[:, 4 * p + 1, 0:n], ACT.Sigmoid, bias=dcol(D_BZ)).then_inc(s["rz"], 1)
                for p, (c, n) in enumerate(PARTS):
                    w = 2 * EB * m + 2 * b + p
                    act.wait_ge(s["u"], w + 1)
                    a(e_n[p][:, 0:n], e_u[p][:, 0:n], ACT.Tanh, bias=col(C_BIHN)).then_inc(s["n"], 1)

            loop(act, EB, body)

        def egru_dve(dve, m, who):
            s = eg[who]
            state = (hs, hd)[who]
            v = nc.vector

            def body(b, half, slot):
                if who == 0:
                    if m < STEPS - 1:
                        dve.wait_ge(s["free"], EB * m + b + 1)
                    v.tensor_tensor(etmp.rearrange("p (t f) -> p t f", f=XF),
                                    pm_s[:, bass.ds(b * BT, BT)].unsqueeze(2).broadcast_to([P, BT, XF]),
                                    carry[:, 0:XF].unsqueeze(1).broadcast_to([P, BT, XF]),
                                    ALU.mult).then_inc(s["tmp"], 1)
                    dve.wait_ge(s["tmp"], EB * m + b + 1)
                    v.tensor_tensor(ering[slot].rearrange("p (t f) -> p t f", f=XF),
                                    y32[:, :, bass.ds(b * BT, BT)].rearrange("p f t -> p t f"),
                                    etmp.rearrange("p (t f) -> p t f", f=XF), ALU.add).then_inc(s["row"], 1)
                for p, (c, n) in enumerate(PARTS):
                    w = 2 * EB * m + 2 * b + p
                    dve.wait_ge(s["mm"], 4 * w + 3)
                    dve.wait_ge(s["rz"], 2 * w + 1)
                    v.scalar_tensor_tensor(out=e_u[p][:, 0:n], in0=ps[:, 4 * p + 2, 0:n], scalar=col(C_BHHN),
                                           in1=e_r[p][:, 0:n], op0=ALU.add, op1=ALU.mult).then_inc(s["dc"], 1)
                    dve.wait_ge(s["dc"], 6 * EB * m + 6 * b + p + 1)
                    dve.wait_ge(s["mm"], 4 * w + 4)
                    v.tensor_tensor(e_u[p][:, 0:n], e_u[p][:, 0:n], ps[:, 4 * p + 3, 0:n], ALU.add)\
                        .then_inc(s["u"], 1)
                for p, (c, n) in enumerate(PARTS):
                    w = 2 * EB * m + 2 * b + p
                    h = state[:, bass.ds(b * SB + c, n)]
                    dve.wait_ge(s["n"], w + 1)
                    v.tensor_tensor(e_d[p][:, 0:n], h, e_n[p][:, 0:n], ALU.subtract).then_inc(s["dc"], 1)
                    dve.wait_ge(s["dc"], 6 * EB * m + 6 * b + 2 * p + 3)
                    dve.wait_ge(s["rz"], 2 * w + 2)
                    v.tensor_tensor(e_d[p][:, 0:n], e_d[p][:, 0:n], e_z[p][:, 0:n], ALU.mult)\
                        .then_inc(s["dc"], 1)
                    dve.wait_ge(s["dc"], 6 * EB * m + 6 * b + 2 * p + 4)
                    v.tensor_tensor(h, e_d[p][:, 0:n], e_n[p][:, 0:n], ALU.add).then_inc(s["h"], 1)

            if m == 0:
                dve.sem_inc(s["h"], 2)
                if who == 0:
                    dve.sem_inc(s["free"], 2)
            loop(dve, EB, body)

        x1s = ag
        fin_rows = r3[:, 0:T * XF]
        fs = {n: sem(f"f_{n}") for n in ("ld", "y", "c", "zc", "sq", "v", "sd", "rs", "rt", "re", "r", "o", "to",
                                          "oe", "keep")}
        fsel = nst[0:16, 0:512]
        f_rs = [e_n[p][:, 0:n // XF] for p, (c, n) in enumerate(PARTS)]
        f_rt = [e_n[p][0:n // XF, P:2 * P] for p, (c, n) in enumerate(PARTS)]

        def keep_sp(sp):
            sp.dma_start(xs_dram, hs).then_inc(fs["keep"], 16)
            sp.wait_ge(fs["keep"], 16)

        def final_sp(sp):
            sp.dma_start(fsel, sel[:, 1024:1536]).then_inc(fs["ld"], 16)
            sp.dma_start(x1s, xs_dram).then_inc(fs["ld"], 16)

        def final_pe(pe):
            mm, tr = nc.tensor.matmul, nc.tensor.transpose

            def body(b, half, slot):
                for p, (c, n) in enumerate(PARTS):
                    w = 2 * b + p
                    pe.wait_ge(fs["y"], w + 1)
                    mm(ps[:, 4 * p, 0:n], k(K_C32), e_u[p], start=True, stop=True).then_inc(fs["c"], 1)
                for p, (c, n) in enumerate(PARTS):
                    w = 2 * b + p
                    pe.wait_ge(fs["sq"], w + 1)
                    for j in range(n // P):
                        m = mm(ps[:, 4 * p + 1, 4 * j:4 * j + 4], e_z[p][:, j * P:(j + 1) * P], k(K_J4, 4),
                               start=True, stop=True)
                    m.then_inc(fs["v"], 1)
                for p, (c, n) in enumerate(PARTS):
                    pe.wait_ge(fs["rs"], 2 * b + p + 1)
                    tr(ps[0:n // XF, 4 * p + 1, P:2 * P], f_rs[p], ident).then_inc(fs["rt"], 1)
                for p, (c, n) in enumerate(PARTS):
                    pe.wait_ge(fs["re"], 2 * b + p + 1)
                    for j in range(n // P):
                        m = mm(ps[:, 4 * p + 1, j * P:(j + 1) * P], fsel[0:n // XF, j * P:(j + 1) * P], f_rt[p],
                               start=True, stop=True)
                    m.then_inc(fs["r"], 1)
                for p, (c, n) in enumerate(PARTS):
                    w = 2 * b + p
                    pe.wait_ge(fs["o"], w + 1)
                    for j in range(n // P):
                        t = tr(ps[:, 4 * p + 2, j * P:(j + 1) * P], e_d[p][:, j * P:(j + 1) * P], ident)
                    t.then_inc(fs["to"], 1)

            pe.wait_ge(fs["ld"], 32)
            loop(pe, EB, body)

        def final_act(act):
            a = nc.scalar.activation

            def body(b, half, slot):
                for p, (c, n) in enumerate(PARTS):
                    act.wait_ge(fs["c"], 2 * b + p + 1)
                    a(e_z[p], ps[:, 4 * p, 0:n], ACT.Square).then_inc(fs["sq"], 1)
                    a(e_r[p], ps[:, 4 * p, 0:n], ACT.Identity).then_inc(fs["zc"], 1)
                for p, (c, n) in enumerate(PARTS):
                    act.wait_ge(fs["v"], 2 * b + p + 1)
                    a(f_rs[p], ps[:, 4 * p + 1, 0:n // XF], ACT.Sqrt, bias=dcol(D_EPS)).then_inc(fs["sd"], 1)
                for p, (c, n) in enumerate(PARTS):
                    act.wait_ge(fs["rt"], 2 * b + p + 1)
                    a(f_rt[p], ps[0:n // XF, 4 * p + 1, P:2 * P], ACT.Identity).then_inc(fs["re"], 1)

            loop(act, EB, body)

        def final_dve(dve):
            v = nc.vector

            def body(b, half, slot):
                for p, (c, n) in enumerate(PARTS):
                    v.tensor_tensor(e_u[p], x1s[:, bass.ds(b * SB + c, n)], hs[:, bass.ds(b * SB + c, n)],
                                    ALU.add).then_inc(fs["y"], 1)
                for p, (c, n) in enumerate(PARTS):
                    w = 2 * b + p
                    dve.wait_ge(fs["sd"], w + 1)
                    v.reciprocal(f_rs[p], f_rs[p]).then_inc(fs["rs"], 1)
                for p, (c, n) in enumerate(PARTS):
                    w = 2 * b + p
                    dve.wait_ge(fs["r"], w + 1)
                    dve.wait_ge(fs["zc"], w + 1)
                    v.tensor_tensor(e_d[p], e_r[p], ps[:, 4 * p + 1, 0:n], ALU.mult).then_inc(fs["o"], 1)
                for p, (c, n) in enumerate(PARTS):
                    dve.wait_ge(fs["to"], 2 * b + p + 1)
                    v.tensor_copy(fin_rows[:, bass.ds(b * SB + c, n)], ps[:, 4 * p + 2, 0:n])\
                        .then_inc(fs["oe"], 1)
                dve.wait_ge(fs["oe"], 2 * b + 2)
                dve.sem_inc(rows_ready, 1)

            dve.wait_ge(fs["ld"], 32)
            loop(dve, EB, body)

        log0, log1 = gat_logits(0), gat_logits(1)
        val0, val1 = gat_values(0), gat_values(1)
        post0, post1 = gat_post(0), gat_post(1)
        block = ctx.enter_context(nc.Block())

        @block.sync
        def _(sp):
            prep_sp(sp)
            barrier(sp, "sp")
            dense_sp(sp, 0, DB)
            sp.sem_inc(dense_done, 1)
            barrier(sp, "sp", dense_sems)
            for log, val, post in ((log0, val0, post0), (log1, val1, post1)):
                log[0](sp)
                barrier(sp, "sp", log[-1])
                val[0](sp)
                barrier(sp, "sp", val[-1])
                post[0](sp)
                barrier(sp, "sp", post[-1])
            dgru_sp(sp)
            barrier(sp, "sp", gru_sems)
            init_sp(sp)
            barrier(sp, "sp")
            keep_sp(sp)
            for m in range(STEPS):
                msg_sp(sp, m)
                barrier(sp, "sp")
                egru_sp(sp, m, 0)
                barrier(sp, "sp")
                if m < STEPS - 1:
                    egru_sp(sp, m, 1)
                    barrier(sp, "sp")
            final_sp(sp)
            sp.wait_ge(put_out, ALL)

        @block.tensor
        def _(pe):
            prep_pe_(pe)
            barrier(pe, "pe")
            sort_pe(pe)
            barrier(pe, "pe")
            flags_pe(pe, 0)
            for l, (log, val, post) in enumerate(((log0, val0, post0), (log1, val1, post1))):
                log[1](pe)
                barrier(pe, "pe")
                softmax_pe(pe, l)
                if l == 0:
                    flags_pe(pe, 1)
                val[1](pe)
                barrier(pe, "pe")
                carry_pe(pe, HF)
                post[1](pe)
                barrier(pe, "pe")
            dgru_pe(pe)
            barrier(pe, "pe")
            init_pe(pe)
            barrier(pe, "pe")
            for m in range(STEPS):
                msg_pe(pe, m)
                barrier(pe, "pe")
                carry_pe(pe, XF)
                egru_pe(pe, m, 0)
                barrier(pe, "pe")
                if m < STEPS - 1:
                    egru_pe(pe, m, 1)
                    barrier(pe, "pe")
            final_pe(pe)

        @block.scalar
        def _(act):
            barrier(act, "act")
            dense_act(act, 0, DB)
            barrier(act, "act")
            for l, (log, val, post) in enumerate(((log0, val0, post0), (log1, val1, post1))):
                log[2](act)
                barrier(act, "act")
                softmax_act(act, l)
                barrier(act, "act")
                post[2](act)
                barrier(act, "act")
            dgru_act(act)
            barrier(act, "act")
            init_act(act)
            barrier(act, "act")
            for m in range(STEPS):
                barrier(act, "act")
                egru_act(act, m, 0)
                barrier(act, "act")
                if m < STEPS - 1:
                    egru_act(act, m, 1)
                    barrier(act, "act")
            final_act(act)

        @block.vector
        def _(dve):
            prep_dve_(dve)
            barrier(dve, "dve")
            sort_dve(dve)
            barrier(dve, "dve")
            flags_dve(dve, 0)
            for l, (log, val, post) in enumerate(((log0, val0, post0), (log1, val1, post1))):
                barrier(dve, "dve")
                softmax_dve(dve, l)
                if l == 0:
                    flags_dve(dve, 1)
                tile_flags(dve, ns_f)
                val[2](dve)
                barrier(dve, "dve")
                scan_y(dve, HF)
                carry_dve(dve, y64[:, :, T - 1], HF, row_f, ALU.mult, ALU.add, 0.0)
                post[3](dve)
                barrier(dve, "dve")
            dgru_dve(dve)
            barrier(dve, "dve")
            barrier(dve, "dve")
            dve.wait_ge(ld_bond, 16)
            for m in range(STEPS):
                msg_dve(dve, m)
                barrier(dve, "dve")
                tile_flags(dve, ns_fs)
                scan_y(dve, XF)
                carry_dve(dve, y32[:, :, T - 1], XF, row_fs, ALU.mult, ALU.add, 0.0)
                egru_dve(dve, m, 0)
                barrier(dve, "dve")
                if m < STEPS - 1:
                    egru_dve(dve, m, 1)
                    barrier(dve, "dve")
            final_dve(dve)

        @block.gpsimd
        def _(pool):
            def scatter(table, index, rows, done):
                for t in range(T):
                    nc.gpsimd.indirect_dma_start(table, bass.IndirectOffsetOnAxis(ap=index(t), axis=0),
                                                 rows(t), None).then_inc(done, 16)

            def gather(rows, table, index, done):
                for t in range(T):
                    nc.gpsimd.indirect_dma_start(rows(t), None, table,
                                                 bass.IndirectOffsetOnAxis(ap=index(t), axis=0)).then_inc(done, 16)

            def scatter_blocks(table, index, rows, done, before):
                for t in range(T):
                    if t % BT == 0:
                        pool.wait_ge(rows_ready, before + t // BT + 1)
                    nc.gpsimd.indirect_dma_start(table, bass.IndirectOffsetOnAxis(ap=index(t), axis=0),
                                                 rows(t), None).then_inc(done, 16)

            counts = [0, 0]

            def gather_blocks(parts, arrived):
                for t in range(T + 1):
                    if t == T or (t > BT and t % BT == 4):
                        b = (t - 1) // BT if t == T else t // BT - 1
                        pool.wait_ge((got_even, got_odd)[b % 2], counts[b % 2])
                        pool.sem_inc(arrived, 1)
                    if t == T:
                        break
                    for rows, table, index in parts:
                        nc.gpsimd.indirect_dma_start(
                            rows(t), None, table, bass.IndirectOffsetOnAxis(ap=index(t), axis=0)
                        ).then_inc((got_even, got_odd)[t // BT % 2], 16)
                        counts[t // BT % 2] += 16

            def at_step(index):
                return lambda t: index[:, t:t + 1]

            pool.wait_ge(rank_ready, 1)
            scatter(tmp_d, at_step(rank_i[0]), lambda t: pay_d[:, t, :], put_tmp_d)
            pool.wait_ge(put_tmp_d, ALL)
            pool.dma_start(pay_d.rearrange("p t c -> p (t c)"),
                           tmp_d.rearrange("(p t) c -> p (t c)", t=T)).then_inc(ld_tmp_d, 16)
            pool.wait_ge(rank_ready, 2)
            pool.wait_ge(ld_pay, 16)
            scatter(tmp_s, at_step(rank_i[1]), lambda t: pay_s[:, t, :], put_tmp_s)
            pool.wait_ge(put_tmp_s, ALL)
            pool.dma_start(pay_s.rearrange("p t c -> p (t c)"),
                           tmp_s.rearrange("(p t) c -> p (t c)", t=T)).then_inc(ld_tmp_s, 16)
            pool.wait_ge(rank_ready, 3)
            pool.wait_ge(init_dram, 16 * 6)
            scatter(sort_d, at_step(rank_i[2]), lambda t: pay_d[:, t, :], put_sort_d)
            pool.wait_ge(put_sort_d, ALL)

            def load_list(tab, to, edge, done):
                pool.dma_start(to, tab[1:EP + 1, :].rearrange("(p t) c -> p t c", t=T)).then_inc(done, 16)
                pool.dma_start(edge[:, 0:2], tab[0:EP, :].rearrange("(p t) c -> p t c", t=T)[:, 0, 0:2])\
                    .then_inc(done, 16)
                pool.dma_start(edge[:, 2:4], tab[2:EP + 2, :].rearrange("(p t) c -> p t c", t=T)[:, T - 1, 0:2])\
                    .then_inc(done, 16)

            load_list(sort_d, kid_d, edge_d, ld_kid_d)
            pool.wait_ge(ld_kid_d, 48)
            gather_blocks([(lambda t: xg[:, 0, t, :], x, lambda t: kid_d[:, t, 0:1]),
                           (lambda t: xg[:, 1, t, :], x, lambda t: kid_d[:, t, 1:2])], x_in)
            pool.wait_ge(rank_ready, 4)
            scatter(sort_s, at_step(rank_i[3]), lambda t: pay_s[:, t, :], put_sort_s)
            pool.wait_ge(put_sort_s, ALL)
            load_list(sort_s.bitcast(I32), pay_si, edge_s, ld_kid_s)
            pool.wait_ge(flags_ready, 2)
            scatter(pos_tab, at_step(put_s), at_step(pos_val), put_pos)
            pool.wait_ge(put_pos, ALL)
            gather(at_step(pos_of), pos_tab[0:NP, :], lambda t: kid_s[:, t, 1:2], got_pos)
            pool.wait_ge(dense_done, 1)
            scatter_blocks(h1_tab, at_step(put_d), lambda t: rows64[:, t, :], put_h1, 0)
            pool.wait_ge(put_h1, ALL)
            gather_blocks([(lambda t: rows64[:, t, :], h1_tab[0:NP, :], lambda t: kid_d[:, t, 0:1])], h1_in)
            scatter_blocks(x1_tab, at_step(put_d), lambda t: x1rows[:, t, :], put_x1, EB)
            pool.wait_ge(put_x1, ALL)
            gather(lambda t: xg[:, 0, t, :], x1_tab[0:NP, :], lambda t: kid_s[:, t, 0:1], got_x1)
            gather(lambda t: xg[:, 1, t, :], x1_tab[0:NP, :], lambda t: kid_s[:, t, 1:2], got_x1)
            pool.wait_ge(got_pos, ALL)
            for m in range(STEPS - 1):
                pool.wait_ge(agg_stored, m + 1)
                gather_blocks([(lambda t: ag[:, t * XF:(t + 1) * XF], agg_tab, at_step(pos_of))], agg_in)
            pool.wait_ge(out_done, 1)
            scatter_blocks(out, at_step(put_s), lambda t: fin_rows[:, t * XF:(t + 1) * XF], put_out, 2 * EB)
            pool.wait_ge(put_out, ALL)


def kernel(**inputs):
    import concourse.bacc as _bacc
    from concourse.bass_utils import run_bass_kernel_spmd as _run

    w = {n: np.asarray(a) for n, a in inputs.items()}
    f4 = np.float32

    def diag(block, n, rows=None, cols=None, places=None):
        r, c = block.shape
        m = np.zeros((rows or n * r, cols or n * c), f4)
        for i in range(n):
            ri, ci = (i, i) if places is None else places[i]
            m[ri * r:ri * r + r, ci * c:ci * c + c] = block
        return m

    eye, j64, j32 = np.eye(P, dtype=f4), np.full((64, 64), 1 / 64, f4), np.full((32, 32), 1 / 32, f4)
    j64, j32 = diag(j64, 2), diag(j32, 4)
    edge = np.arange(EP, dtype=f4).reshape(P, T)
    j2 = diag(np.full((64, 1), 1 / 64, f4), 2)
    j4 = diag(np.full((32, 1), 1 / 32, f4), 4)
    consts = np.concatenate([eye, eye - j64, eye - j32, np.triu(np.ones((P, P), f4), 1), j2, j4,
                             np.broadcast_to(np.arange(512, dtype=f4), (P, 512)), edge, edge + NP], 1)

    nw = w["L0_gnn_node_W"].T
    h0 = [diag(nw, 2, rows=P, places=[(2 * h, 0), (2 * h + 1, 1)]) for h in range(2)]
    xw, wh, at_s, at_d1, at_d2 = [], [], [], [], []
    for l in range(2):
        cw = w[f"L0_gnn_convW{l}"].reshape(HEADS, HF, HF)
        xw.append(diag(cw.transpose(2, 0, 1).reshape(HF, HEADS * HF), 2))
        wh += [diag(cw[h], 2) for h in range(HEADS)]
        for to, name, at in ((at_s, "src", (0,)), (at_d1, "dst", (4, 8)), (at_d2, "src", (8,))):
            for h in range(HEADS):
                m = np.zeros((HF, 12), f4)
                for c in at:
                    m[:, c + h] = w[f"L0_gnn_att_{name}{l}"][h]
                to.append(diag(m, 2))

    def gates(name):
        m = w[name].reshape(3, XF, XF)
        return [diag(m[g].T, 4) for g in range(3)]

    def cols(name, times, parts=1):
        return [np.tile(a, times)[:, None] for a in w[name].reshape(parts, -1)]

    weights = np.concatenate(
        h0 + xw + gates("L1_gnn_W_ih") + gates("L1_gnn_W_hh")
        + cols("L0_gnn_node_b", 2) + cols("L0_gnn_drone_b", 2) + cols("L0_gnn_out_b", 4)
        + cols("L1_gnn_b_ih", 4, 3) + cols("L1_gnn_b_hh", 4, 3)
        + [c for l in range(2) for n in ("convb", "ln_g", "ln_b") for c in cols(f"L0_gnn_{n}{l}", 2)], 1)
    ow = w["L0_gnn_out_W"]
    out_ab = [diag(ow, 2, rows=P, places=[(2 * h, 0), (2 * h + 1, 1)]) for h in range(2)]
    drone = np.zeros((P, P + 1), f4)
    drone[0:16, 0:P] = np.concatenate([w["L0_gnn_drone_W"].T] * 2, 1)
    drone[0:16, P] = w["L0_gnn_drone_feat"][0]
    prep = np.concatenate(wh + at_s + at_d1 + at_d2 + out_ab + [drone], 1)
    ub = w["L1_gnn_W_bond"].reshape(BONDF, XF, XF).transpose(2, 1, 0).reshape(XF, XF * BONDF)
    vbm = w["L1_gnn_b_bond"].reshape(XF, XF).T
    bondw = np.concatenate([diag(ub, 4), diag(vbm, 4)], 1)

    def padded(a, n, value):
        return np.concatenate([a, np.full((n - len(a),) + a.shape[1:], value, a.dtype)])

    sel = np.concatenate([diag(np.ones((1, 64), f4), 16), diag(np.ones((1, 32), f4), 16)], 1)
    arrays = {
        "x_in": padded(w["x"], NP, 0), "src_in": padded(w["src"], EP, N_NODES),
        "dst_in": padded(w["dst"], EP, N_NODES), "attr_in": padded(w["edge_attr_16"], EP, 0),
        "consts_in": consts, "weights_in": weights, "prep_in": prep, "bondw_in": bondw, "sel_in": sel,
    }
    arrays = {n: np.ascontiguousarray(a) for n, a in arrays.items()}
    nc = _bacc.Bacc("TRN2", target_bir_lowering=False, num_devices=1)
    args = [nc.dram_tensor(n, a.shape, mybir.dt.from_np(a.dtype), kind="ExternalInput").ap()
            for n, a in arrays.items()]
    out = nc.dram_tensor("out_0", (NROWS, XF), F32, kind="ExternalOutput").ap()
    build(nc, *args, out)
    r = _run(nc, [arrays], core_ids=[0])
    return r.results[0]["out_0"][0:N_NODES]
```

```python
import numpy as np
import concourse.bass as bass
from concourse import mybir
from contextlib import ExitStack

F32 = mybir.dt.float32
I32 = mybir.dt.int32
ALU = mybir.AluOpType
ACT = mybir.ActivationFunctionType
AX = mybir.AxisListType

P = 128
N_NODES, N_EDGES = 100000, 25000
XF, HF, HEADS, BONDF, STEPS = 32, 64, 4, 16, 4
T = -(-N_EDGES // P)
EP = P * T
DB = -(-N_NODES // (16 * P))
NP = DB * 16 * P
NROWS = NP + EP
BT = 28
EB = T // BT
QB = BT // 4
PAY = 2 + BONDF
DIGIT = 6
BINS = [1 << DIGIT, 1 << DIGIT, (N_NODES >> 2 * DIGIT) + 1]
SENTINEL = 1 << 20
EPS = 1e-5
BIG = 1e30
PARTS = [(0, 512), (512, 384)]
UNITS = [(0, 2), (2, 2), (4, 2), (6, 1)]
ALL = 16 * T

K_ID, K_C64, K_C32, K_LT = (i * P for i in range(4))
K_J2, K_J4 = 4 * P, 4 * P + 2
K_IOTA = 4 * P + 6
K_EDGE = K_IOTA + 512
K_JUNK = K_EDGE + T
K_END = K_JUNK + T
W_H0A, W_H0B = 0, P
W_XW = [2 * P, 2 * P + 512]
W_IH = W_XW[1] + 512
W_HH = W_IH + 3 * P
W_COL = W_HH + 3 * P
(C_NODEB, C_DRONEB, C_OUTB, C_BIHR, C_BIHZ, C_BIHN, C_BHHR, C_BHHZ, C_BHHN) = range(9)
C_CONVB, C_G, C_B = [9, 12], [10, 13], [11, 14]
N_COL = 15
W_END = W_COL + N_COL
V_WH = [0, 4 * P]
V_AS, V_AD1, V_AD2 = [8 * P, 8 * P + 96], [8 * P + 192, 8 * P + 288], [8 * P + 384, 8 * P + 480]
V_OA = 8 * P + 576
V_OB = V_OA + P
V_DW = V_OB + P
V_DF = V_DW + P
V_END = V_DF + 1
D_WC = [0, P]
D_OA, D_OB = 2 * P, 3 * P
D_RS, D_RD = [4 * P, 4 * P + 24], [4 * P + 48, 4 * P + 72]
D_C0 = 4 * P + 96
D_BC = [D_C0 + 1, D_C0 + 2]
D_OBC, D_EPS, D_BR, D_BZ, D_NBZ = D_C0 + 3, D_C0 + 4, D_C0 + 5, D_C0 + 6, D_C0 + 7
D_END = D_C0 + 8


def build(nc, x, src, dst, attr, consts, weights, prep, bondw, sel, out):
    ctx = ExitStack()
    with ctx:
        def sem(name):
            return ctx.enter_context(nc.semaphore(name))

        def dram(name, shape, dt):
            return nc.dram_tensor(name, shape, dt, kind="Internal").ap()

        tmp_d = dram("tmp_d", (EP, 2), I32)
        sort_d = dram("sort_d", (EP + 2, 2), I32)
        tmp_s = dram("tmp_s", (EP, PAY), F32)
        sort_s = dram("sort_s", (EP + 2, PAY), F32)
        h1_tab = dram("h1_tab", (NROWS, HF), F32)
        x1_tab = dram("x1_tab", (NROWS, XF), F32)
        pos_tab = dram("pos_tab", (NROWS, 1), I32)
        agg_tab = dram("agg_tab", (EP + P, XF), F32)
        ht_dram = [dram(f"ht_dram{l}", (EB, P, QB * 512), F32) for l in range(2)]
        h1d_dram = dram("h1d_dram", (EB, P, QB * 256), F32)
        xs_dram = dram("xs_dram", (P, T * XF), F32)
        xt_dram = dram("xt_dram", (EB, P, QB * 256), F32)

        def sb(name, words):
            return ctx.enter_context(nc.sbuf_tensor(name, [P, words], F32))

        kc = sb("kc", K_END)
        wt = sb("wt", W_END)
        dv = sb("dv", D_END)
        r1 = sb("r1", T * HF)
        r2 = sb("r2", T * HF)
        r3 = sb("r3", 2 * QB * 512)
        stage = sb("stage", 2 * BT * HF)
        l12 = sb("l12", 12 * T)
        alpha = sb("alpha", 2 * T * HEADS)
        nst = sb("nst", PAY * T)
        small = sb("small", 23 * T + 5 * P + 300)
        ps = ctx.enter_context(nc.psum_tensor("ps", [P, 8, 512], F32))

        def k(c, n=P):
            return kc[:, c:c + n]

        ident = k(K_ID)

        def col(c):
            return wt[:, W_COL + c:W_COL + c + 1]

        def dcol(c):
            return dv[:, c:c + 1]

        at = [0]

        def carve(n):
            at[0] += n
            return small[:, at[0] - n:at[0]]

        ns_f, nl_f, pm, sm, last, ns_neg, nl_neg, pm_neg, sm_neg = (carve(T) for _ in range(9))
        ns_fs, pm_s = carve(T), carve(T)
        put_d, put_s, pos_val, pos_of = (carve(T).bitcast(I32) for _ in range(4))
        kid_d = carve(2 * T).bitcast(I32).rearrange("p (t c) -> p t c", c=2)
        kid_s = carve(2 * T).bitcast(I32).rearrange("p (t c) -> p t c", c=2)
        rank_i = [carve(T).bitcast(I32) for _ in range(4)]
        row_f, row_r, row_fn, row_rn, row_fs = (carve(P) for _ in range(5))
        edge_d, edge_s = carve(4).bitcast(I32), carve(4).bitcast(I32)
        end_c, carry, lanes = carve(64), carve(64), carve(130)

        phase_ended, phase_begins = sem("phase_ended"), sem("phase_begins")
        ends = {"sp": 0, "pe": 0, "act": 0, "dve": 0}

        def barrier(eng, who, clear=()):
            ends[who] += 1
            eng.drain().then_inc(phase_ended, 1)
            if who == "sp":
                eng.wait_ge(phase_ended, 4 * ends[who])
                for s in clear:
                    eng.sem_clear(s)
                eng.sem_inc(phase_begins, 1)
            else:
                eng.wait_ge(phase_begins, ends[who])

        def phase_sems(phase, names):
            return [nc.alloc_semaphore(name=f"{phase}_{n}") for n in names.split()]

        def phase_over(sems):
            for s in sems:
                nc.release_semaphore(s)

        def loop(eng, n, body):
            with eng.Fori(0, n // 2) as i:
                body(2 * i, i, 0)
                body(2 * i + 1, i, 1)
            body(n - 1, n // 2, 0)

        ld = sem("ld")
        ld_keys, ld_pay, ld_tmp_d, ld_tmp_s = sem("ld_keys"), sem("ld_pay"), sem("ld_tmp_d"), sem("ld_tmp_s")
        init_dram = sem("init_dram")
        rank_ready = sem("rank_ready")
        put_tmp_d, put_tmp_s, put_sort_d, put_sort_s = (sem(f"put_{n}") for n in
                                                         ("tmp_d", "tmp_s", "sort_d", "sort_s"))
        ld_kid_d, ld_kid_s, put_pos, got_pos = (sem(n) for n in ("ld_kid_d", "ld_kid_s", "put_pos", "got_pos"))
        got_even, got_odd = sem("got_even"), sem("got_odd")
        x_in, h1_in, agg_in = sem("x_in"), sem("h1_in"), sem("agg_in")
        flags_ready = sem("flags_ready")
        dense_done = sem("dense_done")
        rows_ready = sem("rows_ready")
        put_h1, put_x1, got_x1 = (sem(n) for n in ("put_h1", "put_x1", "got_x1"))
        out_done = sem("out_done")
        agg_stored, put_out = sem("agg_stored"), sem("put_out")
        prep_pe, prep_dve = sem("prep_pe"), sem("prep_dve")
        sentinel_ready = sem("sentinel_ready")
        fl, fl_pe = sem("fl"), sem("fl_pe")
        tl_d, tl_p = sem("tl_d"), sem("tl_p")
        sx, sx_act = sem("sx"), sem("sx_act")
        sc = sem("sc")

        pw = r1[:, 0:V_END]
        dsel = l12[0:16, 0:1536]
        fill = alpha[:, 0:128]
        pos_fill = alpha[:, 128:128 + NP // P].bitcast(I32)

        def prep_sp(sp):
            sp.dma_start(kc[:], consts).then_inc(ld, 16)
            sp.dma_start(wt[:], weights).then_inc(ld, 16)
            sp.dma_start(pw, prep).then_inc(ld, 16)
            sp.dma_start(dsel, sel).then_inc(ld, 16)
            sp.dma_start(src_t, src.rearrange("(p t) -> p t", t=T)).then_inc(ld_keys, 16)
            sp.dma_start(dst_t, dst.rearrange("(p t) -> p t", t=T)).then_inc(ld_keys, 16)
            sp.dma_start(pay_s[:, :, 2:PAY], attr.rearrange("(p t) c -> p t c", t=T)).then_inc(ld_pay, 16)
            sp.wait_ge(sentinel_ready, 3)
            for r in (0, EP + 1):
                sp.dma_start(sort_d[r:r + 1, :], fill[0:1, 0:2].bitcast(I32)).then_inc(init_dram, 16)
                sp.dma_start(sort_s[r:r + 1, :], fill[0:1, 0:PAY]).then_inc(init_dram, 16)
            sp.dma_start(pos_tab[0:NP, :].rearrange("(p n) c -> p (n c)", p=P), pos_fill).then_inc(init_dram, 16)
            sp.dma_start(agg_tab[EP:EP + P, :], fill[:, 64:64 + XF]).then_inc(init_dram, 16)
            sp.wait_ge(init_dram, 16 * 6)

        def prep_dve_(dve):
            v = nc.vector
            v.memset(fill[:, 0:64].bitcast(I32), SENTINEL).then_inc(sentinel_ready, 1)
            v.memset(fill[:, 64:128], 0.0).then_inc(sentinel_ready, 1)
            v.memset(pos_fill, EP).then_inc(sentinel_ready, 1)
            v.memset(dcol(D_EPS), EPS)
            dve.wait_ge(ld, 64)
            dve.wait_ge(prep_pe, 1)
            v.tensor_tensor(dcol(D_C0), ps[:, 0, 0:1], col(C_NODEB), ALU.add).then_inc(prep_dve, 1)
            dve.wait_ge(prep_dve, 1)
            v.tensor_tensor(dcol(D_C0), dcol(D_C0), col(C_DRONEB), ALU.add)
            for l in range(2):
                v.tensor_single_scalar(dv[:, D_WC[l]:D_WC[l] + P], ps[:, 1 + l, 0:P], 1.0 / HEADS, ALU.mult)
                v.tensor_copy(dv[:, D_RS[l]:D_RS[l] + 24], ps[:, 1 + l, 128:152])
                v.tensor_copy(dv[:, D_RD[l]:D_RD[l] + 24], ps[:, 1 + l, 152:176])
                v.tensor_copy(dcol(D_BC[l]), ps[:, 1 + l, 176:177])
            v.tensor_copy(dv[:, D_OA:D_OA + 2 * P], ps[:, 3, 0:2 * P])
            v.tensor_copy(dcol(D_OBC), ps[:, 3, 256:257])
            v.tensor_tensor(dcol(D_BR), col(C_BIHR), col(C_BHHR), ALU.add)
            v.tensor_tensor(dcol(D_BZ), col(C_BIHZ), col(C_BHHZ), ALU.add).then_inc(prep_dve, 1)
            dve.wait_ge(prep_dve, 2)
            v.tensor_single_scalar(dcol(D_NBZ), dcol(D_BZ), -1.0, ALU.mult)

        def prep_pe_(pe):
            mm = nc.tensor.matmul
            pe.wait_ge(ld, 64)
            mm(ps[:, 0, 0:1], pw[:, V_DW:V_DW + P], pw[:, V_DF:V_DF + 1], start=True, stop=True)
            for l in range(2):
                wh = [pw[:, V_WH[l] + h * P:V_WH[l] + (h + 1) * P] for h in range(HEADS)]
                for h in range(HEADS):
                    mm(ps[:, 1 + l, 0:P], wh[h], k(K_C64), start=h == 0, stop=h == HEADS - 1)
                for h in range(HEADS):
                    mm(ps[:, 1 + l, 128:152], wh[h], pw[:, V_AS[l] + 24 * h:V_AS[l] + 24 * h + 24],
                       start=h == 0, stop=h == HEADS - 1)
                for h in range(HEADS):
                    mm(ps[:, 1 + l, 152:176], wh[h], pw[:, V_AD1[l] + 24 * h:V_AD1[l] + 24 * h + 24],
                       start=h == 0, stop=False)
                    mm(ps[:, 1 + l, 152:176], wh[h], pw[:, V_AD2[l] + 24 * h:V_AD2[l] + 24 * h + 24],
                       start=False, stop=h == HEADS - 1)
                mm(ps[:, 1 + l, 176:177], k(K_C64), col(C_CONVB[l]), start=True, stop=True)
            mm(ps[:, 3, 0:P], pw[:, V_OA:V_OA + P], k(K_C32), start=True, stop=True)
            mm(ps[:, 3, P:2 * P], pw[:, V_OB:V_OB + P], k(K_C32), start=True, stop=True)
            mm(ps[:, 3, 256:257], k(K_C32), col(C_OUTB), start=True, stop=True).then_inc(prep_pe, 1)

        src_t, dst_t = r3[:, 0:T].bitcast(I32), r3[:, T:2 * T].bitcast(I32)
        pay_d = r3[:, 2 * T:4 * T].bitcast(I32).rearrange("p (t c) -> p t c", c=2)
        pay_s = nst[:].rearrange("p (t c) -> p t c", c=PAY)
        pay_si = nst[:].bitcast(I32).rearrange("p (t c) -> p t c", c=PAY)
        digit_i, digit, rank = (r3[:, (4 + i) * T:(5 + i) * T] for i in range(3))
        digit_i = digit_i.bitcast(I32)
        hist, start, junk, ones_b = (r3[:, 8 * T + 512 * i:8 * T + 512 * (i + 1)] for i in range(4))
        s_hist, s_pref, s_pref_used, s_dv = sem("s_hist"), sem("s_pref"), sem("s_pref_used"), sem("s_dv")
        PASSES = 2 * len(BINS)
        TURN, SLOTS = 2, 14
        SPREAD = ((6, 1), (3, 1), (2, 1))
        PAIR_E, SLOT_E = T // TURN, T // TURN // SLOTS
        n_dv = [0]

        def chain_dv(dve, ins):
            ins.then_inc(s_dv, 1)
            n_dv[0] += 1
            dve.wait_ge(s_dv, n_dv[0])

        def sort_start(dve):
            v = nc.vector
            v.memset(ones_b[:], 1.0)
            dve.wait_ge(ld_keys, 32)
            v.tensor_copy(pay_d[:, :, 0], src_t)
            v.tensor_copy(pay_d[:, :, 1], dst_t)
            v.tensor_copy(pay_si[:, :, 0], src_t)
            v.tensor_copy(pay_si[:, :, 1], dst_t)

        def sort_digits(dve, i):
            v, level, of_src = nc.vector, i // 2, i % 2
            key = (dst_t, src_t)[of_src] if level == 0 else (pay_d[:, :, 1], pay_si[:, :, 0])[of_src]
            if level:
                dve.wait_ge((ld_tmp_d, ld_tmp_s)[of_src], 16 * level)
                chain_dv(dve, v.tensor_single_scalar(digit_i, key, DIGIT * level, ALU.logical_shift_right))
                key = digit_i
            if level < 2:
                chain_dv(dve, v.tensor_single_scalar(digit_i, key, (1 << DIGIT) - 1, ALU.bitwise_and))
            v.tensor_copy(digit, digit_i)
            chain_dv(dve, v.memset(hist[:, 0:BINS[level]], 0.0))

        def sort_count(dve, i, base, pair, slot):
            v, bins = nc.vector, BINS[i // 2]
            for u in range(SLOT_E):
                e = pair * PAIR_E + (slot * SLOT_E + u - 2 * TURN * i * PAIR_E)
                v.scalar_tensor_tensor(out=hist[:, 0:bins], in0=k(K_IOTA, bins), scalar=digit[:, bass.ds(e, 1)],
                                       in1=hist[:, 0:bins], op0=ALU.is_equal, op1=ALU.add).then_inc(s_dv, 1)
                dve.wait_ge(s_dv, e + (base + 1))

        def sort_starts(dve, i):
            v, bins = nc.vector, BINS[i // 2]
            v.tensor_copy(start[:, 0:bins], hist[:, 0:bins]).then_inc(s_hist, 1)
            dve.wait_ge(s_pref, i + 1)
            chain_dv(dve, v.tensor_tensor_scan(junk[:, 0:bins], ones_b[:, 0:bins], ps[:, 5, 0:bins], 0.0,
                                               ALU.mult, ALU.add))
            chain_dv(dve, v.tensor_tensor(junk[:, 0:bins], junk[:, 0:bins], ps[:, 5, 0:bins], ALU.subtract))
            chain_dv(dve, v.tensor_tensor(start[:, 0:bins], junk[:, 0:bins], ps[:, 4, 0:bins], ALU.add))
            dve.sem_inc(s_pref_used, 1)

        def sort_rank(dve, i, base, pair, slot):
            v, bins = nc.vector, BINS[i // 2]
            for u in range(SLOT_E):
                e = pair * PAIR_E + (slot * SLOT_E + u - (2 * i + 1) * TURN * PAIR_E)
                d = digit[:, bass.ds(e, 1)]
                v.scalar_tensor_tensor(out=junk[:, 0:bins], in0=k(K_IOTA, bins), scalar=d,
                                       in1=start[:, 0:bins], op0=ALU.is_equal, op1=ALU.mult,
                                       accum_out=rank[:, bass.ds(e, 1)]).then_inc(s_dv, 1)
                dve.wait_ge(s_dv, e * 2 + (base + 1))
                v.scalar_tensor_tensor(out=start[:, 0:bins], in0=k(K_IOTA, bins), scalar=d,
                                       in1=start[:, 0:bins], op0=ALU.is_equal,
                                       op1=ALU.add).then_inc(s_dv, 1)
                dve.wait_ge(s_dv, e * 2 + (base + 2))

        def sort_dve(dve):
            sort_start(dve)
            for i in range(PASSES):
                b0, b1, b2 = (2 * TURN * (2 * i + j) for j in range(3))
                sort_digits(dve, i)
                base = n_dv[0]
                dense_dve(dve, b0, b1, lambda pair, slot: sort_count(dve, i, base, pair, slot))
                n_dv[0] += T
                sort_starts(dve, i)
                base = n_dv[0]
                dense_dve(dve, b1, b2, lambda pair, slot: sort_rank(dve, i, base, pair, slot))
                n_dv[0] += 2 * T
                nc.vector.tensor_single_scalar(rank_i[i % 4], rank, float(i // 2 == 2), ALU.add)\
                    .then_inc(rank_ready, 1)
            dense_dve(dve, 4 * TURN * PASSES, DB)

        def sort_pe(pe):
            mm = nc.tensor.matmul
            for i in range(PASSES):
                b0, b1, b2 = (2 * TURN * (2 * i + j) for j in range(3))
                bins = BINS[i // 2]
                dense_pe(pe, b0, b1)
                pe.wait_ge(s_hist, i + 1)
                pe.wait_ge(dn_xe, b1 + 2)
                mm(ps[:, 4, 0:bins], k(K_LT), start[:, 0:bins], start=True, stop=True)
                mm(ps[:, 5, 0:bins], ones_b[:, 0:P], start[:, 0:bins], start=True, stop=True).then_inc(s_pref, 1)
                pe.wait_ge(s_pref_used, i + 1)
                dense_pe(pe, b1, b2)
            dense_pe(pe, 4 * TURN * PASSES, DB)

        dense_sems = phase_sems("dn", "x0 x1 tr xt hm h z zc sq v sd rs rt re r tn rl hn t1 t1e free xtr xe st")
        dn = dense_sems[0:2]
        (dn_tr, dn_xt, dn_hm, dn_h, dn_z, dn_zc, dn_sq, dn_v, dn_sd, dn_rs, dn_rt, dn_re, dn_r, dn_tn, dn_rl,
         dn_hn, dn_t1, dn_t1e, dn_free, dn_xtr, dn_xe, dn_st) = dense_sems[2:]
        phase_over(dense_sems)
        off = [0]

        def lay(region, n):
            off[0] += n
            return region[:, off[0] - n:off[0]]

        xr, xt_b = [lay(r2, 512) for _ in range(2)], [lay(r2, 512) for _ in range(2)]
        hb, h1b, zc, sq, tn = ([lay(r2, 1024) for _ in range(2)] for _ in range(5))
        h1o = [stage[:, s * 1024:(s + 1) * 1024] for s in range(2)]
        x1o = [stage[:, 2048 + s * 512:2560 + s * 512] for s in range(2)]
        rst = [stage[:, 3072 + s * 16:3088 + s * 16] for s in range(2)]
        rtt = [stage[0:16, 3104 + s * P:3104 + (s + 1) * P] for s in range(2)]
        x_blk = x.rearrange("(b p n) f -> b p (n f)", p=P, n=16)
        h1_blk = h1_tab[0:NP, :].rearrange("(b p n) f -> b p (n f)", p=P, n=16)
        x1_blk = x1_tab[0:NP, :].rearrange("(b p n) f -> b p (n f)", p=P, n=16)
        out_blk = out[0:NP, :].rearrange("(b p n) f -> b p (n f)", p=P, n=16)

        def blk(ap, b):
            return ap[bass.ds(b, 1)].rearrange("o p f -> (o p) f")

        def pairs(eng, first, n, body):
            if n - first > 1:
                with eng.Fori(first // 2, n // 2) as i:
                    body(2 * i, i, 2)
            if n % 2:
                body(n - 1, n // 2, 1)

        def two(s, lo):
            return ps[:, 4 * s + 2 * lo:4 * s + 2 * lo + 2, :]

        def wide(ap):
            return ap.rearrange("p (k c) -> p k c", k=2)

        def dense_sp(sp, first, n):
            def load(b, s):
                sp.dma_start(xr[s], blk(x_blk, b)).then_inc(dn[s], 16)

            def store(b, s):
                sp.wait_ge(dn_t1e, b + s + 3)
                sp.dma_start(blk(h1_blk, b + s), h1o[s]).then_inc(dn_st, 16)
                sp.wait_ge(dn_xe, b + s + 3)
                sp.dma_start(blk(x1_blk, b + s), x1o[s]).then_inc(dn_st, 16)
                sp.wait_ge(dn_st, 32 * b + 32 * s + 32)
                sp.sem_inc(dn_free, 1)

            if first == 0:
                sp.sem_inc(dn_free, 2)
            load(first, 0)
            load(first + 1, 1)
            with sp.Fori(first // 2, n // 2 - 1) as i:
                sp.wait_ge(dn_tr, 2 * i + 2)
                load(2 * i + 2, 0)
                load(2 * i + 3, 1)
                store(2 * i, 0)
                store(2 * i, 1)
            if n % 2:
                sp.wait_ge(dn_tr, n - 1)
                load(n - 1, 0)
            b = n // 2 * 2 - 2
            store(b, 0)
            store(b, 1)
            if n % 2:
                store(n - 1, 0)

        def dense_pe(pe, first, n):
            mm, tr = nc.tensor.matmul, nc.tensor.transpose

            def body(b, i, ns):
                def stats(kk, units):
                    for s in range(ns):
                        pe.wait_ge(dn_sq, 6 * i + ns * kk + s + 1)
                        for j in range(units):
                            c, w = (j % 4 * P + j // 4 * 512, 2) if units == 8 else (j * P, 4)
                            at_ = 4 * (j % 4) + 2 * (j // 4) if units == 8 else 4 * j
                            m = mm(ps[:, 4 * s + 2, at_:at_ + w], sq[s][:, c:c + P],
                                   k(K_J2 if w == 2 else K_J4, w), start=True, stop=True)
                        m.then_inc(dn_v, 1)
                    for s in range(ns):
                        pe.wait_ge(dn_rs, 6 * i + ns * kk + s + 1)
                        tr(ps[0:16, 4 * s + 2, P:2 * P], rst[s], ident).then_inc(dn_rt, 1)
                    for s in range(ns):
                        pe.wait_ge(dn_re, 6 * i + ns * kk + s + 1)
                        for j in range(units):
                            if units == 8:
                                w0 = (4 * (j % 4) + 2 * (j // 4)) * 64
                                o = ps[:, 4 * s + 2 + j // 4, j % 4 * P:(j % 4 + 1) * P]
                            else:
                                w0 = 1024 + j * P
                                o = ps[:, 4 * s + 3, j * P:(j + 1) * P]
                            m = mm(o, dsel[:, w0:w0 + P], rtt[s], start=True, stop=True)
                        m.then_inc(dn_r, 1)

                for s in range(ns):
                    pe.wait_ge(dn[s], 16 * i + 16)
                    pe.wait_ge(dn_xe, b + s + 1)
                    for j in range(4):
                        t = tr(ps[:, 4 * s, j * P:(j + 1) * P], xr[s][:, j * P:(j + 1) * P], ident)
                    t.then_inc(dn_tr, 1)
                for s in range(ns):
                    pe.wait_ge(dn_xt, b + s + 1)
                    for h in range(2):
                        m = mm(ps[:, 4 * s + 2 + h, :], wt[:, (W_H0A, W_H0B)[h]:(W_H0A, W_H0B)[h] + P],
                               xt_b[s], start=True, stop=True)
                    m.then_inc(dn_hm, 1)
                for l in range(2):
                    for s in range(ns):
                        if l == 0:
                            pe.wait_ge(dn_h, b + s + 1)
                        else:
                            pe.wait_ge(dn_hn, 4 * i + s + 1)
                        for h in range(2):
                            m = mm(ps[:, 4 * s + h, :], dv[:, D_WC[l]:D_WC[l] + P],
                                   (hb, h1b)[l][s][:, h * 512:(h + 1) * 512], start=True, stop=True)
                        m.then_inc(dn_z, 1)
                    if l == 1:
                        for s in range(ns):
                            for j in range(8):
                                t = tr(ps[:, 4 * s + 2 + j // 4, j % 4 * P:(j % 4 + 1) * P],
                                       h1b[s][:, j * P:(j + 1) * P], ident)
                            t.then_inc(dn_t1, 1)
                        for s in range(ns):
                            pe.wait_ge(dn_t1e, b + s + 3)
                    stats(l, 8)
                for s in range(ns):
                    pe.wait_ge(dn_hn, 4 * i + ns + s + 1)
                    mm(ps[:, 4 * s, :], k(K_C32), xt_b[s], start=True, stop=False)
                    mm(ps[:, 4 * s, :], dv[:, D_OA:D_OA + P], hb[s][:, 0:512], start=False, stop=False)
                    mm(ps[:, 4 * s, :], dv[:, D_OB:D_OB + P], hb[s][:, 512:1024], start=False,
                       stop=True).then_inc(dn_z, 1)
                stats(2, 4)
                for s in range(ns):
                    pe.wait_ge(dn_tn, 6 * i + 2 * ns + s + 1)
                    for j in range(4):
                        t = tr(ps[:, 4 * s + 1, j * P:(j + 1) * P], tn[s][:, j * P:(j + 1) * P], ident)
                    t.then_inc(dn_xtr, 1)

            pairs(pe, first, n, body)

        def dense_act(act, first, n):
            a = nc.scalar.activation

            def body(b, i, ns):
                def stats(kk):
                    for s in range(ns):
                        act.wait_ge(dn_v, 6 * i + ns * kk + s + 1)
                        a(rst[s], ps[:, 4 * s + 2, 0:16], ACT.Sqrt, bias=dcol(D_EPS)).then_inc(dn_sd, 1)
                    for s in range(ns):
                        act.wait_ge(dn_rt, 6 * i + ns * kk + s + 1)
                        a(rtt[s], ps[0:16, 4 * s + 2, P:2 * P], ACT.Identity).then_inc(dn_re, 1)

                for s in range(ns):
                    act.wait_ge(dn_tr, b + s + 1)
                    a(xt_b[s], ps[:, 4 * s, :], ACT.Identity).then_inc(dn_xt, 1)
                for s in range(ns):
                    act.wait_ge(dn_hm, b + s + 1)
                    a(wide(hb[s]), two(s, 1), ACT.Identity, bias=dcol(D_C0)).then_inc(dn_h, 1)
                for l in range(2):
                    for s in range(ns):
                        act.wait_ge(dn_z, 6 * i + ns * l + s + 1)
                        a(wide(sq[s]), two(s, 0), ACT.Square, bias=dcol(D_BC[l])).then_inc(dn_sq, 1)
                    for s in range(ns if l == 1 else 0):
                        act.wait_ge(dn_free, b + s + 1)
                        act.wait_ge(dn_t1, b + s + 1)
                        a(h1o[s].rearrange("p (j h c) -> p h j c", j=4, h=2),
                          two(s, 1).rearrange("p h (j c) -> p h j c", j=4), ACT.Identity).then_inc(dn_t1e, 1)
                    for s in range(ns):
                        a(wide(zc[s]), two(s, 0), ACT.Identity, bias=dcol(D_BC[l])).then_inc(dn_zc, 1)
                    stats(l)
                    for s in range(ns):
                        act.wait_ge(dn_tn, 6 * i + ns * l + s + 1)
                        a(tn[s], tn[s], ACT.Relu, bias=col(C_B[l]), scale=col(C_G[l])).then_inc(dn_rl, 1)
                for s in range(ns):
                    act.wait_ge(dn_z, 6 * i + ns * 2 + s + 1)
                    a(sq[s][:, 0:512], ps[:, 4 * s, :], ACT.Square, bias=dcol(D_OBC)).then_inc(dn_sq, 1)
                    a(zc[s][:, 0:512], ps[:, 4 * s, :], ACT.Identity, bias=dcol(D_OBC)).then_inc(dn_zc, 1)
                stats(2)
                for s in range(ns):
                    act.wait_ge(dn_xtr, b + s + 1)
                    a(x1o[s], ps[:, 4 * s + 1, :], ACT.Identity).then_inc(dn_xe, 1)

            act.sem_inc(dn_t1e, 2)
            act.sem_inc(dn_xe, 2)
            pairs(act, first, n, body)

        def dense_dve(dve, first, n, between=None):
            v = nc.vector

            def body(b, i, ns):
                slot = [0]

                def meanwhile(slots):
                    for _ in range(slots if between and ns == 2 else 0):
                        between(i, slot[0])
                        slot[0] += 1

                def norm(kk, slots):
                    meanwhile(slots[0])
                    for s in range(ns):
                        dve.wait_ge(dn_sd, 6 * i + ns * kk + s + 1)
                        v.reciprocal(rst[s], rst[s]).then_inc(dn_rs, 1)
                    meanwhile(slots[1])
                    for s in range(ns):
                        dve.wait_ge(dn_r, 6 * i + ns * kk + s + 1)
                        dve.wait_ge(dn_zc, 6 * i + ns * kk + s + 1)
                        if kk < 2:
                            v.tensor_tensor(wide(tn[s]), wide(zc[s]), two(s, 1), ALU.mult).then_inc(dn_tn, 1)
                        else:
                            v.tensor_tensor(tn[s][:, 0:512], zc[s][:, 0:512], ps[:, 4 * s + 3, :],
                                            ALU.mult).then_inc(dn_tn, 1)

                for l in range(2):
                    norm(l, SPREAD[l])
                    for s in range(ns):
                        dve.wait_ge(dn_rl, 4 * i + ns * l + s + 1)
                        v.tensor_tensor((h1b, hb)[l][s], (hb, h1b)[l][s], tn[s], ALU.add).then_inc(dn_hn, 1)
                norm(2, SPREAD[2])

            pairs(dve, first, n, body)

        kx = r2[:, 7000:7000 + T + 2]
        kt = r2[:, 7256:7256 + T]
        border = [r2[:, 7512 + P * i:7640 + P * i] for i in range(3)]
        nfl = [0]

        def flags_dve(dve, order):
            v = nc.vector

            def chain(ins):
                ins.then_inc(fl, 1)
                nfl[0] += 1
                dve.wait_ge(fl, nfl[0])

            dve.wait_ge((ld_kid_d, ld_kid_s)[order], 48)
            if order == 1:
                chain(v.tensor_copy(kid_s, pay_si[:, :, 0:2]))
            key = (kid_d[:, :, 1], kid_s[:, :, 0])[order]
            edge = (edge_d, edge_s)[order]
            nsf, pmx = ((ns_f, pm), (ns_fs, pm_s))[order]
            put = (put_d, put_s)[order]
            v.tensor_copy(kx[:, 0:1], edge[:, 1 - order:2 - order])
            v.tensor_copy(kx[:, T + 1:T + 2], edge[:, 3 - order:4 - order])
            chain(v.tensor_copy(kx[:, 1:T + 1], key))
            chain(v.tensor_tensor(nsf, kx[:, 1:T + 1], kx[:, 0:T], ALU.is_equal))
            chain(v.tensor_tensor_scan(pmx, nsf, nsf, 1.0, ALU.mult, ALU.min))
            chain(v.memset(nsf[:, 0:1], 0.0))
            chain(v.tensor_tensor(kt, kx[:, 1:T + 1], kx[:, 2:T + 2], ALU.is_equal))
            if order == 0:
                chain(v.tensor_tensor_scan(sm[:, ::-1], kt[:, ::-1], kt[:, ::-1], 1.0, ALU.mult, ALU.min))
                chain(v.tensor_copy(nl_f, kt))
                chain(v.memset(nl_f[:, T - 1:T], 0.0))
            chain(v.tensor_scalar(kt, kt, -1.0, 1.0, ALU.mult, ALU.add))
            if order == 0:
                chain(v.tensor_copy(last, kt))
                for a, b in ((ns_neg, ns_f), (nl_neg, nl_f), (pm_neg, pm), (sm_neg, sm)):
                    chain(v.tensor_scalar(a, b, 1.0, BIG, ALU.subtract, ALU.mult))
            chain(v.tensor_tensor(kx[:, 1:T + 1], kx[:, 1:T + 1], k(K_JUNK, T), ALU.subtract))
            chain(v.tensor_tensor(kx[:, 1:T + 1], kx[:, 1:T + 1], kt, ALU.mult))
            chain(v.tensor_tensor(put, kx[:, 1:T + 1], k(K_JUNK, T), ALU.add))
            if order == 0:
                chain(v.tensor_single_scalar(border[0], ident, pm[:, T - 1:T], ALU.mult))
                chain(v.tensor_single_scalar(border[1], ident, sm[:, 0:1], ALU.mult))
            else:
                chain(v.tensor_copy(pos_val, k(K_EDGE, T)))
                chain(v.tensor_single_scalar(border[2], ident, pm_s[:, T - 1:T], ALU.mult))
            v.memset(lanes[:], 1.0).then_inc(flags_ready, 1)
            dve.wait_ge(fl_pe, order + 1)
            for i, row in ((0, row_f), (1, row_r)) if order == 0 else ((2, row_fs),):
                chain(v.tensor_copy(row[0:64, :], ps[0:64, 7, i * P:(i + 1) * P]))
            if order == 0:
                chain(v.tensor_scalar(row_fn[0:64, :], row_f[0:64, :], 1.0, BIG, ALU.subtract, ALU.mult))
                chain(v.tensor_scalar(row_rn[0:64, :], row_r[0:64, :], 1.0, BIG, ALU.subtract, ALU.mult))

        def flags_pe(pe, order):
            pe.wait_ge(flags_ready, order + 1)
            for i in ((0, 1), (2,))[order]:
                m = nc.tensor.matmul(ps[0:64, 7, i * P:(i + 1) * P], lanes[:, 0:64], border[i],
                                     start=True, stop=True)
            m.then_inc(fl_pe, 1)

        ntl = {"d": 0, "p": 0, "pe_d": 0, "pe_p": 0}

        def carry_dve(dve, ends, kk, row, op0, op1, first, reverse=False):
            v = nc.vector

            def chain(ins):
                ins.then_inc(tl_d, 1)
                ntl["d"] += 1

            chain(v.tensor_copy(end_c[:, 0:kk], ends))
            ntl["p"] += 1
            dve.wait_ge(tl_p, ntl["p"])
            if reverse:
                v.memset(lanes[0:kk, P:P + 1], first)
                chain(v.tensor_tensor_scan(lanes[0:kk, 0:P][:, ::-1], row[0:kk, :][:, ::-1],
                                           ps[0:kk, 6, 0:P][:, ::-1], first, op0, op1))
            else:
                v.memset(lanes[0:kk, 0:1], first)
                chain(v.tensor_tensor_scan(lanes[0:kk, 1:P + 1], row[0:kk, :], ps[0:kk, 6, 0:P], first,
                                           op0, op1))
            ntl["p"] += 1
            dve.wait_ge(tl_p, ntl["p"])
            chain(v.tensor_copy(carry[:, 0:kk], ps[:, 7, 0:kk]))
            dve.wait_ge(tl_d, ntl["d"])

        def carry_pe(pe, kk, reverse=False):
            tr = nc.tensor.transpose
            ntl["pe_d"] += 1
            pe.wait_ge(tl_d, ntl["pe_d"])
            tr(ps[0:kk, 6, 0:P], end_c[:, 0:kk], ident).then_inc(tl_p, 1)
            ntl["pe_d"] += 1
            pe.wait_ge(tl_d, ntl["pe_d"])
            tr(ps[:, 7, 0:kk], lanes[0:kk, (1 if reverse else 0):(1 if reverse else 0) + P],
               ident[0:kk, 0:kk]).then_inc(tl_p, 1)
            ntl["pe_d"] += 1

        y64 = r1[:].rearrange("p (f t) -> p f t", t=T)
        rows64 = r2[:].rearrange("p (t f) -> p t f", f=HF)
        xg = r1[:].rearrange("p (d t f) -> p d t f", d=2, f=XF)
        SB = BT * XF
        x1rows = r2[:, 0:T * XF].rearrange("p (t f) -> p t f", f=XF)
        stg = [stage[:, s * BT * HF:(s + 1) * BT * HF] for s in range(2)]
        ht = [r3[:, s * QB * 512:(s + 1) * QB * 512].rearrange("p (q h d c) -> p q h d c", q=QB, h=2, d=2)
              for s in range(2)]
        ht_flat = [r3[:, s * QB * 512:(s + 1) * QB * 512] for s in range(2)]
        xtb = [r2[:, s * QB * 256:(s + 1) * QB * 256] for s in range(2)]
        l12v = l12[:].rearrange("p (j t) -> p j t", j=12)
        alv = alpha[:].rearrange("p (d t h) -> p d t h", d=2, h=HEADS)

        def gat_logits(l):
            sems = phase_sems(f"g{l}", "in0 in1 inh0 inh1 tr xt hm ht lg l12 free st off")
            s_in, s_inh = sems[0:2], sems[2:4]
            s_tr, s_xt, s_hm, s_ht, s_lg, s_l12, s_free, s_st, s_off = sems[4:]
            phase_over(sems)
            ahead_ht = 2 * l

            def sp_(sp):
                def load(b, slot):
                    if l == 0:
                        sp.dma_start(stg[slot].rearrange("p (d c) -> p d c", d=2),
                                     r1[:].rearrange("p (d c) -> p d c", d=2)[:, :, bass.ds(b * SB, SB)])\
                            .then_inc(s_in[slot], 16)
                    else:
                        sp.dma_start(stg[slot], r2[:, bass.ds(b * (BT * HF), BT * HF)])\
                            .then_inc(s_in[slot], 16)
                        sp.dma_start(ht[slot][:, :, :, 1, :],
                                     blk(h1d_dram, b).rearrange("p (q h c) -> p q h c", q=QB, h=2)
                                     ).then_inc(s_inh[slot], 16)

                def body(b, half, slot, ahead=True):
                    if ahead:
                        sp.wait_ge(s_l12, b + 1)
                        sp.sem_inc(s_off, 1)
                        sp.wait_ge((x_in, h1_in)[l], b + 2)
                        load(b + 1, 1 - slot)
                    sp.wait_ge(s_ht, QB * b + QB + ahead_ht)
                    sp.dma_start(blk(ht_dram[l], b), ht_flat[slot]).then_inc(s_st, 16)
                    if l == 0:
                        sp.dma_start(blk(xt_dram, b), xtb[slot]).then_inc(s_st, 16)
                    sp.wait_ge(s_st, (32 - 16 * l) * b + (32 - 16 * l))
                    sp.sem_inc(s_free, 1)

                sp.wait_ge((x_in, h1_in)[l], 1)
                sp.sem_inc(s_free, 2)
                load(0, 0)
                with sp.Fori(0, EB // 2) as i:
                    body(2 * i, i, 0)
                    body(2 * i + 1, i, 1)
                body(EB - 1, EB // 2, 0, ahead=False)

            def pe_(pe):
                mm, tr = nc.tensor.matmul, nc.tensor.transpose

                def body(b, half, slot):
                    pe.wait_ge(s_in[slot], 16 * half + 16)
                    if l == 1:
                        pe.wait_ge(s_inh[slot], 16 * half + 16)

                    def logits(q):
                        pe.wait_ge(s_ht, QB * b + q + 1 + ahead_ht)
                        for h in range(2):
                            o = ps[:, 4 + slot, (2 * q + h) * 24:(2 * q + h) * 24 + 24]
                            mm(o, ht[slot][:, q, h, 0, :], dv[:, D_RS[l]:D_RS[l] + 24], start=True, stop=False)
                            m = mm(o, ht[slot][:, q, h, 1, :], dv[:, D_RD[l]:D_RD[l] + 24],
                                   start=False, stop=True)
                        m.then_inc(s_lg, 1)

                    for q in range(QB):
                        pe.wait_ge((s_xt, s_ht)[l], QB * b + q + 1)
                        if l == 0:
                            tr(ps[:, q % 2, 0:P], stg[slot][:, q * P:(q + 1) * P], ident)
                            tr(ps[:, q % 2, P:2 * P], stg[slot][:, SB + q * P:SB + (q + 1) * P],
                               ident).then_inc(s_tr, 1)
                            pe.wait_ge(s_xt, QB * b + q + 3)
                            rhs = xtb[slot][:, q * 256:(q + 1) * 256]
                            mm(ps[:, 2 + q % 2, 0:256], wt[:, W_H0A:W_H0A + P], rhs, start=True, stop=True)
                            mm(ps[:, 2 + q % 2, 256:512], wt[:, W_H0B:W_H0B + P], rhs,
                               start=True, stop=True).then_inc(s_hm, 1)
                        else:
                            tr(ps[:, q % 2, 0:P], stg[slot][:, (2 * q) * P:(2 * q + 1) * P], ident)
                            tr(ps[:, q % 2, P:2 * P], stg[slot][:, (2 * q + 1) * P:(2 * q + 2) * P],
                               ident).then_inc(s_tr, 1)
                        if q:
                            logits(q - 1)
                    logits(QB - 1)

                loop(pe, EB, body)

            def act_(act):
                a = nc.scalar.activation

                def body(b, half, slot):
                    act.wait_ge(s_free, b + 1)
                    for q in range(QB):
                        act.wait_ge(s_tr, QB * b + q + 1)
                        if l == 0:
                            a(xtb[slot][:, q * 256:(q + 1) * 256], ps[:, q % 2, 0:256],
                              ACT.Identity).then_inc(s_xt, 1)
                            act.wait_ge(s_hm, QB * b + q + 1)
                            a(ht[slot][:, q].rearrange("p h d c -> p (h d c)"), ps[:, 2 + q % 2, :],
                              ACT.Identity, bias=dcol(D_C0)).then_inc(s_ht, 1)
                        else:
                            a(ht[slot][:, q, :, 0, :], ps[:, q % 2, 0:256].rearrange("p (h c) -> p h c", h=2),
                              ACT.Identity).then_inc(s_ht, 1)
                    act.wait_ge(s_lg, QB * b + QB)
                    a(l12v[:, :, bass.ds(b * BT, BT)],
                      ps[:, 4 + slot, 0:12 * BT].rearrange("p (t j) -> p j t", j=12),
                      ACT.Identity).then_inc(s_l12, 1)

                act.sem_inc((s_xt, s_ht)[l], 2)
                act.sem_inc(s_l12, 1)
                loop(act, EB, body)

            return sp_, pe_, act_, sems

        nsx = [0]
        nar = [r2[:, i * HEADS * T:(i + 1) * HEADS * T].rearrange("p (h t) -> p h t", h=HEADS) for i in range(7)]

        def softmax_dve(dve, l):
            v = nc.vector

            def chain(ins):
                ins.then_inc(sx, 1)
                nsx[0] += 1
                dve.wait_ge(sx, nsx[0])

            def scan(o, flag, val, first, op0, op1, rev=False):
                if rev:
                    return v.tensor_tensor_scan(o[:, ::-1], flag[:, ::-1], val[:, ::-1], first, op0, op1)
                return v.tensor_tensor_scan(o, flag, val, first, op0, op1)

            def bt(ap):
                return ap.unsqueeze(1).broadcast_to([P, HEADS, T])

            a_s, a_d, a_sd = (l12v[:, 4 * i:4 * i + 4, :] for i in range(3))
            e, sf, mf, mr, t0, t1, tot = nar
            if l == 1:
                for part in (a_d, a_sd):
                    for h in range(HEADS):
                        chain(v.tensor_tensor(t0[:, h, :], part[:, h, :], last, ALU.mult))
                    for h in range(HEADS):
                        chain(scan(part[:, h, :], nl_f, t0[:, h, :], 0.0, ALU.mult, ALU.add, True))
                    carry_dve(dve, part[:, :, 0], HEADS, row_r, ALU.mult, ALU.add, 0.0, reverse=True)
                    for h in range(HEADS):
                        chain(v.scalar_tensor_tensor(out=part[:, h, :], in0=sm, scalar=carry[:, h:h + 1],
                                                     in1=part[:, h, :], op0=ALU.mult, op1=ALU.add))
            chain(v.tensor_tensor(e, a_s, a_d, ALU.add))
            chain(v.scalar_tensor_tensor(out=e, in0=e, scalar=0.2, in1=e, op0=ALU.mult, op1=ALU.max))
            chain(v.scalar_tensor_tensor(out=sf, in0=a_sd, scalar=0.2, in1=a_sd, op0=ALU.mult, op1=ALU.max))
            chain(v.tensor_tensor(t0, e, sf, ALU.max))
            for h in range(HEADS):
                chain(scan(mf[:, h, :], ns_neg, t0[:, h, :], -BIG, ALU.add, ALU.max))
                chain(scan(mr[:, h, :], nl_neg, t0[:, h, :], -BIG, ALU.add, ALU.max, True))
            carry_dve(dve, mf[:, :, T - 1], HEADS, row_fn, ALU.add, ALU.max, -BIG)
            for h in range(HEADS):
                chain(v.scalar_tensor_tensor(out=mf[:, h, :], in0=pm_neg, scalar=carry[:, h:h + 1],
                                             in1=mf[:, h, :], op0=ALU.add, op1=ALU.max))
            carry_dve(dve, mr[:, :, 0], HEADS, row_rn, ALU.add, ALU.max, -BIG, reverse=True)
            for h in range(HEADS):
                chain(v.scalar_tensor_tensor(out=mr[:, h, :], in0=sm_neg, scalar=carry[:, h:h + 1],
                                             in1=mr[:, h, :], op0=ALU.add, op1=ALU.max))
            chain(v.tensor_tensor(mf, mf, mr, ALU.max))
            chain(v.tensor_tensor(t0, e, mf, ALU.subtract))
            chain(v.tensor_tensor(t1, sf, mf, ALU.subtract))
            dve.sem_inc(sx_act, 1)
            dve.wait_ge(sx_act, 3 * l + 3)
            for h in range(HEADS):
                chain(v.tensor_tensor(sf[:, h, :], t1[:, h, :], last, ALU.mult))
            chain(v.tensor_tensor(t1, e, sf, ALU.add))
            for h in range(HEADS):
                chain(scan(mf[:, h, :], ns_f, t1[:, h, :], 0.0, ALU.mult, ALU.add))
            carry_dve(dve, mf[:, :, T - 1], HEADS, row_f, ALU.mult, ALU.add, 0.0)
            for h in range(HEADS):
                chain(v.scalar_tensor_tensor(out=mf[:, h, :], in0=pm, scalar=carry[:, h:h + 1],
                                             in1=mf[:, h, :], op0=ALU.mult, op1=ALU.add))
            for h in range(HEADS):
                chain(v.tensor_tensor(mr[:, h, :], mf[:, h, :], last, ALU.mult))
            for h in range(HEADS):
                chain(scan(tot[:, h, :], nl_f, mr[:, h, :], 0.0, ALU.mult, ALU.add, True))
            carry_dve(dve, tot[:, :, 0], HEADS, row_r, ALU.mult, ALU.add, 0.0, reverse=True)
            for h in range(HEADS):
                chain(v.scalar_tensor_tensor(out=tot[:, h, :], in0=sm, scalar=carry[:, h:h + 1],
                                             in1=tot[:, h, :], op0=ALU.mult, op1=ALU.add))
            chain(v.tensor_single_scalar(tot, tot, 1e-16, ALU.add))
            chain(v.reciprocal(tot, tot))
            chain(v.tensor_single_scalar(tot, tot, 1.0 / HEADS, ALU.mult))
            chain(v.tensor_tensor(alv[:, 0].rearrange("p t h -> p h t"), e, tot, ALU.mult))
            chain(v.tensor_tensor(alv[:, 1].rearrange("p t h -> p h t"), sf, tot, ALU.mult))

        def softmax_act(act, l):
            e, sf, mf, mr, t0, t1, tot = nar
            act.wait_ge(sx_act, 3 * l + 1)
            nc.scalar.activation(e, t0, ACT.Exp).then_inc(sx_act, 1)
            nc.scalar.activation(t1, t1, ACT.Exp).then_inc(sx_act, 1)

        def softmax_pe(pe, l):
            if l == 1:
                carry_pe(pe, HEADS, reverse=True)
                carry_pe(pe, HEADS, reverse=True)
            carry_pe(pe, HEADS)
            carry_pe(pe, HEADS, reverse=True)
            carry_pe(pe, HEADS)
            carry_pe(pe, HEADS, reverse=True)

        prod = [stage[:, s * 1024:(s + 1) * 1024] for s in range(2)]
        fold = [stage[:, 2048 + s * 512:2560 + s * 512] for s in range(2)]

        def gat_values(l):
            sems = phase_sems(f"v{l}", "in0 in1 mm pr fd y")
            s_in = sems[0:2]
            s_mm, s_pr, s_fd, s_y = sems[2:]
            phase_over(sems)
            PB = 2 * QB

            def sp_(sp):
                def load(b, slot):
                    sp.dma_start(ht_flat[slot], blk(ht_dram[l], b)).then_inc(s_in[slot], 16)

                def body(b, half, slot):
                    sp.wait_ge(s_y, PB * b + 1)
                    load(b + 1, 1 - slot)

                load(0, 0)
                with sp.Fori(0, EB // 2) as i:
                    body(2 * i, i, 0)
                    body(2 * i + 1, i, 1)

            def pe_(pe):
                mm = nc.tensor.matmul

                def body(b, half, slot):
                    pe.wait_ge(s_in[slot], 16 * half + 16)
                    for j in range(PB):
                        pe.wait_ge(s_pr, PB * b + j + 1)
                        for d in range(2):
                            m = mm(ps[:, 2 * (j % 2) + d, :], ht[slot][:, j // 2, j % 2, d, :],
                                   wt[:, W_XW[l]:W_XW[l] + 512], start=True, stop=True)
                        m.then_inc(s_mm, 1)

                loop(pe, EB, body)

            def dve_(dve):
                v = nc.vector

                def finish(b, j):
                    g = j % 2
                    dve.wait_ge(s_pr, PB * b + j + 3)
                    v.tensor_tensor(fold[g], prod[g][:, 0:512], prod[g][:, 512:1024], ALU.add).then_inc(s_fd, 1)
                    dve.wait_ge(s_fd, PB * b + j + 1)
                    v.tensor_reduce(y64[:, :, bass.ds(b * BT + 2 * j, 2)].rearrange("p f t -> p t f"),
                                    fold[g].rearrange("p (t h f) -> p t f h", t=2, h=HEADS),
                                    AX.X, ALU.add).then_inc(s_y, 1)

                def body(b, half, slot):
                    for j in range(PB):
                        g = j % 2
                        dve.wait_ge(s_mm, PB * b + j + 1)
                        v.tensor_tensor(
                            prod[g].rearrange("p (d u f) -> p d u f", d=2, u=2 * HEADS),
                            ps[:, 2 * g:2 * g + 2, :].rearrange("p d (u f) -> p d u f", u=2 * HEADS),
                            alv[:, :, bass.ds(b * BT + 2 * j, 2), :].rearrange("p d t h -> p d (t h)")
                            .unsqueeze(3).broadcast_to([P, 2, 2 * HEADS, HF]),
                            ALU.mult).then_inc(s_pr, 1)
                        if j:
                            finish(b, j - 1)
                    finish(b, PB - 1)

                dve.sem_inc(s_pr, 2)
                loop(dve, EB, body)

            return sp_, pe_, dve_, sems

        nscn = [0]
        steps = nst[:, 0:16 * T]

        def tile_flags(dve, flag):
            nc.vector.tensor_copy(steps.rearrange("p (i t) -> p i t", t=T),
                                  flag.unsqueeze(1).broadcast_to([P, 16, T])).then_inc(sc, 1)
            nscn[0] += 1
            dve.wait_ge(sc, nscn[0])

        def scan_y(dve, feats):
            for i in range(feats // 16):
                part = r1[:, i * 16 * T:(i + 1) * 16 * T]
                nc.vector.tensor_tensor_scan(part, steps, part, 0.0, ALU.mult, ALU.add).then_inc(sc, 1)
                nscn[0] += 1
            dve.wait_ge(sc, nscn[0])

        ptmp = l12[:, 0:BT * HF]
        pbufs = [nst[:, i * 512:(i + 1) * 512] for i in range(6)] + [alpha[:, 1040:1552], l12[:, 1792:2304]]
        pst, pzc, psq, ptn = (pbufs[2 * i:2 * i + 2] for i in range(4))
        psel = [alpha[0:8, 0:512], alpha[0:8, 512:768]]
        prs = [alpha[:, 768 + 8 * g:776 + 8 * g] for g in range(2)]
        prt = [alpha[0:8, 784 + g * P:784 + (g + 1) * P] for g in range(2)]

        def gat_post(l):
            sems = phase_sems(f"p{l}", "in0 in1 sel tmp row tr st z zc sq v sd rs rt re r tn rl hn to oe free dma")
            s_in = sems[0:2]
            (s_sel, s_tmp, s_row, s_tr, s_st, s_z, s_zc, s_sq, s_v, s_sd, s_rs, s_rt, s_re, s_r, s_tn, s_rl,
             s_hn, s_to, s_oe, s_free, s_dma) = sems[2:]
            phase_over(sems)
            NU = len(UNITS)
            base = [r3[:, s * QB * 512:(s + 1) * QB * 512] for s in range(2)]
            res = [x_[:, 0:QB * 256] for x_ in base]
            hout = [x_[:, QB * 256:QB * 512] for x_ in base]
            xin = [r2[:, T * XF + s * QB * P:T * XF + (s + 1) * QB * P] for s in range(2)]
            per = 1 + l
            couples = [(i, [(g,) + UNITS[i + g] for g in range(2)]) for i in (0, 2)]

            def sp_(sp):
                def load(b, slot):
                    if l == 0:
                        sp.dma_start(res[slot].rearrange("p (q h c) -> p q h c", q=QB, h=2),
                                     blk(ht_dram[0], b).rearrange("p (q h d c) -> p q h d c", q=QB, h=2, d=2)
                                     [:, :, :, 1, :]).then_inc(s_in[slot], 16)
                    else:
                        sp.dma_start(res[slot], blk(h1d_dram, b)).then_inc(s_in[slot], 16)
                        sp.dma_start(xin[slot].rearrange("p (q c) -> p q c", q=QB),
                                     blk(xt_dram, b).rearrange("p (q d c) -> p q d c", q=QB, d=2)
                                     [:, :, 1, :]).then_inc(s_in[slot], 16)

                def body(b, half, slot, ahead=True):
                    if ahead:
                        sp.wait_ge(s_oe, NU * b + 2)
                        load(b + 1, 1 - slot)
                    if l == 0:
                        sp.wait_ge(s_hn, NU * b + NU)
                        sp.dma_start(blk(h1d_dram, b), hout[slot]).then_inc(s_dma, 16)
                        sp.wait_ge(s_dma, 16 * b + 16)
                        sp.sem_inc(s_free, 1)

                if l == 0:
                    sp.sem_inc(s_free, 2)
                for part, c in zip(psel, (0, 1024)):
                    sp.dma_start(part, sel[0:8, c:c + part.shape[1]]).then_inc(s_sel, 16)
                load(0, 0)
                with sp.Fori(0, EB // 2) as i:
                    body(2 * i, i, 0)
                    body(2 * i + 1, i, 1)
                body(EB - 1, EB // 2, 0, ahead=False)

            def pe_(pe):
                mm, tr = nc.tensor.matmul, nc.tensor.transpose

                def body(b, half, slot):
                    pe.wait_ge(s_row, b + 1)
                    for i, couple in couples:
                        w = NU * b + i

                        def stats(kk):
                            for g, q0, nq in couple:
                                pe.wait_ge(s_sq, per * w + 2 * kk + g + 1)
                                for j in range((2 - kk) * nq):
                                    c = 2 + 2 * kk
                                    m = mm(ps[:, 4 + g, c * j:c * (j + 1)], psq[g][:, j * P:(j + 1) * P],
                                           k((K_J2, K_J4)[kk], c), start=True, stop=True)
                                m.then_inc(s_v, 1)
                            for g, q0, nq in couple:
                                pe.wait_ge(s_rs, per * w + 2 * kk + g + 1)
                                tr(ps[0:4 * nq, 4 + g, P:2 * P], prs[g][:, 0:4 * nq], ident).then_inc(s_rt, 1)
                            for g, q0, nq in couple:
                                pe.wait_ge(s_re, per * w + 2 * kk + g + 1)
                                for j in range((2 - kk) * nq):
                                    m = mm(ps[:, 4 + g, j * P:(j + 1) * P],
                                           psel[kk][0:4 * nq, j * P:(j + 1) * P], prt[g][0:4 * nq, :],
                                           start=True, stop=True)
                                m.then_inc(s_r, 1)

                        for g, q0, nq in couple:
                            pe.wait_ge(s_oe, w + g + 1)
                            for j in range(2 * nq):
                                c = (2 * q0 + j) * P
                                t = tr(ps[:, g, j * P:(j + 1) * P], stg[slot][:, c:c + P], ident)
                            t.then_inc(s_tr, 1)
                        for g, q0, nq in couple:
                            pe.wait_ge(s_st, w + g + 1)
                            mm(ps[:, 2 + g, 0:nq * 256], k(K_C64), pst[g][:, 0:nq * 256],
                               start=True, stop=True).then_inc(s_z, 1)
                        stats(0)
                        for g, q0, nq in couple:
                            pe.wait_ge(s_hn, w + g + 1)
                            ho = hout[slot][:, q0 * 256:(q0 + nq) * 256]
                            if l == 0:
                                for j in range(2 * nq):
                                    t = tr(ps[:, 6 + g, j * P:(j + 1) * P], ho[:, j * P:(j + 1) * P], ident)
                                t.then_inc(s_to, 1)
                            else:
                                m = nq * P
                                hv = ho.rearrange("p (q h c) -> p q h c", q=nq, h=2)
                                pe.wait_ge(s_in[slot], 32 * half + 32)
                                mm(ps[:, 6 + g, 0:m], k(K_C32), xin[slot][:, q0 * P:q0 * P + m],
                                   start=True, stop=False)
                                mm(ps[:, 6 + g, 0:m], dv[:, D_OA:D_OA + P], hv[:, :, 0, :],
                                   start=False, stop=False)
                                mm(ps[:, 6 + g, 0:m], dv[:, D_OB:D_OB + P], hv[:, :, 1, :],
                                   start=False, stop=True).then_inc(s_z, 1)
                        if l == 1:
                            stats(1)
                            for g, q0, nq in couple:
                                pe.wait_ge(s_tn, 2 * w + 2 + g + 1)
                                for j in range(nq):
                                    t = tr(ps[:, g, j * P:(j + 1) * P], ptn[g][:, j * P:(j + 1) * P], ident)
                                t.then_inc(s_to, 1)

                pe.wait_ge(s_sel, 32)
                loop(pe, EB, body)

            def act_(act):
                a = nc.scalar.activation

                def body(b, half, slot):
                    for i, couple in couples:
                        w = NU * b + i

                        def stats(kk):
                            for g, q0, nq in couple:
                                act.wait_ge(s_v, per * w + 2 * kk + g + 1)
                                a(prs[g][:, 0:4 * nq], ps[:, 4 + g, 0:4 * nq], ACT.Sqrt,
                                  bias=dcol(D_EPS)).then_inc(s_sd, 1)
                            for g, q0, nq in couple:
                                act.wait_ge(s_rt, per * w + 2 * kk + g + 1)
                                a(prt[g][0:4 * nq, :], ps[0:4 * nq, 4 + g, P:2 * P],
                                  ACT.Identity).then_inc(s_re, 1)

                        for g, q0, nq in couple:
                            act.wait_ge(s_tr, w + g + 1)
                            a(pst[g][:, 0:nq * 256], ps[:, g, 0:nq * 256], ACT.Identity).then_inc(s_st, 1)
                        for g, q0, nq in couple:
                            act.wait_ge(s_z, per * w + g + 1)
                            a(psq[g][:, 0:nq * 256], ps[:, 2 + g, 0:nq * 256], ACT.Square,
                              bias=dcol(D_BC[l])).then_inc(s_sq, 1)
                            a(pzc[g][:, 0:nq * 256], ps[:, 2 + g, 0:nq * 256], ACT.Identity,
                              bias=dcol(D_BC[l])).then_inc(s_zc, 1)
                        stats(0)
                        for g, q0, nq in couple:
                            act.wait_ge(s_tn, per * w + g + 1)
                            a(ptn[g][:, 0:nq * 256], ptn[g][:, 0:nq * 256], ACT.Relu, bias=col(C_B[l]),
                              scale=col(C_G[l])).then_inc(s_rl, 1)
                        if l == 1:
                            for g, q0, nq in couple:
                                m = nq * P
                                act.wait_ge(s_z, 2 * w + 2 + g + 1)
                                a(psq[g][:, 0:m], ps[:, 6 + g, 0:m], ACT.Square,
                                  bias=dcol(D_OBC)).then_inc(s_sq, 1)
                                a(pzc[g][:, 0:m], ps[:, 6 + g, 0:m], ACT.Identity,
                                  bias=dcol(D_OBC)).then_inc(s_zc, 1)
                            stats(1)

                loop(act, EB, body)

            def dve_(dve):
                v = nc.vector

                def sums(b, slot):
                    v.tensor_tensor(ptmp.rearrange("p (t f) -> p t f", f=HF),
                                    pm[:, bass.ds(b * BT, BT)].unsqueeze(2).broadcast_to([P, BT, HF]),
                                    carry[:, 0:HF].unsqueeze(1).broadcast_to([P, BT, HF]),
                                    ALU.mult).then_inc(s_tmp, 1)
                    dve.wait_ge(s_tmp, b + 1)
                    v.tensor_tensor(stg[slot].rearrange("p (t f) -> p t f", f=HF),
                                    y64[:, :, bass.ds(b * BT, BT)].rearrange("p f t -> p t f"),
                                    ptmp.rearrange("p (t f) -> p t f", f=HF), ALU.add).then_inc(s_row, 1)

                def body(b, half, slot):
                    sums(b, slot)
                    if l == 0:
                        dve.wait_ge(s_free, b + 1)
                    dve.wait_ge(s_in[slot], (16 + 16 * l) * half + (16 + 16 * l))
                    for i, couple in couples:
                        w = NU * b + i

                        def norm(kk):
                            for g, q0, nq in couple:
                                dve.wait_ge(s_sd, per * w + 2 * kk + g + 1)
                                v.reciprocal(prs[g][:, 0:4 * nq], prs[g][:, 0:4 * nq]).then_inc(s_rs, 1)
                            for g, q0, nq in couple:
                                n = nq * (256, P)[kk]
                                dve.wait_ge(s_r, per * w + 2 * kk + g + 1)
                                dve.wait_ge(s_zc, per * w + 2 * kk + g + 1)
                                v.tensor_tensor(ptn[g][:, 0:n], pzc[g][:, 0:n], ps[:, 4 + g, 0:n],
                                                ALU.mult).then_inc(s_tn, 1)

                        norm(0)
                        for g, q0, nq in couple:
                            dve.wait_ge(s_rl, w + g + 1)
                            v.tensor_tensor(hout[slot][:, q0 * 256:(q0 + nq) * 256],
                                            res[slot][:, q0 * 256:(q0 + nq) * 256],
                                            ptn[g][:, 0:nq * 256], ALU.add).then_inc(s_hn, 1)
                        if l == 1:
                            norm(1)
                        for g, q0, nq in couple:
                            dve.wait_ge(s_to, w + g + 1)
                            if l == 0:
                                v.tensor_copy(r2[:, bass.ds(b * (BT * HF) + q0 * 256, nq * 256)],
                                              ps[:, 6 + g, 0:nq * 256]).then_inc(s_oe, 1)
                            else:
                                v.tensor_copy(r2[:, bass.ds(b * (BT * XF) + q0 * P, nq * P)],
                                              ps[:, g, 0:nq * P]).then_inc(s_oe, 1)
                    dve.wait_ge(s_oe, NU * b + NU + 2)
                    dve.sem_inc(rows_ready, 1)

                dve.sem_inc(s_oe, 2)
                loop(dve, EB, body)

            return sp_, pe_, act_, dve_, sems

        off[0] = 0
        gxr, gx, gh, g_r, g_z, g_w, g_u, g_n, g_d, go = ([lay(r2, 512) for _ in range(2)] for _ in range(10))
        gru_sems = phase_sems("q", "in0 in1 sel tr x mm rz u n zh dc h y c zc sq v sd rs rt re r o to oe free st")
        gi = gru_sems[0:2]
        (q_sel, q_tr, q_x, q_mm, q_rz, q_u, q_n, q_zh, q_dc, q_h, q_y, q_c, q_zc, q_sq, q_v, q_sd, q_rs, q_rt, q_re,
         q_r, q_o, q_to, q_oe, q_free, q_st) = gru_sems[2:]
        qsel = l12[0:16, 0:512]
        table = stage[:, 0:2]
        qrs = [g_n[s][:, 0:16] for s in range(2)]
        qrt = [g_n[s][0:16, P:2 * P] for s in range(2)]
        phase_over(gru_sems)

        def gate(w, g):
            return wt[:, w + g * P:w + (g + 1) * P]

        def dgru_sp(sp):
            def load(b, slot):
                sp.dma_start(gxr[slot], blk(x1_blk, b)).then_inc(gi[slot], 16)

            def body(b, i, ns):
                for s in range(ns):
                    sp.wait_ge(q_oe, b + s + 2 + 1)
                    sp.dma_start(blk(out_blk, b + s), go[s]).then_inc(q_st, 16)
                    sp.wait_ge(q_st, 16 * b + 16 * s + 16)
                    sp.sem_inc(q_free, 1)

            sp.dma_start(qsel, sel[:, 1024:1536]).then_inc(q_sel, 16)
            sp.wait_ge(put_x1, ALL)
            sp.sem_inc(q_free, 2)
            load(0, 0)
            load(1, 1)
            with sp.Fori(0, DB // 2 - 1) as i:
                sp.wait_ge(q_tr, 2 * i + 2)
                load(2 * i + 2, 0)
                load(2 * i + 3, 1)
                body(2 * i, i, 2)
            sp.wait_ge(q_tr, DB - 1)
            load(DB - 1, 0)
            body(DB - 3, DB // 2 - 1, 2)
            body(DB - 1, DB // 2, 1)
            sp.sem_inc(out_done, 1)

        def dgru_pe(pe):
            mm, tr = nc.tensor.matmul, nc.tensor.transpose

            def body(b, i, ns):
                for s in range(ns):
                    pe.wait_ge(gi[s], 16 * i + 16)
                    pe.wait_ge(q_oe, b + s + 1)
                    for j in range(4):
                        t = tr(ps[:, 6 + s, j * P:(j + 1) * P], gxr[s][:, j * P:(j + 1) * P], ident)
                    t.then_inc(q_tr, 1)
                for st in range(STEPS):
                    for s in range(ns):
                        c = 8 * i + ns * st + s
                        if st == 0:
                            pe.wait_ge(q_x, b + s + 1)
                        else:
                            pe.wait_ge(q_h, c - ns + 1)
                        for g in (1, 0, 2):
                            mm(ps[:, 3 * s + g, :], gate(W_HH, g), (gx if st == 0 else gh)[s],
                               start=True, stop=True).then_inc(q_mm, 1)
                for s in range(ns):
                    pe.wait_ge(q_y, b + s + 1)
                    mm(ps[:, 3 * s, :], k(K_C32), g_u[s], start=True, stop=True).then_inc(q_c, 1)
                for s in range(ns):
                    pe.wait_ge(q_sq, b + s + 1)
                    for j in range(4):
                        m = mm(ps[:, 3 * s + 1, 4 * j:4 * j + 4], g_z[s][:, j * P:(j + 1) * P], k(K_J4, 4),
                               start=True, stop=True)
                    m.then_inc(q_v, 1)
                for s in range(ns):
                    pe.wait_ge(q_rs, b + s + 1)
                    tr(ps[0:16, 3 * s + 1, P:2 * P], qrs[s], ident).then_inc(q_rt, 1)
                for s in range(ns):
                    pe.wait_ge(q_re, b + s + 1)
                    for j in range(4):
                        m = mm(ps[:, 3 * s + 1, j * P:(j + 1) * P], qsel[:, j * P:(j + 1) * P], qrt[s],
                               start=True, stop=True)
                    m.then_inc(q_r, 1)
                for s in range(ns):
                    pe.wait_ge(q_o, b + s + 1)
                    for j in range(4):
                        t = tr(ps[:, 6 + s, j * P:(j + 1) * P], g_d[s][:, j * P:(j + 1) * P], ident)
                    t.then_inc(q_to, 1)

            pe.wait_ge(q_sel, 16)
            pairs(pe, 0, DB, body)

        def dgru_act(act):
            a = nc.scalar.activation

            def body(b, i, ns):
                a(table[:, 0:1], dcol(D_EPS), ACT.Sigmoid)
                for s in range(ns):
                    act.wait_ge(q_tr, b + s + 1)
                    a(gx[s], ps[:, 6 + s, :], ACT.Identity).then_inc(q_x, 1)
                for st in range(STEPS):
                    for s in range(ns):
                        c = 8 * i + ns * st + s
                        act.wait_ge(q_mm, 3 * c + 1)
                        a(g_z[s], ps[:, 3 * s + 1, :], ACT.Sigmoid, bias=dcol(D_BZ)).then_inc(q_rz, 1)
                        a(g_w[s], ps[:, 3 * s + 1, :], ACT.Sigmoid, bias=dcol(D_NBZ), scale=-1.0)\
                            .then_inc(q_rz, 1)
                        act.wait_ge(q_mm, 3 * c + 2)
                        a(g_r[s], ps[:, 3 * s, :], ACT.Sigmoid, bias=dcol(D_BR)).then_inc(q_rz, 1)
                    for s in range(ns):
                        c = 8 * i + ns * st + s
                        act.wait_ge(q_u, c + 1)
                        a(g_n[s], g_u[s], ACT.Tanh, bias=col(C_BIHN)).then_inc(q_n, 1)
                a(table[:, 1:2], dcol(D_EPS), ACT.Sqrt)
                for s in range(ns):
                    act.wait_ge(q_c, b + s + 1)
                    a(g_z[s], ps[:, 3 * s, :], ACT.Square).then_inc(q_sq, 1)
                    a(g_r[s], ps[:, 3 * s, :], ACT.Identity).then_inc(q_zc, 1)
                for s in range(ns):
                    act.wait_ge(q_v, b + s + 1)
                    a(qrs[s], ps[:, 3 * s + 1, 0:16], ACT.Sqrt, bias=dcol(D_EPS)).then_inc(q_sd, 1)
                for s in range(ns):
                    act.wait_ge(q_rt, b + s + 1)
                    a(qrt[s], ps[0:16, 3 * s + 1, P:2 * P], ACT.Identity).then_inc(q_re, 1)

            pairs(act, 0, DB, body)

        def dgru_dve(dve):
            v = nc.vector

            def body(b, i, ns):
                for st in range(STEPS):
                    for s in range(ns):
                        c = 8 * i + ns * st + s
                        h = (gx if st == 0 else gh)[s]
                        dve.wait_ge(q_rz, 3 * c + 1)
                        if st:
                            dve.wait_ge(q_h, c - ns + 1)
                        v.tensor_tensor(g_z[s], g_z[s], h, ALU.mult).then_inc(q_zh, 1)
                        dve.wait_ge(q_mm, 3 * c + 3)
                        dve.wait_ge(q_rz, 3 * c + 3)
                        v.scalar_tensor_tensor(out=g_u[s], in0=ps[:, 3 * s + 2, :], scalar=col(C_BHHN),
                                               in1=g_r[s], op0=ALU.add, op1=ALU.mult).then_inc(q_u, 1)
                    for s in range(ns):
                        c = 8 * i + ns * st + s
                        dve.wait_ge(q_n, c + 1)
                        v.tensor_tensor(g_d[s], g_w[s], g_n[s], ALU.mult).then_inc(q_dc, 1)
                        dve.wait_ge(q_dc, c + 1)
                        dve.wait_ge(q_zh, c + 1)
                        v.tensor_tensor(gh[s], g_d[s], g_z[s], ALU.add).then_inc(q_h, 1)
                for s in range(ns):
                    dve.wait_ge(q_h, 8 * i + ns * (STEPS - 1) + s + 1)
                    v.tensor_tensor(g_u[s], gx[s], gh[s], ALU.add).then_inc(q_y, 1)
                for s in range(ns):
                    dve.wait_ge(q_sd, b + s + 1)
                    v.reciprocal(qrs[s], qrs[s]).then_inc(q_rs, 1)
                for s in range(ns):
                    dve.wait_ge(q_r, b + s + 1)
                    dve.wait_ge(q_zc, b + s + 1)
                    v.tensor_tensor(g_d[s], g_r[s], ps[:, 3 * s + 1, :], ALU.mult).then_inc(q_o, 1)
                for s in range(ns):
                    dve.wait_ge(q_to, b + s + 1)
                    dve.wait_ge(q_free, b + s + 1)
                    v.tensor_copy(go[s], ps[:, 6 + s, :]).then_inc(q_oe, 1)

            dve.sem_inc(q_oe, 2)
            pairs(dve, 0, DB, body)

        hs = r2[:, T * XF:2 * T * XF]
        work = r2[:, T * BONDF:T * XF]
        bondv = r2[:, 0:T * BONDF].rearrange("p (t c) -> p t c", c=BONDF)
        hd = r3[:, 0:T * XF]
        y32 = r1[:, 0:T * XF].rearrange("p (f t) -> p f t", t=T)
        ag = r1[:, T * XF:2 * T * XF]
        uw = l12[:, 0:4 * 512]
        vb = l12[:, 2048:2048 + P]
        mi = [sem(f"mi_in{s}") for s in range(2)]
        mi_tr, mi_cp, ld_bond, ld_uw = sem("mi_tr"), sem("mi_cp"), sem("ld_bond"), sem("ld_uw")

        def init_sp(sp):
            def load(b, slot):
                sp.dma_start(stg[slot].rearrange("p (d c) -> p d c", d=2),
                             r1[:].rearrange("p (d c) -> p d c", d=2)[:, :, bass.ds(b * SB, SB)])\
                    .then_inc(mi[slot], 16)

            sp.dma_start(bondv, sort_s[1:EP + 1, 2:PAY].rearrange("(p t) c -> p t c", t=T)).then_inc(ld_bond, 16)
            sp.dma_start(l12[:, 0:2176], bondw).then_inc(ld_uw, 16)
            sp.wait_ge(got_x1, 2 * ALL)
            load(0, 0)
            with sp.Fori(0, EB // 2) as i:
                for s in range(2):
                    sp.wait_ge(mi_cp, 4 * i + 2 * s + 1)
                    load(2 * i + s + 1, 1 - s)

        def init_pe(pe):
            tr = nc.tensor.transpose

            def body(b, half, slot):
                pe.wait_ge(mi[slot], 16 * half + 16)
                pe.wait_ge(mi_cp, 2 * b + 1)
                for d in range(2):
                    for q in range(QB):
                        t = tr(ps[:, 2 * d + q // 4, (q % 4) * P:(q % 4 + 1) * P],
                               stg[slot][:, d * SB + q * P:d * SB + (q + 1) * P], ident)
                t.then_inc(mi_tr, 1)

            loop(pe, EB, body)

        def init_act(act):
            a = nc.scalar.activation

            def body(b, half, slot):
                act.wait_ge(mi_tr, b + 1)
                for o, d in ((hs, 0), (hd, 1)):
                    for p, (c, n) in enumerate(PARTS):
                        last_ = a(o[:, bass.ds(b * SB + c, n)], ps[:, 2 * d + p, 0:n], ACT.Identity)
                last_.then_inc(mi_cp, 2)

            act.sem_inc(mi_cp, 1)
            loop(act, EB, body)

        mg = [sem(f"mg_in{s}") for s in range(2)]
        mg_mm, mg_v, mg_pr, mg_rd, mg_y = (sem(f"mg_{n}") for n in ("mm", "v", "pr", "rd", "y"))
        hq = [stage[:, s * SB:(s + 1) * SB] for s in range(2)]
        msum = work[:, 2 * SB + 1024:2 * SB + 1024 + P]
        mprod = [alpha[:, 0:1024], work[:, 2 * SB:2 * SB + 1024]]
        uw4 = uw.rearrange("p (q c) -> p q c", q=4)
        PB = 2 * QB

        def msg_sp(sp):
            def load(b, slot):
                sp.dma_start(hq[slot], hd[:, bass.ds(b * SB, SB)]).then_inc(mg[slot], 16)

            load(0, 0)
            with sp.Fori(0, EB // 2) as i:
                for s in range(2):
                    sp.wait_ge(mg_y, 2 * QB * i + QB * s + 1)
                    load(2 * i + s + 1, 1 - s)

        def msg_pe_group(pe, m, b, h, q):
            mm = nc.tensor.matmul
            lhs = h[:, q * P:(q + 1) * P]
            for r in range(2):
                pe.wait_ge(mg_pr, PB * EB * m + PB * b + 2 * q + r + 1)
                for j in range(2):
                    t = mm(ps[:, 3 + 2 * r + j, :], lhs, uw4[:, 2 * r + j, :], start=True, stop=True)
                t.then_inc(mg_mm, 1)
            pe.wait_ge(mg_y, QB * EB * m + QB * b + q + 1)
            mm(ps[:, 7, 0:P], lhs, vb, start=True, stop=True).then_inc(mg_v, 1)

        def msg_dve_group(dve, m, b, q):
            v = nc.vector
            w = PB * EB * m + PB * b + 2 * q
            u = QB * EB * m + QB * b + q
            for r in range(2):
                dve.wait_ge(mg_mm, w + r + 1)
                v.tensor_tensor(
                    mprod[r].rearrange("p (t i k) -> p t i k", t=2, k=BONDF),
                    ps[:, 3 + 2 * r:5 + 2 * r, :].rearrange("p t (i k) -> p t i k", k=BONDF),
                    bondv[:, bass.ds(b * BT + 4 * q + 2 * r, 2), :].unsqueeze(2)
                    .broadcast_to([P, 2, XF, BONDF]), ALU.mult).then_inc(mg_pr, 1)
            for r in range(2):
                dve.wait_ge(mg_pr, w + r + 3)
                v.tensor_reduce(msum[:, r * 64:(r + 1) * 64],
                                mprod[r].rearrange("p (u k) -> p u k", k=BONDF), AX.X, ALU.add).then_inc(mg_rd, 1)
            dve.wait_ge(mg_v, u + 1)
            dve.wait_ge(mg_rd, w + 2)
            v.tensor_tensor(y32[:, :, bass.ds(b * BT + 4 * q, 4)].rearrange("p f t -> p t f"),
                            msum.rearrange("p (t f) -> p t f", f=XF),
                            ps[:, 7, 0:P].rearrange("p (t f) -> p t f", f=XF), ALU.add).then_inc(mg_y, 1)
            dve.wait_ge(mg_y, u + 2)

        def msg_pe(pe):
            def body(b, half, slot):
                pe.wait_ge(mg[slot], 16 * half + 16)
                for q in range(QB):
                    msg_pe_group(pe, 0, b, hq[slot], q)

            loop(pe, EB, body)

        def msg_dve(dve):
            def body(b, half, slot):
                for q in range(QB):
                    msg_dve_group(dve, 0, b, q)

            dve.sem_inc(mg_pr, 2)
            dve.sem_inc(mg_y, 1)
            loop(dve, EB, body)

        ering = [stage[:, s * SB:(s + 1) * SB] for s in range(2)]
        etmp = stage[:, 2 * SB:3 * SB]
        e_at, e_r, e_z = ([nst[:, i * SB + c:i * SB + c + n] for c, n in PARTS] for i in range(3))
        e_u, e_n = ([work[:, i * SB + c:i * SB + c + n] for c, n in PARTS] for i in range(2))
        e_d = e_u
        r_tmp, r_row, r_st, r_free = (sem(f"r_{n}") for n in ("tmp", "row", "st", "free"))

        def form_rows(dve, b, slot, tmp, row, before):
            v = nc.vector
            v.tensor_tensor(etmp.rearrange("p (t f) -> p t f", f=XF),
                            pm_s[:, bass.ds(b * BT, BT)].unsqueeze(2).broadcast_to([P, BT, XF]),
                            carry[:, 0:XF].unsqueeze(1).broadcast_to([P, BT, XF]), ALU.mult).then_inc(tmp, 1)
            dve.wait_ge(tmp, before + b + 1)
            v.tensor_tensor(ering[slot].rearrange("p (t f) -> p t f", f=XF),
                            y32[:, :, bass.ds(b * BT, BT)].rearrange("p f t -> p t f"),
                            etmp.rearrange("p (t f) -> p t f", f=XF), ALU.add).then_inc(row, 1)
            dve.wait_ge(row, before + b + 1)

        def rows_dve(dve, m):
            def body(b, half, slot):
                dve.wait_ge(r_free, EB * m + b + 1)
                form_rows(dve, b, slot, r_tmp, r_row, EB * m)

            if m == 0:
                dve.sem_inc(r_free, 2)
            loop(dve, EB, body)
            dve.wait_ge(r_free, EB * (m + 1) + 2)

        def rows_sp(sp, m):
            def body(b, half, slot):
                sp.wait_ge(r_row, EB * m + b + 1)
                sp.dma_start(agg_tab[0:EP, :].rearrange("(p t) f -> p (t f)", t=T)
                             [:, bass.ds(b * SB, SB)], ering[slot]).then_inc(r_st, 16)
                sp.wait_ge(r_st, 16 * EB * m + 16 * b + 16)
                sp.sem_inc(r_free, 1)

            loop(sp, EB, body)
            sp.sem_inc(agg_stored, 1)

        es = {n: sem(f"e_{n}") for n in ("tmp", "row", "tr", "at", "mm", "rz", "u", "n", "dc", "h")}

        def srcgru_pe(pe, m):
            s = es
            mm, tr = nc.tensor.matmul, nc.tensor.transpose

            def body(b, half, slot):
                pe.wait_ge(s["row"], EB * m + b + 1)
                for p, (c, n) in enumerate(PARTS):
                    w = 2 * EB * m + 2 * b + p
                    pe.wait_ge(s["h"], w + 1)
                    for j in range(n // P):
                        t = tr(ps[:, 4 * p + 3, j * P:(j + 1) * P], ering[slot][:, c + j * P:c + (j + 1) * P],
                               ident)
                    t.then_inc(s["tr"], 1)
                for p, (c, n) in enumerate(PARTS):
                    w = 2 * EB * m + 2 * b + p
                    h = hs[:, bass.ds(b * SB + c, n)]
                    pe.wait_ge(s["at"], w + 1)
                    for g in range(2):
                        mm(ps[:, 4 * p + g, 0:n], gate(W_IH, g), e_at[p], start=True, stop=False)
                        mm(ps[:, 4 * p + g, 0:n], gate(W_HH, g), h, start=False, stop=True).then_inc(s["mm"], 1)
                    mm(ps[:, 4 * p + 2, 0:n], gate(W_HH, 2), h, start=True, stop=True).then_inc(s["mm"], 1)
                    mm(ps[:, 4 * p + 3, 0:n], gate(W_IH, 2), e_at[p], start=True, stop=True)\
                        .then_inc(s["mm"], 1)

            loop(pe, EB, body)

        def srcgru_act(act, m):
            s = es
            a = nc.scalar.activation

            def body(b, half, slot):
                for p, (c, n) in enumerate(PARTS):
                    w = 2 * EB * m + 2 * b + p
                    act.wait_ge(s["tr"], w + 1)
                    a(e_at[p], ps[:, 4 * p + 3, 0:n], ACT.Identity).then_inc(s["at"], 1)
                for p, (c, n) in enumerate(PARTS):
                    w = 2 * EB * m + 2 * b + p
                    act.wait_ge(s["mm"], 4 * w + 1)
                    a(e_r[p], ps[:, 4 * p, 0:n], ACT.Sigmoid, bias=dcol(D_BR)).then_inc(s["rz"], 1)
                    act.wait_ge(s["mm"], 4 * w + 2)
                    a(e_z[p], ps[:, 4 * p + 1, 0:n], ACT.Sigmoid, bias=dcol(D_BZ)).then_inc(s["rz"], 1)
                for p, (c, n) in enumerate(PARTS):
                    act.wait_ge(s["u"], 2 * EB * m + 2 * b + p + 1)
                    a(e_n[p], e_u[p], ACT.Tanh, bias=col(C_BIHN)).then_inc(s["n"], 1)

            loop(act, EB, body)

        def new_input(dve, s, w, p, hn, inp, dc):
            n = PARTS[p][1]
            dve.wait_ge(s["mm"], 4 * w + 3)
            dve.wait_ge(s["rz"], 2 * w + 1)
            nc.vector.scalar_tensor_tensor(out=e_u[p], in0=ps[:, hn, 0:n], scalar=col(C_BHHN),
                                           in1=e_r[p], op0=ALU.add, op1=ALU.mult).then_inc(s["dc"], 1)
            dve.wait_ge(s["dc"], dc)
            dve.wait_ge(s["mm"], 4 * w + 4)
            nc.vector.tensor_tensor(e_u[p], e_u[p], ps[:, inp, 0:n], ALU.add).then_inc(s["u"], 1)

        def new_state(dve, s, w, p, old, new, dc):
            v = nc.vector
            dve.wait_ge(s["n"], w + 1)
            v.tensor_tensor(e_d[p], old, e_n[p], ALU.subtract).then_inc(s["dc"], 1)
            dve.wait_ge(s["dc"], dc)
            dve.wait_ge(s["rz"], 2 * w + 2)
            v.tensor_tensor(e_d[p], e_d[p], e_z[p], ALU.mult).then_inc(s["dc"], 1)
            dve.wait_ge(s["dc"], dc + 1)
            v.tensor_tensor(new, e_d[p], e_n[p], ALU.add).then_inc(s["h"], 1)

        def srcgru_dve(dve, m):
            def body(b, half, slot):
                form_rows(dve, b, slot, es["tmp"], es["row"], EB * m)
                for p in range(2):
                    new_input(dve, es, 2 * EB * m + 2 * b + p, p, 4 * p + 2, 4 * p + 3,
                              6 * EB * m + 6 * b + p + 1)
                for p, (c, n) in enumerate(PARTS):
                    h = hs[:, bass.ds(b * SB + c, n)]
                    new_state(dve, es, 2 * EB * m + 2 * b + p, p, h, h, 6 * EB * m + 6 * b + 2 * p + 3)

            if m == 0:
                dve.sem_inc(es["h"], 2)
            loop(dve, EB, body)

        ed = {n: sem(f"d_{n}") for n in ("in0", "in1", "tr", "at", "mm", "rz", "u", "n", "dc", "h", "st", "free")}
        fring = [stage[:, (2 + s) * SB:(3 + s) * SB] for s in range(2)]

        def dst_sp(sp, m):
            s = ed

            def load(b, slot):
                sp.wait_ge(agg_in, EB * m + b + 1)
                sp.dma_start(fring[slot], ag[:, bass.ds(b * SB, SB)]).then_inc(s[f"in{slot}"], 16)

            def body(b, slot, ahead=True):
                sp.wait_ge(s["h"], 2 * EB * m + 2 * b + 4)
                sp.dma_start(hd[:, bass.ds(b * SB, SB)], hq[slot]).then_inc(s["st"], 16)
                sp.wait_ge(s["st"], 16 * EB * m + 16 * b + 16)
                sp.sem_inc(s["free"], 1)
                if ahead:
                    load(b + 2, slot)

            load(0, 0)
            load(1, 1)
            with sp.Fori(0, EB // 2 - 1) as i:
                body(2 * i, 0)
                body(2 * i + 1, 1)
            body(EB - 3, 0)
            body(EB - 2, 1, ahead=False)
            body(EB - 1, 0, ahead=False)

        def dst_msg(eng, gru, msg):
            def body(b, half, slot):
                before = gru(b, half, slot)
                for q in range(QB):
                    if before[q]:
                        before[q]()
                    msg(b - 1, 1 - slot, q)

            for step in gru(0, 0, 0):
                if step:
                    step()
            with eng.Fori(0, EB // 2) as i:
                body(2 * i + 1, i, 1)
                body(2 * i + 2, i + 1, 0)
            for q in range(QB):
                msg(EB - 1, 0, q)

        def dst_pe(pe, m):
            s = ed
            mm, tr = nc.tensor.matmul, nc.tensor.transpose

            def gru(b, half, slot):
                def parts(p):
                    c, n = PARTS[p]
                    w = 2 * EB * m + 2 * b + p
                    h = hd[:, bass.ds(b * SB + c, n)]

                    def turn():
                        if p == 0:
                            pe.wait_ge(s[f"in{slot}"], 16 * (4 - slot) * m + 16 * half + 16)
                        pe.wait_ge(s["u"], w + 1)
                        for j in range(n // P):
                            t = tr(ps[:, 0, j * P:(j + 1) * P], fring[slot][:, c + j * P:c + (j + 1) * P], ident)
                        t.then_inc(s["tr"], 1)

                    def r_z():
                        pe.wait_ge(s["at"], w + 1)
                        for g in range(2):
                            mm(ps[:, g, 0:n], gate(W_IH, g), e_at[p], start=True, stop=False)
                            mm(ps[:, g, 0:n], gate(W_HH, g), h, start=False, stop=True).then_inc(s["mm"], 1)

                    def new():
                        mm(ps[:, 2, 0:n], gate(W_HH, 2), h, start=True, stop=True).then_inc(s["mm"], 1)
                        pe.wait_ge(s["rz"], 2 * w + 1)
                        mm(ps[:, 0, 0:n], gate(W_IH, 2), e_at[p], start=True, stop=True).then_inc(s["mm"], 1)

                    return [turn, r_z, new]

                return parts(0) + parts(1) + [None]

            def msg(b, slot, q):
                if q == 0:
                    pe.wait_ge(s["h"], 2 * EB * m + 2 * b + 4)
                msg_pe_group(pe, m + 1, b, hq[slot], q)

            dst_msg(pe, gru, msg)

        def dst_act(act, m):
            s = ed
            a = nc.scalar.activation

            def body(b, half, slot):
                for p, (c, n) in enumerate(PARTS):
                    w = 2 * EB * m + 2 * b + p
                    act.wait_ge(s["tr"], w + 1)
                    a(e_at[p], ps[:, 0, 0:n], ACT.Identity).then_inc(s["at"], 1)
                    act.wait_ge(s["mm"], 4 * w + 1)
                    a(e_r[p], ps[:, 0, 0:n], ACT.Sigmoid, bias=dcol(D_BR)).then_inc(s["rz"], 1)
                    act.wait_ge(s["mm"], 4 * w + 2)
                    a(e_z[p], ps[:, 1, 0:n], ACT.Sigmoid, bias=dcol(D_BZ)).then_inc(s["rz"], 1)
                    act.wait_ge(s["u"], w + 2)
                    a(e_n[p], e_u[p], ACT.Tanh, bias=col(C_BIHN)).then_inc(s["n"], 1)

            loop(act, EB, body)

        def dst_dve(dve, m):
            s = ed

            def gru(b, half, slot):
                def parts(p):
                    c, n = PARTS[p]
                    w = 2 * EB * m + 2 * b + p

                    def first():
                        new_input(dve, s, w, p, 2, 0, 3 * w + 1)

                    def second():
                        if p == 0:
                            dve.wait_ge(s["free"], EB * m + b + 1)
                        new_state(dve, s, w, p, hd[:, bass.ds(b * SB + c, n)], hq[slot][:, c:c + n], 3 * w + 2)

                    return [first, second]

                return [None, None] + parts(0) + [None] + parts(1)

            if m == 0:
                dve.sem_inc(s["u"], 1)
                dve.sem_inc(s["h"], 2)
                dve.sem_inc(s["free"], 2)
            dst_msg(dve, gru, lambda b, slot, q: msg_dve_group(dve, m + 1, b, q))

        x1s = ag
        fin_rows = r3[:, 0:T * XF]
        fs = {n: sem(f"f_{n}") for n in ("ld", "y", "c", "zc", "sq", "v", "sd", "rs", "rt", "re", "r", "o", "to",
                                          "oe", "keep")}
        fsel = nst[0:16, 0:512]
        f_rs = [e_n[p][:, 0:n // XF] for p, (c, n) in enumerate(PARTS)]
        f_rt = [e_n[p][0:n // XF, P:2 * P] for p, (c, n) in enumerate(PARTS)]

        def keep_sp(sp):
            sp.dma_start(xs_dram, hs).then_inc(fs["keep"], 16)
            sp.wait_ge(fs["keep"], 16)

        def final_sp(sp):
            sp.dma_start(fsel, sel[:, 1024:1536]).then_inc(fs["ld"], 16)
            sp.dma_start(x1s, xs_dram).then_inc(fs["ld"], 16)

        def final_pe(pe):
            mm, tr = nc.tensor.matmul, nc.tensor.transpose

            def body(b, half, slot):
                for p, (c, n) in enumerate(PARTS):
                    w = 2 * b + p
                    pe.wait_ge(fs["y"], w + 1)
                    mm(ps[:, 4 * p, 0:n], k(K_C32), e_u[p], start=True, stop=True).then_inc(fs["c"], 1)
                for p, (c, n) in enumerate(PARTS):
                    w = 2 * b + p
                    pe.wait_ge(fs["sq"], w + 1)
                    for j in range(n // P):
                        m = mm(ps[:, 4 * p + 1, 4 * j:4 * j + 4], e_z[p][:, j * P:(j + 1) * P], k(K_J4, 4),
                               start=True, stop=True)
                    m.then_inc(fs["v"], 1)
                for p, (c, n) in enumerate(PARTS):
                    pe.wait_ge(fs["rs"], 2 * b + p + 1)
                    tr(ps[0:n // XF, 4 * p + 1, P:2 * P], f_rs[p], ident).then_inc(fs["rt"], 1)
                for p, (c, n) in enumerate(PARTS):
                    pe.wait_ge(fs["re"], 2 * b + p + 1)
                    for j in range(n // P):
                        m = mm(ps[:, 4 * p + 1, j * P:(j + 1) * P], fsel[0:n // XF, j * P:(j + 1) * P], f_rt[p],
                               start=True, stop=True)
                    m.then_inc(fs["r"], 1)
                for p, (c, n) in enumerate(PARTS):
                    w = 2 * b + p
                    pe.wait_ge(fs["o"], w + 1)
                    for j in range(n // P):
                        t = tr(ps[:, 4 * p + 2, j * P:(j + 1) * P], e_d[p][:, j * P:(j + 1) * P], ident)
                    t.then_inc(fs["to"], 1)

            pe.wait_ge(fs["ld"], 32)
            loop(pe, EB, body)

        def final_act(act):
            a = nc.scalar.activation

            def body(b, half, slot):
                for p, (c, n) in enumerate(PARTS):
                    act.wait_ge(fs["c"], 2 * b + p + 1)
                    a(e_z[p], ps[:, 4 * p, 0:n], ACT.Square).then_inc(fs["sq"], 1)
                    a(e_r[p], ps[:, 4 * p, 0:n], ACT.Identity).then_inc(fs["zc"], 1)
                for p, (c, n) in enumerate(PARTS):
                    act.wait_ge(fs["v"], 2 * b + p + 1)
                    a(f_rs[p], ps[:, 4 * p + 1, 0:n // XF], ACT.Sqrt, bias=dcol(D_EPS)).then_inc(fs["sd"], 1)
                for p, (c, n) in enumerate(PARTS):
                    act.wait_ge(fs["rt"], 2 * b + p + 1)
                    a(f_rt[p], ps[0:n // XF, 4 * p + 1, P:2 * P], ACT.Identity).then_inc(fs["re"], 1)

            loop(act, EB, body)

        def final_dve(dve):
            v = nc.vector

            def body(b, half, slot):
                for p, (c, n) in enumerate(PARTS):
                    v.tensor_tensor(e_u[p], x1s[:, bass.ds(b * SB + c, n)], hs[:, bass.ds(b * SB + c, n)],
                                    ALU.add).then_inc(fs["y"], 1)
                for p, (c, n) in enumerate(PARTS):
                    w = 2 * b + p
                    dve.wait_ge(fs["sd"], w + 1)
                    v.reciprocal(f_rs[p], f_rs[p]).then_inc(fs["rs"], 1)
                for p, (c, n) in enumerate(PARTS):
                    w = 2 * b + p
                    dve.wait_ge(fs["r"], w + 1)
                    dve.wait_ge(fs["zc"], w + 1)
                    v.tensor_tensor(e_d[p], e_r[p], ps[:, 4 * p + 1, 0:n], ALU.mult).then_inc(fs["o"], 1)
                for p, (c, n) in enumerate(PARTS):
                    dve.wait_ge(fs["to"], 2 * b + p + 1)
                    v.tensor_copy(fin_rows[:, bass.ds(b * SB + c, n)], ps[:, 4 * p + 2, 0:n])\
                        .then_inc(fs["oe"], 1)
                dve.wait_ge(fs["oe"], 2 * b + 2)
                dve.sem_inc(rows_ready, 1)

            dve.wait_ge(fs["ld"], 32)
            loop(dve, EB, body)

        log0, log1 = gat_logits(0), gat_logits(1)
        val0, val1 = gat_values(0), gat_values(1)
        post0, post1 = gat_post(0), gat_post(1)
        block = ctx.enter_context(nc.Block())

        @block.sync
        def _(sp):
            prep_sp(sp)
            barrier(sp, "sp")
            dense_sp(sp, 0, DB)
            sp.sem_inc(dense_done, 1)
            barrier(sp, "sp", dense_sems)
            for log, val, post in ((log0, val0, post0), (log1, val1, post1)):
                log[0](sp)
                barrier(sp, "sp", log[-1])
                val[0](sp)
                barrier(sp, "sp", val[-1])
                post[0](sp)
                barrier(sp, "sp", post[-1])
            dgru_sp(sp)
            barrier(sp, "sp", gru_sems)
            init_sp(sp)
            barrier(sp, "sp")
            keep_sp(sp)
            msg_sp(sp)
            barrier(sp, "sp")
            for m in range(STEPS):
                if m < STEPS - 1:
                    rows_sp(sp, m)
                barrier(sp, "sp")
                if m < STEPS - 1:
                    dst_sp(sp, m)
                    barrier(sp, "sp")
            final_sp(sp)
            sp.wait_ge(put_out, ALL)

        @block.tensor
        def _(pe):
            prep_pe_(pe)
            barrier(pe, "pe")
            sort_pe(pe)
            barrier(pe, "pe")
            flags_pe(pe, 0)
            for l, (log, val, post) in enumerate(((log0, val0, post0), (log1, val1, post1))):
                log[1](pe)
                barrier(pe, "pe")
                softmax_pe(pe, l)
                val[1](pe)
                if l == 0:
                    flags_pe(pe, 1)
                barrier(pe, "pe")
                carry_pe(pe, HF)
                post[1](pe)
                barrier(pe, "pe")
            dgru_pe(pe)
            barrier(pe, "pe")
            init_pe(pe)
            barrier(pe, "pe")
            msg_pe(pe)
            barrier(pe, "pe")
            for m in range(STEPS):
                carry_pe(pe, XF)
                srcgru_pe(pe, m)
                barrier(pe, "pe")
                if m < STEPS - 1:
                    dst_pe(pe, m)
                    barrier(pe, "pe")
            final_pe(pe)

        @block.scalar
        def _(act):
            barrier(act, "act")
            dense_act(act, 0, DB)
            barrier(act, "act")
            for l, (log, val, post) in enumerate(((log0, val0, post0), (log1, val1, post1))):
                log[2](act)
                barrier(act, "act")
                softmax_act(act, l)
                barrier(act, "act")
                post[2](act)
                barrier(act, "act")
            dgru_act(act)
            barrier(act, "act")
            init_act(act)
            barrier(act, "act")
            barrier(act, "act")
            for m in range(STEPS):
                srcgru_act(act, m)
                barrier(act, "act")
                if m < STEPS - 1:
                    dst_act(act, m)
                    barrier(act, "act")
            final_act(act)

        @block.vector
        def _(dve):
            prep_dve_(dve)
            barrier(dve, "dve")
            sort_dve(dve)
            barrier(dve, "dve")
            flags_dve(dve, 0)
            for l, (log, val, post) in enumerate(((log0, val0, post0), (log1, val1, post1))):
                barrier(dve, "dve")
                softmax_dve(dve, l)
                val[2](dve)
                if l == 0:
                    flags_dve(dve, 1)
                tile_flags(dve, ns_f)
                barrier(dve, "dve")
                scan_y(dve, HF)
                carry_dve(dve, y64[:, :, T - 1], HF, row_f, ALU.mult, ALU.add, 0.0)
                post[3](dve)
                barrier(dve, "dve")
            dgru_dve(dve)
            barrier(dve, "dve")
            barrier(dve, "dve")
            dve.wait_ge(ld_bond, 16)
            msg_dve(dve)
            barrier(dve, "dve")
            for m in range(STEPS):
                tile_flags(dve, ns_fs)
                scan_y(dve, XF)
                carry_dve(dve, y32[:, :, T - 1], XF, row_fs, ALU.mult, ALU.add, 0.0)
                if m < STEPS - 1:
                    rows_dve(dve, m)
                srcgru_dve(dve, m)
                barrier(dve, "dve")
                if m < STEPS - 1:
                    dst_dve(dve, m)
                    barrier(dve, "dve")
            final_dve(dve)

        @block.gpsimd
        def _(pool):
            def scatter(table, index, rows, done):
                for t in range(T):
                    nc.gpsimd.indirect_dma_start(table, bass.IndirectOffsetOnAxis(ap=index(t), axis=0),
                                                 rows(t), None).then_inc(done, 16)

            def gather(rows, table, index, done):
                for t in range(T):
                    nc.gpsimd.indirect_dma_start(rows(t), None, table,
                                                 bass.IndirectOffsetOnAxis(ap=index(t), axis=0)).then_inc(done, 16)

            def scatter_blocks(table, index, rows, done, before):
                for t in range(T):
                    if t % BT == 0:
                        pool.wait_ge(rows_ready, before + t // BT + 1)
                    nc.gpsimd.indirect_dma_start(table, bass.IndirectOffsetOnAxis(ap=index(t), axis=0),
                                                 rows(t), None).then_inc(done, 16)

            counts = [0, 0]

            def gather_blocks(parts, arrived):
                for t in range(T + 1):
                    if t == T or (t > BT and t % BT == 4):
                        b = (t - 1) // BT if t == T else t // BT - 1
                        pool.wait_ge((got_even, got_odd)[b % 2], counts[b % 2])
                        pool.sem_inc(arrived, 1)
                    if t == T:
                        break
                    for rows, table, index in parts:
                        nc.gpsimd.indirect_dma_start(
                            rows(t), None, table, bass.IndirectOffsetOnAxis(ap=index(t), axis=0)
                        ).then_inc((got_even, got_odd)[t // BT % 2], 16)
                        counts[t // BT % 2] += 16

            def at_step(index):
                return lambda t: index[:, t:t + 1]

            for level in range(2):
                pool.wait_ge(rank_ready, 2 * level + 1)
                scatter(tmp_d, at_step(rank_i[2 * level]), lambda t: pay_d[:, t, :], put_tmp_d)
                pool.wait_ge(put_tmp_d, (level + 1) * ALL)
                pool.dma_start(pay_d.rearrange("p t c -> p (t c)"),
                               tmp_d.rearrange("(p t) c -> p (t c)", t=T)).then_inc(ld_tmp_d, 16)
                pool.wait_ge(rank_ready, 2 * level + 2)
                if level == 0:
                    pool.wait_ge(ld_pay, 16)
                scatter(tmp_s, at_step(rank_i[2 * level + 1]), lambda t: pay_s[:, t, :], put_tmp_s)
                pool.wait_ge(put_tmp_s, (level + 1) * ALL)
                pool.dma_start(pay_s.rearrange("p t c -> p (t c)"),
                               tmp_s.rearrange("(p t) c -> p (t c)", t=T)).then_inc(ld_tmp_s, 16)
            pool.wait_ge(rank_ready, 5)
            pool.wait_ge(init_dram, 16 * 6)
            scatter(sort_d, at_step(rank_i[0]), lambda t: pay_d[:, t, :], put_sort_d)
            pool.wait_ge(put_sort_d, ALL)

            def load_list(tab, to, edge, done):
                pool.dma_start(to, tab[1:EP + 1, :].rearrange("(p t) c -> p t c", t=T)).then_inc(done, 16)
                pool.dma_start(edge[:, 0:2], tab[0:EP, :].rearrange("(p t) c -> p t c", t=T)[:, 0, 0:2])\
                    .then_inc(done, 16)
                pool.dma_start(edge[:, 2:4], tab[2:EP + 2, :].rearrange("(p t) c -> p t c", t=T)[:, T - 1, 0:2])\
                    .then_inc(done, 16)

            load_list(sort_d, kid_d, edge_d, ld_kid_d)
            pool.wait_ge(ld_kid_d, 48)
            gather_blocks([(lambda t: xg[:, 0, t, :], x, lambda t: kid_d[:, t, 0:1]),
                           (lambda t: xg[:, 1, t, :], x, lambda t: kid_d[:, t, 1:2])], x_in)
            pool.wait_ge(rank_ready, 6)
            scatter(sort_s, at_step(rank_i[1]), lambda t: pay_s[:, t, :], put_sort_s)
            pool.wait_ge(put_sort_s, ALL)
            load_list(sort_s.bitcast(I32), pay_si, edge_s, ld_kid_s)
            pool.wait_ge(dense_done, 1)
            scatter_blocks(h1_tab, at_step(put_d), lambda t: rows64[:, t, :], put_h1, 0)
            pool.wait_ge(put_h1, ALL)
            gather_blocks([(lambda t: rows64[:, t, :], h1_tab[0:NP, :], lambda t: kid_d[:, t, 0:1])], h1_in)
            pool.wait_ge(flags_ready, 2)
            scatter(pos_tab, at_step(put_s), at_step(pos_val), put_pos)
            pool.wait_ge(put_pos, ALL)
            gather(at_step(pos_of), pos_tab[0:NP, :], lambda t: kid_s[:, t, 1:2], got_pos)
            scatter_blocks(x1_tab, at_step(put_d), lambda t: x1rows[:, t, :], put_x1, EB)
            pool.wait_ge(put_x1, ALL)
            gather(lambda t: xg[:, 0, t, :], x1_tab[0:NP, :], lambda t: kid_s[:, t, 0:1], got_x1)
            gather(lambda t: xg[:, 1, t, :], x1_tab[0:NP, :], lambda t: kid_s[:, t, 1:2], got_x1)
            pool.wait_ge(got_pos, ALL)
            for m in range(STEPS - 1):
                pool.wait_ge(agg_stored, m + 1)
                gather_blocks([(lambda t: ag[:, t * XF:(t + 1) * XF], agg_tab, at_step(pos_of))], agg_in)
            pool.wait_ge(out_done, 1)
            scatter_blocks(out, at_step(put_s), lambda t: fin_rows[:, t * XF:(t + 1) * XF], put_out, 2 * EB)
            pool.wait_ge(put_out, ALL)


def kernel(**inputs):
    import concourse.bacc as _bacc
    from concourse.bass_utils import run_bass_kernel_spmd as _run

    w = {n: np.asarray(a) for n, a in inputs.items()}
    f4 = np.float32

    def diag(block, n, rows=None, cols=None, places=None):
        r, c = block.shape
        m = np.zeros((rows or n * r, cols or n * c), f4)
        for i in range(n):
            ri, ci = (i, i) if places is None else places[i]
            m[ri * r:ri * r + r, ci * c:ci * c + c] = block
        return m

    eye, j64, j32 = np.eye(P, dtype=f4), np.full((64, 64), 1 / 64, f4), np.full((32, 32), 1 / 32, f4)
    j64, j32 = diag(j64, 2), diag(j32, 4)
    edge = np.arange(EP, dtype=f4).reshape(P, T)
    j2 = diag(np.full((64, 1), 1 / 64, f4), 2)
    j4 = diag(np.full((32, 1), 1 / 32, f4), 4)
    consts = np.concatenate([eye, eye - j64, eye - j32, np.triu(np.ones((P, P), f4), 1), j2, j4,
                             np.broadcast_to(np.arange(512, dtype=f4), (P, 512)), edge, edge + NP], 1)

    nw = w["L0_gnn_node_W"].T
    h0 = [diag(nw, 2, rows=P, places=[(2 * h, 0), (2 * h + 1, 1)]) for h in range(2)]
    xw, wh, at_s, at_d1, at_d2 = [], [], [], [], []
    for l in range(2):
        cw = w[f"L0_gnn_convW{l}"].reshape(HEADS, HF, HF)
        xw.append(diag(cw.transpose(2, 0, 1).reshape(HF, HEADS * HF), 2))
        wh += [diag(cw[h], 2) for h in range(HEADS)]
        for to, name, at in ((at_s, "src", (0,)), (at_d1, "dst", (4, 8)), (at_d2, "src", (8,))):
            for h in range(HEADS):
                m = np.zeros((HF, 12), f4)
                for c in at:
                    m[:, c + h] = w[f"L0_gnn_att_{name}{l}"][h]
                to.append(diag(m, 2))

    def gates(name):
        m = w[name].reshape(3, XF, XF)
        return [diag(m[g].T, 4) for g in range(3)]

    def cols(name, times, parts=1):
        return [np.tile(a, times)[:, None] for a in w[name].reshape(parts, -1)]

    weights = np.concatenate(
        h0 + xw + gates("L1_gnn_W_ih") + gates("L1_gnn_W_hh")
        + cols("L0_gnn_node_b", 2) + cols("L0_gnn_drone_b", 2) + cols("L0_gnn_out_b", 4)
        + cols("L1_gnn_b_ih", 4, 3) + cols("L1_gnn_b_hh", 4, 3)
        + [c for l in range(2) for n in ("convb", "ln_g", "ln_b") for c in cols(f"L0_gnn_{n}{l}", 2)], 1)
    ow = w["L0_gnn_out_W"]
    out_ab = [diag(ow, 2, rows=P, places=[(2 * h, 0), (2 * h + 1, 1)]) for h in range(2)]
    drone = np.zeros((P, P + 1), f4)
    drone[0:16, 0:P] = np.concatenate([w["L0_gnn_drone_W"].T] * 2, 1)
    drone[0:16, P] = w["L0_gnn_drone_feat"][0]
    prep = np.concatenate(wh + at_s + at_d1 + at_d2 + out_ab + [drone], 1)
    ub = w["L1_gnn_W_bond"].reshape(BONDF, XF, XF).transpose(2, 1, 0).reshape(XF, XF * BONDF)
    vbm = w["L1_gnn_b_bond"].reshape(XF, XF).T
    bondw = np.concatenate([diag(ub, 4), diag(vbm, 4)], 1)

    def padded(a, n, value):
        return np.concatenate([a, np.full((n - len(a),) + a.shape[1:], value, a.dtype)])

    sel = np.concatenate([diag(np.ones((1, 64), f4), 16), diag(np.ones((1, 32), f4), 16)], 1)
    arrays = {
        "x_in": padded(w["x"], NP, 0), "src_in": padded(w["src"], EP, N_NODES),
        "dst_in": padded(w["dst"], EP, N_NODES), "attr_in": padded(w["edge_attr_16"], EP, 0),
        "consts_in": consts, "weights_in": weights, "prep_in": prep, "bondw_in": bondw, "sel_in": sel,
    }
    arrays = {n: np.ascontiguousarray(a) for n, a in arrays.items()}
    nc = _bacc.Bacc("TRN2", target_bir_lowering=False, num_devices=1)
    args = [nc.dram_tensor(n, a.shape, mybir.dt.from_np(a.dtype), kind="ExternalInput").ap()
            for n, a in arrays.items()]
    out = nc.dram_tensor("out_0", (NROWS, XF), F32, kind="ExternalOutput").ap()
    build(nc, *args, out)
    r = _run(nc, [arrays], core_ids=[0])
    return r.results[0]["out_0"][0:N_NODES]
```
